# Optimizing a Trainium2 kernel written in Bass

```python
import numpy as np
import jax
import jax.numpy as jnp

def _softmax(x, axis=-1):
    return jax.nn.softmax(x, axis=axis)

def _gelu(x):
    return jax.nn.gelu(x, approximate=True)

def _silu(x):
    return jax.nn.silu(x)

def _sigmoid(x):
    return jax.nn.sigmoid(x)

def _layernorm(x, axis=-1, eps=1e-05):
    m = jnp.mean(x, axis=axis, keepdims=True)
    v = jnp.var(x, axis=axis, keepdims=True)
    return (x - m) / jnp.sqrt(v + eps)

def _scatter_add(tgt, idx, src, axis=0):
    return tgt.at[idx].add(src)

def _segment_sum(src, seg, n):
    return jax.ops.segment_sum(src, seg, n)
kernel_name = 'mk_perceiver_d1_seqx_r2_82fbac'

def setup_inputs(seed: int=0):
    np.random.seed(seed)
    _w = jnp.asarray

    def _rec_inputs():
        import jax
        import jax.numpy as jnp
        _rk = jax.random.key(seed)
        x = -0.0005207 + 1.001 * jax.random.normal(jax.random.fold_in(_rk, 1), (4, 128, 512), jnp.float32)
        _lenS = 128 - jax.random.randint(jax.random.fold_in(_rk, 7), (4,), 0, max(1, 128 // 4) + 1, jnp.int32)
        _lenS2 = 2048 - jax.random.randint(jax.random.fold_in(_rk, 8), (4,), 0, max(1, 2048 // 4) + 1, jnp.int32)
        _ctx_1024P = jax.random.normal(jax.random.fold_in(_rk, 11), (4, 16, 512), jnp.float32)
        _ctx_1024c = jax.random.dirichlet(jax.random.fold_in(_rk, 511), 0.3 * jnp.ones((16,), jnp.float32), (4, 2048))
        _ctx_1024t = jnp.einsum('bsk,bkd->bsd', _ctx_1024c, _ctx_1024P)
        _ctx_1024t = _ctx_1024t * jax.lax.rsqrt(jnp.mean(jnp.square(_ctx_1024t)) + 1e-12) * 0.953939
        ctx_1024 = -1.52775e-05 + 0.999936 * (_ctx_1024t + 0.3 * jax.random.normal(jax.random.fold_in(_rk, 611), (4, 2048, 512), jnp.float32))
        return (x, ctx_1024)
    x, ctx_1024 = _rec_inputs()

    def _L0_xattn_setup():
        import jax, jax.numpy as jnp
        import numpy as np
        DIM = 512
        HEADS = 16
        DHEAD = 64
        INNER = HEADS * DHEAD
        EPS = 1e-05

        def layer_norm(x, g, b):
            mu = jnp.mean(x, axis=-1, keepdims=True)
            var = jnp.mean(jnp.square(x - mu), axis=-1, keepdims=True)
            return (x - mu) * jax.lax.rsqrt(var + EPS) * g + b

        def apply_rope(x, cos, sin):
            d2 = x.shape[-1] // 2
            x1, x2 = (x[..., :d2], x[..., d2:])
            return jnp.concatenate([x1 * cos - x2 * sin, x2 * cos + x1 * sin], axis=-1)
        key = jax.random.key(seed)
        ks = jax.random.split(key, 10)
        B, N, S = (8, 128, 2048)
        latents = jax.random.normal(ks[0], (B, N, DIM), dtype=jnp.float32)
        context = jax.random.normal(ks[1], (B, S, DIM), dtype=jnp.float32)
        cos = jax.random.uniform(ks[2], (S, DHEAD // 2), dtype=jnp.float32)
        sin = jax.random.uniform(ks[3], (S, DHEAD // 2), dtype=jnp.float32)
        init = lambda k, shp, fan_in: jax.random.normal(k, shp, dtype=jnp.float32) / np.sqrt(fan_in)
        return {'latents': latents, 'context': context, 'cos': cos, 'sin': sin, 'ln_lat_g': jnp.ones((DIM,), jnp.float32), 'ln_lat_b': jnp.zeros((DIM,), jnp.float32), 'ln_ctx_g': jnp.ones((DIM,), jnp.float32), 'ln_ctx_b': jnp.zeros((DIM,), jnp.float32), 'Wq': init(ks[4], (DIM, INNER), DIM), 'Wkv': init(ks[5], (DIM, 2 * INNER), DIM), 'Wo': init(ks[6], (INNER, DIM), INNER), 'bo': jnp.zeros((DIM,), jnp.float32)}
    _L0_xattn_all = _L0_xattn_setup()
    _L0_xattn_in = {k: v for k, v in _L0_xattn_all.items() if k in ('cos', 'sin', 'ln_lat_g', 'ln_lat_b', 'ln_ctx_g', 'ln_ctx_b', 'Wq', 'Wkv', 'Wo', 'bo')}
    del _L0_xattn_all

    def _L0_attn_setup():
        import jax, jax.numpy as jnp
        import numpy as np
        B, N, C, H = (8, 2048, 512, 16)
        D = C // H
        EPS = 1e-12

        def _l2norm(x):
            n = jnp.sqrt(jnp.sum(x * x, axis=-1, keepdims=True))
            return x / jnp.maximum(n, EPS)
        key = jax.random.key(seed)
        ks = jax.random.split(key, 5)
        return {'x': jax.random.normal(ks[0], (B, N, C), dtype=jnp.float32), 'qkv_w': jax.random.normal(ks[1], (C, 3 * C), dtype=jnp.float32) * 0.02, 'qkv_b': jax.random.normal(ks[2], (3 * C,), dtype=jnp.float32) * 0.02, 'proj_w': jax.random.normal(ks[3], (C, C), dtype=jnp.float32) * 0.02, 'proj_b': jax.random.normal(ks[4], (C,), dtype=jnp.float32) * 0.02}
    _L0_attn_all = _L0_attn_setup()
    _L0_attn_in = {k: v for k, v in _L0_attn_all.items() if k in ('qkv_w', 'qkv_b', 'proj_w', 'proj_b')}
    del _L0_attn_all

    def _L0_ffn_setup():
        import jax, jax.numpy as jnp
        import numpy as np
        K_TOP = 2
        W_SCALE = 0.02
        key = jax.random.key(seed)
        ks = jax.random.split(key, 8)
        D, F, E = (512, 512, 8)
        B, T = (4, 1024)
        x = jax.random.normal(ks[0], (B, T, D), dtype=jnp.float32)
        router_w = jax.random.normal(ks[1], (D, E), dtype=jnp.float32) * W_SCALE
        sg = jax.random.normal(ks[2], (D, F), dtype=jnp.float32) * W_SCALE
        su = jax.random.normal(ks[3], (D, F), dtype=jnp.float32) * W_SCALE
        sd = jax.random.normal(ks[4], (F, D), dtype=jnp.float32) * W_SCALE
        wg = jax.random.normal(ks[5], (E, D, F), dtype=jnp.float32) * W_SCALE
        wu = jax.random.normal(ks[6], (E, D, F), dtype=jnp.float32) * W_SCALE
        wd = jax.random.normal(ks[7], (E, F, D), dtype=jnp.float32) * W_SCALE
        return {'x': x, 'router_w': router_w, 'sg': sg, 'su': su, 'sd': sd, 'wg': wg, 'wu': wu, 'wd': wd}
    _L0_ffn_all = _L0_ffn_setup()
    _L0_ffn_in = {k: v for k, v in _L0_ffn_all.items() if k in ('router_w', 'sg', 'su', 'sd', 'wg', 'wu', 'wd')}
    del _L0_ffn_all
    return {'x': x, 'ctx_1024': ctx_1024, 'L0_xattn_cos': _L0_xattn_in['cos'], 'L0_xattn_sin': _L0_xattn_in['sin'], 'L0_xattn_ln_lat_g': _L0_xattn_in['ln_lat_g'], 'L0_xattn_ln_lat_b': _L0_xattn_in['ln_lat_b'], 'L0_xattn_ln_ctx_g': _L0_xattn_in['ln_ctx_g'], 'L0_xattn_ln_ctx_b': _L0_xattn_in['ln_ctx_b'], 'L0_xattn_Wq': _L0_xattn_in['Wq'], 'L0_xattn_Wkv': _L0_xattn_in['Wkv'], 'L0_xattn_Wo': _L0_xattn_in['Wo'], 'L0_xattn_bo': _L0_xattn_in['bo'], 'L0_attn_qkv_w': _L0_attn_in['qkv_w'], 'L0_attn_qkv_b': _L0_attn_in['qkv_b'], 'L0_attn_proj_w': _L0_attn_in['proj_w'], 'L0_attn_proj_b': _L0_attn_in['proj_b'], 'L0_ffn_router_w': _L0_ffn_in['router_w'], 'L0_ffn_sg': _L0_ffn_in['sg'], 'L0_ffn_su': _L0_ffn_in['su'], 'L0_ffn_sd': _L0_ffn_in['sd'], 'L0_ffn_wg': _L0_ffn_in['wg'], 'L0_ffn_wu': _L0_ffn_in['wu'], 'L0_ffn_wd': _L0_ffn_in['wd']}

def reference(x, ctx_1024, L0_xattn_cos, L0_xattn_sin, L0_xattn_ln_lat_g, L0_xattn_ln_lat_b, L0_xattn_ln_ctx_g, L0_xattn_ln_ctx_b, L0_xattn_Wq, L0_xattn_Wkv, L0_xattn_Wo, L0_xattn_bo, L0_attn_qkv_w, L0_attn_qkv_b, L0_attn_proj_w, L0_attn_proj_b, L0_ffn_router_w, L0_ffn_sg, L0_ffn_su, L0_ffn_sd, L0_ffn_wg, L0_ffn_wu, L0_ffn_wd):
    import jax
    import jax.numpy as jnp

    def _L0_xattn_ref(latents, context, cos, sin, ln_lat_g, ln_lat_b, ln_ctx_g, ln_ctx_b, Wq, Wkv, Wo, bo):
        import jax, jax.numpy as jnp
        import numpy as np
        DIM = 512
        HEADS = 16
        DHEAD = 64
        INNER = HEADS * DHEAD
        EPS = 1e-05

        def layer_norm(x, g, b):
            mu = jnp.mean(x, axis=-1, keepdims=True)
            var = jnp.mean(jnp.square(x - mu), axis=-1, keepdims=True)
            return (x - mu) * jax.lax.rsqrt(var + EPS) * g + b

        def apply_rope(x, cos, sin):
            d2 = x.shape[-1] // 2
            x1, x2 = (x[..., :d2], x[..., d2:])
            return jnp.concatenate([x1 * cos - x2 * sin, x2 * cos + x1 * sin], axis=-1)
        b, n, _ = latents.shape
        s = context.shape[1]
        lat = layer_norm(latents, ln_lat_g, ln_lat_b)
        ctx = layer_norm(context, ln_ctx_g, ln_ctx_b)
        q = (lat @ Wq).reshape(b, n, HEADS, DHEAD).transpose(0, 2, 1, 3)
        kv = ctx @ Wkv
        k, v = jnp.split(kv, 2, axis=-1)
        k = k.reshape(b, s, HEADS, DHEAD).transpose(0, 2, 1, 3)
        v = v.reshape(b, s, HEADS, DHEAD).transpose(0, 2, 1, 3)
        k = apply_rope(k, cos[None, None], sin[None, None])
        scale = DHEAD ** (-0.5)
        attn = jnp.einsum('bhnd,bhsd->bhns', q, k) * scale
        attn = jnp.clip(attn, -11.0, 11.0)
        attn = jax.nn.softmax(attn, axis=-1)
        out = jnp.einsum('bhns,bhsd->bhnd', attn, v)
        out = out.transpose(0, 2, 1, 3).reshape(b, n, INNER)
        return out @ Wo + bo

    def _L0_attn_ref(x, qkv_w, qkv_b, proj_w, proj_b):
        import jax, jax.numpy as jnp
        import numpy as np
        B, N, C, H = (8, 2048, 512, 16)
        D = C // H
        EPS = 1e-12

        def _l2norm(x):
            n = jnp.sqrt(jnp.sum(x * x, axis=-1, keepdims=True))
            return x / jnp.maximum(n, EPS)
        b, n, c = x.shape
        qkv = (x @ qkv_w + qkv_b).reshape(b, n, 3, H, D)
        qkv = jnp.transpose(qkv, (2, 0, 3, 1, 4))
        q, k, v = (qkv[0], qkv[1], qkv[2])
        q = _l2norm(q)
        k = _l2norm(k)
        kv = jnp.einsum('bhnd,bhne->bhde', k, v)
        out = jnp.einsum('bhnd,bhde->bhne', q, kv)
        out = jnp.transpose(out, (0, 2, 1, 3)).reshape(b, n, c)
        return out @ proj_w + proj_b

    def _L0_ffn_ref(x, router_w, sg, su, sd, wg, wu, wd):
        import jax, jax.numpy as jnp
        import numpy as np
        K_TOP = 2
        W_SCALE = 0.02
        B, T, D = x.shape
        E = wg.shape[0]
        flat = x.reshape(-1, D)
        N = flat.shape[0]
        shared = jax.nn.silu(flat @ sg) * (flat @ su) @ sd
        probs = jax.nn.softmax(flat @ router_w, axis=-1)
        topk_p, topk_i = jax.lax.top_k(probs, K_TOP)
        topk_p = topk_p / (jnp.sum(topk_p, axis=-1, keepdims=True) + 1e-09)
        cw = jnp.zeros((N, E), dtype=flat.dtype).at[jnp.arange(N)[:, None], topk_i].add(topk_p)
        h = jax.nn.silu(jnp.einsum('nd,edf->nef', flat, wg)) * jnp.einsum('nd,edf->nef', flat, wu)
        eo = jnp.einsum('nef,efd->ned', h, wd)
        routed = jnp.einsum('ned,ne->nd', eo, cw)
        return (shared + routed).reshape(B, T, D)
    x = x + _L0_xattn_ref(_layernorm(x, axis=-1), ctx_1024, L0_xattn_cos, L0_xattn_sin, L0_xattn_ln_lat_g, L0_xattn_ln_lat_b, L0_xattn_ln_ctx_g, L0_xattn_ln_ctx_b, L0_xattn_Wq, L0_xattn_Wkv, L0_xattn_Wo, L0_xattn_bo)
    x = x + _L0_attn_ref(_layernorm(x, axis=-1), L0_attn_qkv_w, L0_attn_qkv_b, L0_attn_proj_w, L0_attn_proj_b)
    x = x + _L0_ffn_ref(_layernorm(x, axis=-1), L0_ffn_router_w, L0_ffn_sg, L0_ffn_su, L0_ffn_sd, L0_ffn_wg, L0_ffn_wu, L0_ffn_wd)
    return x

_drawn_inputs = setup_inputs


def setup_inputs(seed=0):
    import zlib

    import numpy as np

    out = dict(_drawn_inputs(seed))
    spreads = {'L0_xattn_ln_lat_g': (1.0, 0.6),
     'L0_xattn_ln_lat_b': (0.0, 0.316),
     'L0_xattn_ln_ctx_g': (1.0, 0.2),
     'L0_xattn_ln_ctx_b': (0.0, 0.1),
     'L0_xattn_bo': (0.0, 0.1)}
    factors = {'L0_xattn_cos': 7.15,
     'L0_xattn_sin': 7.121,
     'L0_attn_proj_b': 4.744,
     'L0_ffn_router_w': 3.212,
     'L0_ffn_wg': 2.77,
     'L0_ffn_wu': 2.702,
     'L0_ffn_wd': 2.712}
    for name, (base, spread) in spreads.items():
        noise = np.random.default_rng([zlib.crc32(name.encode()), seed]).standard_normal(out[name].shape)
        drawn = base * np.exp(spread * noise) if base else spread * noise
        out[name] = jnp.asarray(drawn.astype(out[name].dtype))
    for name, factor in factors.items():
        out[name] = (out[name] * factor).astype(out[name].dtype)
    return out
```

```python
from contextlib import ExitStack

import concourse.bass as bass
from concourse import mybir
from concourse.alu_op_type import AluOpType as ALU

F32 = mybir.dt.float32
F32R = mybir.dt.float32r
U32 = mybir.dt.uint32
ACT = mybir.ActivationFunctionType
AX_X = mybir.AxisListType.X

P = 128
BATCH = 4
QUERIES = 128
CTX = 2048
DIM = 512
KT = DIM // P
EPS = 1e-5

HEADS = 16
DHEAD = 64
HALF = DHEAD // 2
INNER = HEADS * DHEAD
CLIP = 11.0
SCALE = DHEAD ** -0.5
CHUNK = 512
ROW_TILES = CHUNK // P
CHUNKS = CTX // CHUNK
STEPS = 8
BSTEPS = STEPS * CHUNKS
PAIRS = HEADS // 2
SCORE_LAG = 3
VALUE_LAG = 4

LHEADS = 16
LD = DIM // LHEADS
NORM_EPS = 1e-12
GROUP = P // LD

EXPERTS = 8
ALL_EXPERTS = EXPERTS + 1
TOKENS = BATCH * QUERIES


def wait(eng, sem, value):
    if isinstance(value, int) and value <= 0:
        return
    eng.wait_ge(sem, value)


def prepare(nc, d, keep):
    with ExitStack() as ctx:
        def sb(name, shape, dt=F32):
            return ctx.enter_context(nc.sbuf_tensor(name, shape, dt))

        def sem(name):
            return ctx.enter_context(nc.semaphore(name))

        x_in = sb("x_in", [P, BATCH, DIM])
        wq = sb("wq", [P, KT, INNER])
        w_raw = sb("w_raw", [P, KT // 2, INNER])
        lat_g = sb("lat_g", [P, KT])
        lat_b = sb("lat_b", [P, KT])
        stats = sb("a_stats", [P, BATCH, 6])
        mean_var = sb("a_mean_var", [P, BATCH, 2])
        var_eps = sb("a_var_eps", [P, BATCH])
        rstd = sb("a_rstd", [P, BATCH])
        lat_t = sb("lat_t", [P, KT, TOKENS])
        q_stage = sb("q_stage", [P, 2, 2, 2, TOKENS], F32R)
        ps = ctx.enter_context(nc.psum_tensor("a_ps", [P, 8, 512], F32))

        x_landed = sem("a_x_landed")
        small_landed = sem("a_small_landed")
        wq_landed = sem("a_wq_landed")
        raw_landed = [sem(f"a_raw_landed{i}") for i in range(4)]
        raw_hi = sem("a_raw_hi")
        raw_lo = sem("a_raw_lo")
        const_ready = sem("a_const_ready")
        dve_step = sem("a_dve_step")
        var_ready = sem("a_var_ready")
        rstd_ready = sem("a_rstd_ready")
        norm_ready = sem("a_norm_ready")
        tr_ready = sem("a_tr_ready")
        lat_ready = sem("a_lat_ready")
        q_ready = sem("a_q_ready")
        q_hi = sem("a_q_hi")
        q_lo = sem("a_q_lo")
        q_stored = [sem(f"a_q_stored{i}") for i in range(2)]

        pieces = [(w, half) for w in range(2) for half in range(2)]

        def raw_source(n):
            w, half = pieces[n]
            return d["wk" if w == 0 else "wv"].rearrange("(t p) n -> p t n", p=P)[:, 2 * half:2 * half + 2, :]

        def split_target(n, part):
            w, half = pieces[n]
            return keep["wk_" + part if w == 0 else "wv_" + part][:, 2 * half:2 * half + 2, :]

        block = ctx.enter_context(nc.Block())

        @block.sync
        def _(sp):
            sp.dma_start(x_in[:], d["x"].rearrange("b n d -> n b d")).then_inc(x_landed, 16)
            sp.dma_start(lat_g[:], d["lat_g"]).then_inc(small_landed, 16)
            sp.dma_start(lat_b[:], d["lat_b"]).then_inc(small_landed, 16)
            sp.dma_start(keep["ctx_g"][:], d["ctx_g"]).then_inc(small_landed, 16)
            sp.dma_start(keep["ctx_b"][:], d["ctx_b"]).then_inc(small_landed, 16)
            for n in ("cos", "sin"):
                angles = bass.AP(d[n].tensor, 0, [[CTX, HALF], [0, P // HALF], [1, CTX]])
                sp.dma_start(keep[n][:], angles).then_inc(small_landed, 16)
            sp.dma_start(wq[:], d["wq"].rearrange("(t p) n -> p t n", p=P)).then_inc(wq_landed, 16)
            for m in range(PAIRS):
                sp.wait_ge(q_lo, m + 1)
                for b in range(BATCH):
                    sp.dma_start(d["q_scratch"][b, m],
                                 q_stage[:, m % 2, :, :, b * P:(b + 1) * P].bitcast(F32)).then_inc(q_stored[m % 2], 16)
            for i in range(2):
                sp.wait_ge(q_stored[i], 16 * BATCH * PAIRS // 2)
            sp.wait_ge(small_landed, 16 * 6)

        @block.gpsimd
        def _(pool):
            nc.gpsimd.memset(keep["ident"][:], 0.0).then_inc(const_ready, 1)
            nc.gpsimd.memset(keep["minus_half"][:], -0.5).then_inc(const_ready, 1)
            nc.gpsimd.memset(keep["v"][:, :, :, DHEAD:DHEAD + 1], 1.0).then_inc(const_ready, 1)
            pool.wait_ge(const_ready, 3)
            nc.gpsimd.affine_select(out=keep["ident"][:], in_=keep["ident"][:], compare_op=ALU.not_equal, fill=1.0,
                                    base=0, pattern=[[-1, P]], channel_multiplier=1).then_inc(const_ready, 1)
            for r in range(2):
                pool.wait_ge(var_ready, r + 1)
                nc.gpsimd.tensor_tensor(rstd[:], var_eps[:], keep["minus_half"][:, 0:BATCH], ALU.pow).then_inc(rstd_ready, 1)

        @block.scalar
        def _(act):
            for n in range(4):
                if n >= 1:
                    act.wait_ge(raw_lo, n)
                act.dma_start(w_raw[:], raw_source(n)).then_inc(raw_landed[n], 16)
                act.wait_ge(raw_landed[n], 16)
                nc.scalar.activation(split_target(n, "hi"), w_raw[:], ACT.Copy).then_inc(raw_hi, 1)
            for m in range(PAIRS):
                act.wait_ge(q_ready, m + 1)
                if m >= 2:
                    act.wait_ge(q_stored[m % 2], 16 * BATCH * (m // 2))
                q = ps[:, 4 + m % 4, :]
                for j in range(2):
                    for side in range(2):
                        hi = nc.scalar.activation(q_stage[64 * side:64 * side + 64, m % 2, j, 0, :],
                                                  q[64 * j:64 * j + 64, :], ACT.Copy)
                hi.then_inc(q_hi, 1)

        @block.vector
        def _(dve):
            chain = [0]

            def link(ins):
                chain[0] += 1
                ins.then_inc(dve_step, 1)
                dve.wait_ge(dve_step, chain[0])

            dve.wait_ge(x_landed, 16)
            for r in range(2):
                for b in range(BATCH):
                    stat = nc.vector.bn_stats(stats[:, b, :], x_in[:, b, :])
                link(stat)
                for b in range(BATCH):
                    stat = nc.vector.bn_aggr(mean_var[:, b, :], stats[:, b, :])
                link(stat)
                nc.vector.tensor_scalar(var_eps[:], mean_var[:, :, 1], EPS, None, ALU.add).then_inc(var_ready, 1)
                dve.wait_ge(rstd_ready, r + 1)
                for b in range(BATCH):
                    norm = nc.vector.tensor_scalar(x_in[:, b, :], x_in[:, b, :], mean_var[:, b, 0:1],
                                                   rstd[:, b:b + 1], ALU.subtract, ALU.mult)
                norm.then_inc(norm_ready, 1)
                dve.wait_ge(norm_ready, r + 1)
            dve.wait_ge(small_landed, 16 * 6)
            for b in range(BATCH):
                dve.wait_ge(tr_ready, b + 1)
                for t in range(KT):
                    out = nc.vector.tensor_scalar(lat_t[:, t, b * P:(b + 1) * P], ps[:, b, t * P:(t + 1) * P],
                                                  lat_g[:, t:t + 1], lat_b[:, t:t + 1], ALU.mult, ALU.add)
                out.then_inc(lat_ready, 1)

            def split_low(n):
                dve.wait_ge(raw_hi, n + 1)
                nc.vector.tensor_tensor(split_target(n, "lo"), w_raw[:], split_target(n, "hi").bitcast(F32),
                                        ALU.subtract).then_inc(raw_lo, 1)

            for n in range(4):
                split_low(n)
            for m in range(PAIRS):
                dve.wait_ge(q_hi, m + 1)
                q = ps[:, 4 + m % 4, :]
                for j in range(2):
                    for side in range(2):
                        lo = nc.vector.tensor_tensor(q_stage[64 * side:64 * side + 64, m % 2, j, 1, :],
                                                     q[64 * j:64 * j + 64, :],
                                                     q_stage[64 * j:64 * j + 64, m % 2, j, 0, :].bitcast(F32), ALU.subtract)
                lo.then_inc(q_lo, 1)

        @block.tensor
        def _(pe):
            pe.wait_ge(const_ready, 4)
            pe.wait_ge(norm_ready, 2)
            for b in range(BATCH):
                for t in range(KT):
                    tr = nc.tensor.transpose(ps[:, b, t * P:(t + 1) * P], x_in[:, b, t * P:(t + 1) * P], keep["ident"][:])
                tr.then_inc(tr_ready, 1)
            pe.wait_ge(lat_ready, BATCH)
            pe.wait_ge(wq_landed, 16)
            for m in range(PAIRS):
                if m >= 4:
                    pe.wait_ge(q_lo, m - 3)
                for t in range(KT):
                    mm = nc.tensor.matmul(ps[:, 4 + m % 4, :], wq[:, t, m * P:(m + 1) * P], lat_t[:, t, :],
                                          start=(t == 0), stop=(t == KT - 1))
                mm.then_inc(q_ready, 1)


def attend(nc, d, keep):
    with ExitStack() as ctx:
        def sb(name, shape, dt=F32):
            return ctx.enter_context(nc.sbuf_tensor(name, shape, dt))

        def psum(name, shape):
            return ctx.enter_context(nc.psum_tensor(name, shape, F32))

        def sem(name):
            return ctx.enter_context(nc.semaphore(name))

        wk_hi, wk_lo, wv_hi, wv_lo = (keep[n] for n in ("wk_hi", "wk_lo", "wv_hi", "wv_lo"))
        cos, sin, v = keep["cos"], keep["sin"], keep["v"]
        row_in = sb("row_in", [P, ROW_TILES, DIM])
        stats = sb("stats", [P, 2, 6])
        mean_var = sb("mean_var", [P, 2, 2])
        var_eps = sb("var_eps", [P, 2])
        rstd = sb("rstd", [P, 2])
        x_full = sb("x_full", [P, 2, KT, P])
        x_hi = sb("x_hi", [P, 2, KT, CHUNK], F32R)
        x_lo = sb("x_lo", [P, 2, KT, CHUNK], F32R)
        a_cos = sb("a_cos", [P, CHUNK])
        b_sin = sb("b_sin", [P, CHUNK])
        b_cos = sb("b_cos", [P, CHUNK])
        a_sin = sb("a_sin", [P, CHUNK])
        first_hi = sb("first_hi", [P, CHUNK], F32R)
        second_hi = sb("second_hi", [P, CHUNK], F32R)
        keys = sb("keys", [P, 2, 4, CHUNK], F32R)
        queries = sb("queries", [P, PAIRS, 2, 2, QUERIES], F32R)
        probs = sb("probs", [P, 2, 2, CHUNK])
        acc = sb("acc", [P, HEADS, DHEAD + 1])
        recip = sb("recip", [P, 2])
        attn = sb("attn", [P, INNER])

        ps_tr = psum("ps_tr", [P, KT, P])
        ps_v = psum("ps_v", [P, 2, 512])
        ps_k = psum("ps_k", [P, 2, 512])
        ps_s = psum("ps_s", [P, ROW_TILES, 2, QUERIES])
        ps_o = psum("ps_o", [P, 512])

        row_landed = [sem(f"row_landed{i}") for i in range(ROW_TILES)]
        stats_ready = sem("stats_ready")
        mean_ready = sem("mean_ready")
        var_ready = sem("var_ready")
        rstd_ready = sem("rstd_ready")
        row_ready = sem("row_ready")
        tr_ready = sem("tr_ready")
        full_ready = sem("full_ready")
        hi_ready = sem("hi_ready")
        lo_ready = sem("lo_ready")
        v_ready = sem("v_ready")
        v_stored = sem("v_stored")
        k_ready = sem("k_ready")
        k_turned = sem("k_turned")
        rope_ready = sem("rope_ready")
        rope_hi = sem("rope_hi")
        rope_lo = sem("rope_lo")
        keys_landed = [sem(f"keys_landed{i}") for i in range(2)]
        q_landed = [sem(f"q_landed{i}") for i in range(PAIRS)]
        s_ready = sem("s_ready")
        s_copied = sem("s_copied")
        s_taken = sem("s_taken")
        clipped = sem("clipped")
        probs_ready = sem("probs_ready")
        o_ready = sem("o_ready")
        o_added = sem("o_added")
        recip_ready = sem("recip_ready")
        attn_ready = sem("attn_ready")
        attn_stored = sem("attn_stored")

        rows = d["ctx"].rearrange("b (t p) d -> (b t) p d", p=P)
        ROWS_OF_BATCH = CTX // P
        last_step = BATCH * BSTEPS

        def run(eng, step):
            for t in range(STEPS):
                step(0, t)
            with eng.Fori(0, BATCH - 1) as b:
                for t in range(STEPS, STEPS + BSTEPS):
                    step(b, t)
            for t in range(STEPS, BSTEPS + VALUE_LAG + 2):
                step(BATCH - 1, t)

        def exists(b, t):
            return not isinstance(b, int) or 0 <= BSTEPS * b + t < last_step

        def next_row_tile(b, t):
            if t % 2 == 0 and exists(b, t) and exists(b, t + STEPS):
                return b * ROWS_OF_BATCH + (t // 2 + ROW_TILES)
            return None

        block = ctx.enter_context(nc.Block())

        @block.sync
        def _(sp):
            def load_rows(tile, slot):
                wait(sp, tr_ready, tile - (ROW_TILES - 1))
                sp.dma_start(row_in[:, slot, :], rows[tile]).then_inc(row_landed[slot], 16)

            for i in range(ROW_TILES):
                load_rows(i, i)
            for m in range(PAIRS):
                sp.dma_start(queries[:, m].bitcast(F32), d["q_scratch"][0, m]).then_inc(q_landed[m], 16)

            def step(b, t):
                tile = next_row_tile(b, t)
                if tile is not None:
                    load_rows(tile, t // 2 % ROW_TILES)
                if t % 2 == 0 and exists(b, t - 2):
                    group = b * (BSTEPS // 2) + (t // 2 - 1)
                    slot = (t // 2 - 1) % 2
                    parts = ((rope_hi, first_hi, 1), (rope_hi, second_hi, 2),
                             (rope_lo, a_cos, 1), (rope_lo, b_cos, 2))
                    for i, (made, part, n) in enumerate(parts):
                        wait(sp, made, 2 * group + n)
                        sp.dma_start(keys[HALF * i:HALF * (i + 1), slot].bitcast(F32),
                                     part[:].bitcast(F32)).then_inc(keys_landed[slot], 16)
                pair = t - SCORE_LAG - 1
                if STEPS * (CHUNKS - 1) <= pair % BSTEPS and pair >= 0 and exists(b, pair + STEPS):
                    m = pair % STEPS
                    whose = b + pair // BSTEPS
                    wait(sp, s_ready, b * (2 * BSTEPS) + 2 * (pair + 1))
                    sp.dma_start(queries[:, m].bitcast(F32), d["q_scratch"][whose + 1, m]).then_inc(q_landed[m], 16)
                pair = t - VALUE_LAG - 2
                if pair % BSTEPS == BSTEPS - 1 and exists(b, pair):
                    whose = b + pair // BSTEPS
                    wait(sp, attn_ready, PAIRS * whose + PAIRS)
                    sp.dma_start(d["attn_scratch"][whose], attn[:]).then_inc(attn_stored, 16)

            run(sp, step)
            sp.wait_ge(attn_stored, 16 * BATCH)

        @block.gpsimd
        def _(pool):
            def raise_power(tile, slot):
                wait(pool, var_ready, tile + 1)
                nc.gpsimd.tensor_tensor(rstd[:, slot:slot + 1], var_eps[:, slot:slot + 1], keep["minus_half"][:, 0:1],
                                        ALU.pow).then_inc(rstd_ready, 1)

            def rows_low(tile, buf, slot, i):
                wait(pool, hi_ready, tile + 1)
                cols = slice(i * P, (i + 1) * P)
                nc.gpsimd.tensor_tensor(x_lo[:, buf, :, cols], x_full[:, slot], x_hi[:, buf, :, cols].bitcast(F32),
                                        ALU.subtract).then_inc(lo_ready, 1)

            for i in range(ROW_TILES):
                raise_power(i, i % 2)
                if i >= 1:
                    rows_low(i - 1, 0, (i - 1) % 2, i - 1)
            rows_low(ROW_TILES - 1, 0, 1, ROW_TILES - 1)

            def step(b, t):
                tile = next_row_tile(b, t)
                if tile is not None:
                    raise_power(tile, t // 2 % 2)
                tile = next_row_tile(b, t - 1)
                if tile is not None:
                    rows_low(tile, (t // STEPS + 1) % 2, t // 2 % 2, t // 2 % ROW_TILES)
                if t % 2 == 0 and exists(b, t - 2):
                    group = b * (BSTEPS // 2) + (t // 2 - 1)
                    for n, (full, hi) in enumerate(((a_cos, first_hi), (b_cos, second_hi))):
                        wait(pool, rope_hi, 2 * group + (n + 1))
                        nc.gpsimd.tensor_tensor(full[:].bitcast(F32R), full[:], hi[:].bitcast(F32),
                                                ALU.subtract).then_inc(rope_lo, 1)

            run(pool, step)

        @block.scalar
        def _(act):
            def rows_high(tile, buf, slot, i):
                wait(act, full_ready, tile + 1)
                wait(act, k_ready, 2 * tile - 2 * i - STEPS)
                nc.scalar.activation(x_hi[:, buf, :, i * P:(i + 1) * P], x_full[:, slot], ACT.Copy).then_inc(hi_ready, 1)

            for i in range(ROW_TILES):
                rows_high(i, 0, i % 2, i)

            def copy_scores(b, pair, j):
                if exists(b, pair):
                    count = b * (2 * BSTEPS) + (2 * pair + j + 1)
                    if j == 0:
                        wait(act, o_ready, b * BSTEPS + (pair - 1))
                    wait(act, s_ready, count)
                    nc.scalar.activation(probs[:, pair % 2, j, :].rearrange("p (i n) -> p i n", n=P), ps_s[:, :, 1, :],
                                         ACT.Copy).then_inc(s_copied, 1)

            def step(b, t):
                copy_scores(b, t - VALUE_LAG, 1)
                pair = t - VALUE_LAG
                if exists(b, pair):
                    wait(act, clipped, b * (2 * BSTEPS) + 2 * (pair + 1))
                    nc.scalar.activation(probs[:, pair % 2], probs[:, pair % 2], ACT.Exp, scale=SCALE).then_inc(probs_ready, 1)
                if exists(b, t):
                    p = t % STEPS
                    wait(act, v_ready, b * BSTEPS + (t + 1))
                    wait(act, o_ready, b * BSTEPS + (t - p - STEPS + 4 * (p // 4 + 1)))
                    half = p // ROW_TILES
                    nc.scalar.activation(v[:, p % ROW_TILES, 8 * half:8 * half + 8, 0:DHEAD],
                                         ps_v[:, t % 2, :].rearrange("p (h e) -> p h e", e=DHEAD), ACT.Copy).then_inc(v_stored, 1)
                copy_scores(b, t - SCORE_LAG, 0)
                if t % 2 == 0 and exists(b, t - 2):
                    group = b * (BSTEPS // 2) + (t // 2 - 1)
                    for n, (full, hi) in enumerate(((a_cos, first_hi), (b_cos, second_hi))):
                        wait(act, rope_ready, 2 * group + (n + 1))
                        nc.scalar.activation(hi[:], full[:], ACT.Copy).then_inc(rope_hi, 1)
                if t % 2 == 1:
                    tile = next_row_tile(b, t - 1)
                    if tile is not None:
                        rows_high(tile, (t // STEPS + 1) % 2, t // 2 % 2, t // 2 % ROW_TILES)

            run(act, step)

        @block.vector
        def _(dve):
            def row_stats(tile, slot, ring, turn):
                wait(dve, row_landed[slot], 16 * turn)
                wait(dve, row_ready, tile - 1)
                nc.vector.bn_stats(stats[:, ring, :], row_in[:, slot, :]).then_inc(stats_ready, 1)

            def row_variance(tile, ring):
                nc.vector.bn_aggr(mean_var[:, ring, :], stats[:, ring, :]).then_inc(mean_ready, 1)
                wait(dve, mean_ready, tile + 1)
                nc.vector.tensor_scalar(var_eps[:, ring:ring + 1], mean_var[:, ring, 1:2], EPS, None, ALU.add).then_inc(var_ready, 1)

            def row_norm(tile, slot, ring):
                wait(dve, rstd_ready, tile + 1)
                nc.vector.tensor_scalar(row_in[:, slot, :], row_in[:, slot, :], mean_var[:, ring, 0:1],
                                        rstd[:, ring:ring + 1], ALU.subtract, ALU.mult).then_inc(row_ready, 1)

            def rows_full(tile, ring):
                wait(dve, tr_ready, tile + 1)
                wait(dve, lo_ready, tile - 1)
                for k in range(KT):
                    out = nc.vector.tensor_scalar(x_full[:, ring, k, :], ps_tr[:, k, :], keep["ctx_g"][:, k:k + 1],
                                                  keep["ctx_b"][:, k:k + 1], ALU.mult, ALU.add)
                out.then_inc(full_ready, 1)

            for i in range(ROW_TILES):
                row_stats(i, i, i % 2, 1)
                wait(dve, stats_ready, i + 1)
                row_variance(i, i % 2)
                row_norm(i, i, i % 2)
                rows_full(i, i % 2)
            row_stats(ROW_TILES, 0, 0, 2)

            def take_scores(b, pair, j):
                if exists(b, pair):
                    taken = b * (2 * BSTEPS) + (2 * pair + j + 1)
                    mine = probs[:, pair % 2, j, :]
                    wait(dve, s_copied, taken)
                    tiles = mine.rearrange("p (i n) -> p i n", n=P)
                    nc.vector.tensor_tensor(tiles, ps_s[:, :, 0, :], tiles, ALU.add).then_inc(s_taken, 1)
                    wait(dve, s_taken, taken)
                    nc.vector.tensor_scalar(mine, mine, CLIP / SCALE, -CLIP / SCALE, ALU.min, ALU.max).then_inc(clipped, 1)

            def step(b, t):
                tile = next_row_tile(b, t)
                if tile is not None:
                    wait(dve, stats_ready, tile + 1)
                take_scores(b, t - VALUE_LAG, 1)
                if tile is not None:
                    row_variance(tile, t // 2 % 2)
                pair = t - VALUE_LAG - 1
                if exists(b, pair):
                    n = b * BSTEPS + pair
                    m = pair % STEPS
                    mine = acc[:, 2 * m:2 * m + 2, :]
                    got = ps_o[:, 0:2 * (DHEAD + 1)].rearrange("p (h e) -> p h e", h=2)
                    chunk = pair // STEPS % CHUNKS
                    wait(dve, o_ready, n + 1)
                    whose = b + pair // BSTEPS
                    if chunk == 0 and m == 0:
                        wait(dve, attn_ready, PAIRS * whose)
                    if chunk == 0 and m == 2:
                        wait(dve, attn_stored, 16 * whose)
                    if chunk == 0:
                        nc.vector.tensor_copy(mine, got).then_inc(o_added, 1)
                    else:
                        wait(dve, o_added, n - (STEPS - 1))
                        nc.vector.tensor_tensor(mine, got, mine, ALU.add).then_inc(o_added, 1)
                    if chunk == CHUNKS - 1:
                        wait(dve, o_added, n + 1)
                        if m >= 1:
                            wait(dve, attn_ready, PAIRS * whose + m)
                        nc.vector.reciprocal(recip[:], acc[:, 2 * m:2 * m + 2, DHEAD]).then_inc(recip_ready, 1)
                        wait(dve, recip_ready, PAIRS * whose + (m + 1))
                        for j in range(2):
                            h = 2 * m + j
                            out = nc.vector.tensor_scalar(attn[:, h * DHEAD:(h + 1) * DHEAD], acc[:, h, 0:DHEAD],
                                                          recip[:, j:j + 1], None, ALU.mult)
                        out.then_inc(attn_ready, 1)
                if exists(b, t - 1):
                    n = b * BSTEPS + (t - 1)
                    group = b * (BSTEPS // 2) + (t - 1) // 2
                    angles = slice((t - 1) // STEPS % CHUNKS * CHUNK, (t - 1) // STEPS % CHUNKS * CHUNK + CHUNK)
                    wait(dve, k_ready, n + 1)
                    if t % 2 == 1:
                        slot = ((t - 1) // 2 - 1) % 2
                        turns = b * (BSTEPS // 4) + ((t - 1) // 2 - 1) // 2 + 1
                        wait(dve, keys_landed[slot], 64 * turns)
                        nc.vector.tensor_tensor(a_cos[:], ps_k[:, 0, :], cos[:, angles], ALU.mult)
                        nc.vector.tensor_tensor(a_sin[:], ps_k[:, 0, :], sin[:, angles], ALU.mult).then_inc(k_turned, 1)
                    else:
                        nc.vector.tensor_tensor(b_sin[:], ps_k[:, 1, :], sin[:, angles], ALU.mult)
                        nc.vector.tensor_tensor(b_cos[:], ps_k[:, 1, :], cos[:, angles], ALU.mult).then_inc(k_turned, 1)
                        wait(dve, k_turned, n + 1)
                        nc.vector.tensor_tensor(a_cos[:], a_cos[:], b_sin[:], ALU.subtract).then_inc(rope_ready, 1)
                        nc.vector.tensor_tensor(b_cos[:], b_cos[:], a_sin[:], ALU.add).then_inc(rope_ready, 1)
                take_scores(b, t - SCORE_LAG, 0)
                tile = next_row_tile(b, t)
                if tile is not None:
                    row_norm(tile, t // 2 % ROW_TILES, t // 2 % 2)
                tile = next_row_tile(b, t - 1)
                if tile is not None:
                    rows_full(tile, t // 2 % 2)
                tile = next_row_tile(b, t + 1)
                if tile is not None:
                    i = (t + 1) // 2
                    row_stats(tile, i % ROW_TILES, i % 2, b * CHUNKS + (i // ROW_TILES + 2))

            run(dve, step)

        @block.tensor
        def _(pe):
            def turn_rows(tile, slot):
                wait(pe, row_ready, tile + 1)
                wait(pe, full_ready, tile)
                for k in range(KT):
                    tr = nc.tensor.transpose(ps_tr[:, k, :], row_in[:, slot, k * P:(k + 1) * P], keep["ident"][:])
                tr.then_inc(tr_ready, 1)

            for i in range(ROW_TILES):
                turn_rows(i, i)

            def product(out, left, right, first, last):
                nc.tensor.matmul(out, left[0], right[0], start=first, stop=False)
                nc.tensor.matmul(out, left[0], right[1], start=False, stop=False)
                return nc.tensor.matmul(out, left[1], right[0], start=False, stop=last)

            def score(b, pair, j):
                if exists(b, pair):
                    m = pair % STEPS
                    slot = pair // 2 % 2
                    if j == 0:
                        wait(pe, keys_landed[slot], 64 * (b * (BSTEPS // 4) + pair // 4 + 1))
                        wait(pe, q_landed[m], 16 * (b + (pair // BSTEPS + 1)))
                    wait(pe, s_taken, b * (2 * BSTEPS) + (2 * pair + j))
                    for i in range(ROW_TILES):
                        mm = nc.tensor.matmul(ps_s[:, i], keys[:, slot, 2 * (pair % 2) + j, i * P:(i + 1) * P],
                                              queries[:, m, j], start=True, stop=True)
                    mm.then_inc(s_ready, 1)

            def step(b, t):
                p = t % STEPS
                buf = t // STEPS % 2
                if exists(b, t):
                    n = b * BSTEPS + t
                    if p == 0:
                        wait(pe, lo_ready, b * ROWS_OF_BATCH + (t // 2 + ROW_TILES))
                    wait(pe, v_stored, n - 1)
                    for k in range(KT):
                        cols = slice(p % ROW_TILES * P, (p % ROW_TILES + 1) * P)
                        heads = slice(p // ROW_TILES * 512, (p // ROW_TILES + 1) * 512)
                        mm = product(ps_v[:, t % 2, :], (x_hi[:, buf, k, cols], x_lo[:, buf, k, cols]),
                                     (wv_hi[:, k, heads], wv_lo[:, k, heads]), k == 0, k == KT - 1)
                    mm.then_inc(v_ready, 1)
                score(b, t - SCORE_LAG, 0)
                if exists(b, t):
                    n = b * BSTEPS + t
                    wait(pe, k_turned, n - 1)
                    for k in range(KT):
                        cols = slice(p * P, (p + 1) * P)
                        mm = product(ps_k[:, t % 2, :], (wk_hi[:, k, cols], wk_lo[:, k, cols]),
                                     (x_hi[:, buf, k, :], x_lo[:, buf, k, :]), k == 0, k == KT - 1)
                    mm.then_inc(k_ready, 1)
                score(b, t - SCORE_LAG, 1)
                pair = t - VALUE_LAG
                if exists(b, pair):
                    n = b * BSTEPS + pair
                    m = pair % STEPS
                    wait(pe, probs_ready, n + 1)
                    wait(pe, o_added, n)
                    wait(pe, v_stored, b * BSTEPS + (pair - m + 4 * (m // 4 + 1)))
                    for j in range(2):
                        for i in range(ROW_TILES):
                            mm = nc.tensor.matmul(ps_o[:, j * (DHEAD + 1):(j + 1) * (DHEAD + 1)],
                                                  probs[:, pair % 2, j, i * P:(i + 1) * P], v[:, i, 2 * m + j, :],
                                                  start=(i == 0), stop=(i == ROW_TILES - 1))
                    mm.then_inc(o_ready, 1)
                tile = next_row_tile(b, t)
                if tile is not None:
                    turn_rows(tile, t // 2 % ROW_TILES)

            run(pe, step)


def mix(nc, d, keep):
    with ExitStack() as ctx:
        def sb(name, shape, dt=F32):
            return ctx.enter_context(nc.sbuf_tensor(name, shape, dt))

        def sem(name):
            return ctx.enter_context(nc.semaphore(name))

        x3, xt_hi, xt_lo, weight_rows = (keep[n] for n in ("x3", "xt_hi", "xt_lo", "weight_rows"))
        ident = keep["ident"]
        attn = sb("c_attn", [P, BATCH, INNER])
        attn_t = sb("attn_t", [P, INNER // P, TOKENS])
        wo = sb("wo", [P, INNER // P, DIM])
        x_res = sb("x_res", [P, BATCH, DIM])
        bo = sb("bo", [P, DIM])
        qkv_w = sb("qkv_w", [P, KT, 3 * DIM])
        qkv_b = sb("qkv_b", [P, 3 * DIM])
        proj_w = sb("proj_w", [P, KT, DIM])
        proj_b = sb("proj_b", [P, DIM])
        router_w = sb("router_w", [P, KT, EXPERTS])
        x_norm = sb("x_norm", [P, BATCH, DIM])
        x_t = sb("x_t", [P, KT, TOKENS])
        qkv = sb("qkv", [P, BATCH, 3 * DIM])
        out_t = sb("out_t", [P, KT, TOKENS])
        stats = sb("c_stats", [P, BATCH, 6])
        mean_var = sb("c_mean_var", [P, BATCH, 2])
        var_eps = sb("c_var_eps", [P, BATCH])
        rstd = sb("c_rstd", [P, BATCH])
        sums = sb("sums", [P, BATCH, 2 * LHEADS])
        norms = sb("norms", [P, BATCH, 2 * LHEADS])
        half = sb("half", [P, BATCH, 2 * LHEADS])
        block_mask = sb("block_mask", [P, P])
        pick = sb("pick", [ALL_EXPERTS, ALL_EXPERTS, P])
        weights_t = sb("weights_t", [ALL_EXPERTS, TOKENS])
        numbers = sb("numbers", [P, EXPERTS])
        top = sb("top", [P, BATCH, 8])
        top_at = sb("top_at", [P, BATCH, 8], U32)
        top_atf = sb("top_atf", [P, BATCH, 8])
        routed = sb("routed", [P, BATCH, EXPERTS])
        chosen = sb("chosen", [P, 2, BATCH, EXPERTS])
        peak = sb("peak", [P, BATCH])
        total = sb("total", [P, BATCH])
        squares = attn
        kv = attn_t[:, 0:KT, :]
        q_t = attn_t[:, KT:2 * KT, :]
        ps = ctx.enter_context(nc.psum_tensor("c_ps", [P, 8, 512], F32))

        attn_landed = [sem(f"c_attn_landed{i}") for i in range(BATCH)]
        x_landed = sem("c_x_landed")
        small_landed = sem("c_small_landed")
        wo_landed = sem("c_wo_landed")
        qkv_landed = sem("c_qkv_landed")
        proj_landed = sem("c_proj_landed")
        const_ready = sem("c_const_ready")
        attn_turned = sem("c_attn_turned")
        attn_t_ready = [sem(f"c_attn_t_ready{i}") for i in range(2)]
        wo_done = sem("c_wo_done")
        dve_step = sem("c_dve_step")
        var_ready = sem("c_var_ready")
        rstd_ready = sem("c_rstd_ready")
        norm_ready = sem("c_norm_ready")
        x_turned = sem("c_x_turned")
        x_t_ready = sem("c_x_t_ready")
        qkv_done = sem("c_qkv_done")
        qkv_ready = sem("c_qkv_ready")
        sums_ready = sem("c_sums_ready")
        roots_ready = sem("c_roots_ready")
        unit_ready = sem("c_unit_ready")
        kv_done = sem("c_kv_done")
        kv_ready = sem("c_kv_ready")
        q_turned = sem("c_q_turned")
        q_t_ready = sem("c_q_t_ready")
        out_done = sem("c_out_done")
        out_t_ready = sem("c_out_t_ready")
        proj_done = sem("c_proj_done")
        hi_ready = sem("c_hi_ready")
        lo_ready = sem("c_lo_ready")
        logits_done = sem("c_logits_done")
        shifted_ready = sem("c_shifted_ready")
        exp_ready = sem("c_exp_ready")
        chosen_ready = sem("c_chosen_ready")
        weights_turned = sem("c_weights_turned")
        weights_t_ready = sem("c_weights_t_ready")
        rows_done = sem("c_rows_done")
        rows_ready = sem("c_rows_ready")

        def rows_of(name, width):
            return bass.AP(d[name].tensor, 0, [[0, P], [1, width]])

        def tiles(name):
            return d[name].rearrange("(t p) n -> p t n", p=P)

        def qkv_bank(b, j):
            return (3 * b + j) % 8

        block = ctx.enter_context(nc.Block())

        @block.sync
        def _(sp):
            for b in range(BATCH):
                sp.dma_start(attn[:, b, :], d["attn_scratch"][b]).then_inc(attn_landed[b], 16)
            sp.dma_start(wo[:], tiles("wo")).then_inc(wo_landed, 16)
            sp.dma_start(x_res[:], d["x"].rearrange("b n d -> n b d")).then_inc(x_landed, 16)
            sp.dma_start(bo[:], rows_of("bo", DIM)).then_inc(small_landed, 16)
            sp.dma_start(qkv_b[:], rows_of("qkv_b", 3 * DIM)).then_inc(small_landed, 16)
            sp.dma_start(proj_b[:], rows_of("proj_b", DIM)).then_inc(small_landed, 16)
            sp.dma_start(router_w[:], tiles("router_w")).then_inc(small_landed, 16)
            sp.dma_start(qkv_w[:], tiles("qkv_w")).then_inc(qkv_landed, 16)
            sp.dma_start(proj_w[:], tiles("proj_w")).then_inc(proj_landed, 16)

        @block.gpsimd
        def _(pool):
            nc.gpsimd.memset(block_mask[:], 0.0).then_inc(const_ready, 1)
            nc.gpsimd.memset(pick[:], 0.0).then_inc(const_ready, 1)
            nc.gpsimd.memset(weights_t[:], 1.0).then_inc(const_ready, 1)
            nc.gpsimd.memset(half[:], 0.5).then_inc(const_ready, 1)
            for e in range(EXPERTS):
                number = nc.gpsimd.memset(numbers[:, e:e + 1], float(e))
            number.then_inc(const_ready, 1)
            pool.wait_ge(const_ready, 5)
            for g in range(GROUP):
                nc.gpsimd.memset(block_mask[g * LD:(g + 1) * LD, g * LD:(g + 1) * LD], 1.0).then_inc(const_ready, 1)
                pool.wait_ge(const_ready, 5 + g + 1)
            nc.gpsimd.affine_select(out=pick[:], in_=pick[:], compare_op=ALU.not_equal, fill=1.0, base=0,
                                    pattern=[[-1, ALL_EXPERTS], [0, P]], channel_multiplier=1).then_inc(const_ready, 1)
            pool.wait_ge(const_ready, 5 + GROUP + 1)
            pool.wait_ge(var_ready, 1)
            nc.gpsimd.tensor_tensor(rstd[:], var_eps[:], keep["minus_half"][:, 0:BATCH], ALU.pow).then_inc(rstd_ready, 1)
            pool.wait_ge(sums_ready, 1)
            nc.gpsimd.tensor_tensor(norms[:], sums[:], half[:], ALU.pow).then_inc(roots_ready, 1)
            pool.wait_ge(var_ready, 2)
            nc.gpsimd.tensor_tensor(rstd[:], var_eps[:], keep["minus_half"][:, 0:BATCH], ALU.pow).then_inc(rstd_ready, 1)

        @block.scalar
        def _(act):
            def turned(out, bank, done):
                nc.scalar.activation(out, ps[:, bank, :].rearrange("p (t n) -> p t n", n=P), ACT.Copy).then_inc(done, 1)

            for b in range(BATCH):
                act.wait_ge(attn_turned, 2 * b + 2)
                turned(attn_t[:, KT:2 * KT, b * P:(b + 1) * P], 2 * b + 1, attn_t_ready[1])
            for b in range(BATCH):
                act.wait_ge(x_turned, b + 1)
                turned(x_t[:, :, b * P:(b + 1) * P], 4 + b, x_t_ready)
            for b in range(BATCH):
                act.wait_ge(q_turned, b + 1)
                turned(q_t[:, :, b * P:(b + 1) * P], 4 + b, q_t_ready)
            for b in range(BATCH):
                act.wait_ge(out_done, b + 1)
                turned(out_t[:, :, b * P:(b + 1) * P], b, out_t_ready)
            for b in range(BATCH):
                act.wait_ge(x_turned, BATCH + b + 1)
                cols = slice(b * P, (b + 1) * P)
                turned(x_t[:, :, cols], b, x_t_ready)
                turned(xt_hi[:, :, cols], b, hi_ready)
            act.wait_ge(shifted_ready, 1)
            nc.scalar.activation(routed[:], routed[:], ACT.Exp).then_inc(exp_ready, 1)
            for e in range(ALL_EXPERTS):
                act.wait_ge(rows_done, e + 1)
                nc.scalar.activation(weight_rows[:, e, :], ps[:, e % 2, :], ACT.Copy).then_inc(rows_ready, 1)

        @block.vector
        def _(dve):
            chain = [0]

            def link(ins):
                chain[0] += 1
                ins.then_inc(dve_step, 1)
                dve.wait_ge(dve_step, chain[0])

            def layer_norm(source, turn):
                for b in range(BATCH):
                    stat = nc.vector.bn_stats(stats[:, b, :], source[:, b, :])
                link(stat)
                for b in range(BATCH):
                    stat = nc.vector.bn_aggr(mean_var[:, b, :], stats[:, b, :])
                link(stat)
                nc.vector.tensor_scalar(var_eps[:], mean_var[:, :, 1], EPS, None, ALU.add).then_inc(var_ready, 1)
                dve.wait_ge(rstd_ready, turn)
                for b in range(BATCH):
                    nc.vector.tensor_scalar(x_norm[:, b, :], source[:, b, :], mean_var[:, b, 0:1],
                                            rstd[:, b:b + 1], ALU.subtract, ALU.mult).then_inc(norm_ready, 1)

            for b in range(BATCH):
                dve.wait_ge(attn_turned, 2 * b + 1)
                nc.vector.tensor_copy(attn_t[:, 0:KT, b * P:(b + 1) * P],
                                      ps[:, 2 * b, :].rearrange("p (t n) -> p t n", n=P)).then_inc(attn_t_ready[0], 1)
            dve.wait_ge(x_landed, 16)
            dve.wait_ge(small_landed, 16 * 4)
            for b in range(BATCH):
                add = nc.vector.tensor_tensor(x_res[:, b, :], x_res[:, b, :], bo[:], ALU.add)
            link(add)
            for b in range(BATCH):
                dve.wait_ge(wo_done, b + 1)
                add = nc.vector.tensor_tensor(x_res[:, b, :], ps[:, b, :], x_res[:, b, :], ALU.add)
            link(add)
            layer_norm(x_res, 1)
            for b in range(BATCH):
                for j in range(3):
                    dve.wait_ge(qkv_done, 3 * b + j + 1)
                    add = nc.vector.tensor_tensor(qkv[:, b, j * DIM:(j + 1) * DIM], ps[:, qkv_bank(b, j), :],
                                                  qkv_b[:, j * DIM:(j + 1) * DIM], ALU.add).then_inc(qkv_ready, 1)
            dve.wait_ge(qkv_ready, 3 * BATCH)
            for b in range(BATCH):
                square = nc.vector.tensor_tensor(squares[:, b, :], qkv[:, b, 0:2 * DIM], qkv[:, b, 0:2 * DIM], ALU.mult)
            link(square)
            for b in range(BATCH):
                red = nc.vector.tensor_reduce(sums[:, b, :], squares[:, b, :].rearrange("p (h e) -> p h e", e=LD), AX_X, ALU.add)
            red.then_inc(sums_ready, 1)
            dve.wait_ge(roots_ready, 1)
            link(nc.vector.tensor_scalar(norms[:], norms[:], NORM_EPS, None, ALU.max))
            link(nc.vector.reciprocal(norms[:], norms[:]))
            for b in range(BATCH):
                heads = qkv[:, b, 0:2 * DIM].rearrange("p (h e) -> p h e", e=LD)
                scale = norms[:, b, :].unsqueeze(2).to_broadcast([P, 2 * LHEADS, LD])
                nc.vector.tensor_tensor(heads, heads, scale, ALU.mult).then_inc(unit_ready, 1)
            dve.wait_ge(const_ready, 5 + GROUP + 1)
            for b in range(BATCH):
                dve.wait_ge(kv_done, b + 1)
                nc.vector.tensor_tensor(kv[:, :, b * P:(b + 1) * P], ps[:, b, :].rearrange("p (t n) -> p t n", n=P),
                                        block_mask[:].unsqueeze(1).to_broadcast([P, KT, P]), ALU.mult).then_inc(kv_ready, 1)
            for b in range(BATCH):
                add = nc.vector.tensor_tensor(x_res[:, b, :], x_res[:, b, :], proj_b[:], ALU.add)
            link(add)
            for b in range(BATCH):
                dve.wait_ge(proj_done, b + 1)
                add = nc.vector.tensor_tensor(x3[:, b, :], ps[:, 4 + b, :], x_res[:, b, :], ALU.add)
            link(add)
            layer_norm(x3, 2)
            for b in range(BATCH):
                cols = slice(b * P, (b + 1) * P)
                dve.wait_ge(hi_ready, b + 1)
                nc.vector.tensor_tensor(xt_lo[:, :, cols], x_t[:, :, cols], xt_hi[:, :, cols].bitcast(F32),
                                        ALU.subtract).then_inc(lo_ready, 1)
            dve.wait_ge(logits_done, 1)
            logits = ps[:, 4, 0:BATCH * EXPERTS].rearrange("p (b e) -> p b e", b=BATCH)
            link(nc.vector.tensor_reduce(peak[:], logits, AX_X, ALU.max))
            for b in range(BATCH):
                shift = nc.vector.tensor_scalar(routed[:, b, :], logits[:, b, :], peak[:, b:b + 1], None, ALU.subtract)
            shift.then_inc(shifted_ready, 1)
            dve.wait_ge(exp_ready, 1)
            link(nc.vector.tensor_reduce(total[:], routed[:], AX_X, ALU.add))
            link(nc.vector.reciprocal(total[:], total[:]))
            for b in range(BATCH):
                prob = nc.vector.tensor_scalar(routed[:, b, :], routed[:, b, :], total[:, b:b + 1], None, ALU.mult)
            link(prob)
            for b in range(BATCH):
                best = nc.vector.max(top[:, b, :], routed[:, b, :])
            link(best)
            for b in range(BATCH):
                where = nc.vector.max_index(top_at[:, b, :], top[:, b, :], routed[:, b, :])
            link(where)
            nc.vector.tensor_copy(top_atf[:], top_at[:])
            link(nc.vector.tensor_tensor(peak[:], top[:, :, 0], top[:, :, 1], ALU.add))
            link(nc.vector.tensor_scalar(peak[:], peak[:], 1e-9, None, ALU.add))
            link(nc.vector.reciprocal(peak[:], peak[:]))
            for b in range(BATCH):
                scaled = nc.vector.tensor_scalar(top[:, b, 0:2], top[:, b, 0:2], peak[:, b:b + 1], None, ALU.mult)
            link(scaled)
            for k in range(2):
                for b in range(BATCH):
                    part = nc.vector.tensor_scalar(chosen[:, k, b, :], numbers[:], top_atf[:, b, k:k + 1],
                                                   top[:, b, k:k + 1], ALU.is_equal, ALU.mult)
            link(part)
            nc.vector.tensor_tensor(chosen[:, 0], chosen[:, 0], chosen[:, 1], ALU.add).then_inc(chosen_ready, 1)
            dve.wait_ge(weights_turned, 1)
            nc.vector.tensor_copy(weights_t[0:EXPERTS, :], ps[0:EXPERTS, 5, :]).then_inc(weights_t_ready, 1)

        @block.tensor
        def _(pe):
            def turn(out_bank, source, done):
                for t in range(KT):
                    tr = nc.tensor.transpose(ps[:, out_bank, t * P:(t + 1) * P], source[:, t * P:(t + 1) * P], ident[:])
                tr.then_inc(done, 1)

            for b in range(BATCH):
                pe.wait_ge(attn_landed[b], 16)
                turn(2 * b, attn[:, b, 0:DIM], attn_turned)
                turn(2 * b + 1, attn[:, b, DIM:2 * DIM], attn_turned)
            pe.wait_ge(wo_landed, 16)
            for b in range(BATCH):
                pe.wait_ge(attn_t_ready[0], b + 1)
                pe.wait_ge(attn_t_ready[1], b + 1)
                for t in range(INNER // P):
                    mm = nc.tensor.matmul(ps[:, b, :], attn_t[:, t, b * P:(b + 1) * P], wo[:, t, :],
                                          start=(t == 0), stop=(t == INNER // P - 1))
                mm.then_inc(wo_done, 1)
            for b in range(BATCH):
                pe.wait_ge(norm_ready, b + 1)
                turn(4 + b, x_norm[:, b, :], x_turned)
            pe.wait_ge(qkv_landed, 16)
            for b in range(BATCH):
                pe.wait_ge(x_t_ready, b + 1 if b == 0 else BATCH)
                for j in range(3):
                    if 3 * b + j >= 8:
                        pe.wait_ge(qkv_ready, 3 * b + j - 7)
                    for t in range(KT):
                        mm = nc.tensor.matmul(ps[:, qkv_bank(b, j), :], x_t[:, t, b * P:(b + 1) * P],
                                              qkv_w[:, t, j * DIM:(j + 1) * DIM], start=(t == 0), stop=(t == KT - 1))
                    mm.then_inc(qkv_done, 1)
            for b in range(BATCH):
                pe.wait_ge(unit_ready, b + 1)
                turn(4 + b, qkv[:, b, 0:DIM], q_turned)
                for g in range(KT):
                    k = qkv[:, b, DIM + g * P:DIM + (g + 1) * P]
                    v = qkv[:, b, 2 * DIM + g * P:2 * DIM + (g + 1) * P]
                    mm = nc.tensor.matmul(ps[:, b, g * P:(g + 1) * P], k, v, start=True, stop=True)
                mm.then_inc(kv_done, 1)
            for b in range(BATCH):
                pe.wait_ge(kv_ready, b + 1)
                pe.wait_ge(q_t_ready, b + 1)
                for g in range(KT):
                    mm = nc.tensor.matmul(ps[:, b, g * P:(g + 1) * P], kv[:, g, b * P:(b + 1) * P],
                                          q_t[:, g, b * P:(b + 1) * P], start=True, stop=True)
                mm.then_inc(out_done, 1)
            pe.wait_ge(proj_landed, 16)
            for b in range(BATCH):
                pe.wait_ge(out_t_ready, b + 1)
                for t in range(KT):
                    mm = nc.tensor.matmul(ps[:, 4 + b, :], out_t[:, t, b * P:(b + 1) * P], proj_w[:, t, :],
                                          start=(t == 0), stop=(t == KT - 1))
                mm.then_inc(proj_done, 1)
            for b in range(BATCH):
                pe.wait_ge(norm_ready, BATCH + b + 1)
                turn(b, x_norm[:, b, :], x_turned)
            for b in range(BATCH):
                pe.wait_ge(x_t_ready, BATCH + b + 1)
                for t in range(KT):
                    mm = nc.tensor.matmul(ps[:, 4, b * EXPERTS:(b + 1) * EXPERTS], x_t[:, t, b * P:(b + 1) * P],
                                          router_w[:, t, :], start=(t == 0), stop=(t == KT - 1))
            mm.then_inc(logits_done, 1)
            pe.wait_ge(chosen_ready, 1)
            for b in range(BATCH):
                tr = nc.tensor.transpose(ps[0:EXPERTS, 5, b * P:(b + 1) * P], chosen[:, 0, b, :], ident[:])
            tr.then_inc(weights_turned, 1)
            pe.wait_ge(weights_t_ready, 1)
            pe.wait_ge(hi_ready, BATCH)
            for e in range(ALL_EXPERTS):
                if e >= 2:
                    pe.wait_ge(rows_ready, e - 1)
                nc.tensor.matmul(ps[:, e % 2, :], pick[:, e, :], weights_t[:], start=True, stop=True).then_inc(rows_done, 1)


def experts(nc, d, keep):
    with ExitStack() as ctx:
        def sb(name, shape, dt=F32):
            return ctx.enter_context(nc.sbuf_tensor(name, shape, dt))

        def sem(name):
            return ctx.enter_context(nc.semaphore(name))

        x3, xt_hi, xt_lo, weight_rows = (keep[n] for n in ("x3", "xt_hi", "xt_lo", "weight_rows"))
        GATE, UP, DOWN = range(3)
        NAMES = ("gate", "up", "down")
        raw = [sb(f"{n}_raw", [P, KT, DIM]) for n in NAMES]
        w_hi = [sb(f"{n}_hi", [P, KT, DIM], F32R) for n in NAMES]
        w_lo = [sb(f"{n}_lo", [P, KT, DIM], F32R) for n in NAMES]
        silu = sb("silu", [P, 2, TOKENS])
        hidden = sb("hidden", [P, 2, TOKENS])
        h_hi = sb("h_hi", [P, KT, TOKENS], F32R)
        h_lo = sb("h_lo", [P, KT, TOKENS], F32R)
        y = sb("y", [P, BATCH, DIM])
        ps_gate = ctx.enter_context(nc.psum_tensor("ps_gate", [P, 2, 512], F32))
        ps_up = ctx.enter_context(nc.psum_tensor("ps_up", [P, 2, 512], F32))
        ps_y = ctx.enter_context(nc.psum_tensor("ps_y", [P, BATCH, 512], F32))

        raw_landed = [sem(f"{n}_landed") for n in NAMES]
        raw_hi = [sem(f"{n}_hi_ready") for n in NAMES]
        raw_lo = [sem(f"{n}_lo_ready") for n in NAMES]
        gate_up_done = sem("gate_up_done")
        silu_ready = sem("silu_ready")
        product_ready = sem("product_ready")
        hidden_ready = sem("hidden_ready")
        h_hi_ready = sem("h_hi_ready")
        h_lo_ready = sem("h_lo_ready")
        down_done = sem("down_done")
        y_ready = sem("y_ready")
        y_stored = sem("y_stored")

        def run(eng, expert):
            expert(0, first=True, last=False)
            with eng.Fori(1, ALL_EXPERTS - 1) as e:
                expert(e, first=False, last=False)
            expert(ALL_EXPERTS - 1, first=False, last=True)

        block = ctx.enter_context(nc.Block())

        @block.sync
        def _(sp):
            def expert(e, first, last):
                for w in (GATE, UP, DOWN):
                    wait(sp, raw_lo[w], e)
                    sp.dma_start(raw[w][:], d[NAMES[w]][e].rearrange("(t p) n -> p t n", p=P)).then_inc(raw_landed[w], 16)

            run(sp, expert)
            for b in range(BATCH):
                sp.wait_ge(y_ready, b + 1)
                sp.dma_start(d["out"][b], y[:, b, :]).then_inc(y_stored, 16)
            sp.wait_ge(y_stored, 16 * BATCH)

        @block.scalar
        def _(act):
            def split_high(w, e):
                wait(act, raw_landed[w], 16 * (e + 1))
                if w == DOWN:
                    wait(act, down_done, e)
                else:
                    wait(act, gate_up_done, KT * e)
                nc.scalar.activation(w_hi[w][:], raw[w][:], ACT.Copy).then_inc(raw_hi[w], 1)

            split_high(GATE, 0)
            split_high(UP, 0)

            def expert(e, first, last):
                split_high(DOWN, e)
                for f in range(KT):
                    n = e * KT + f
                    wait(act, gate_up_done, n + 1)
                    wait(act, product_ready, n - 1)
                    nc.scalar.activation(silu[:, f % 2, :], ps_gate[:, f % 2, :], ACT.Silu).then_inc(silu_ready, 1)
                    wait(act, hidden_ready, n + 1)
                    nc.scalar.activation(h_hi[:, f, :], hidden[:, f % 2, :], ACT.Copy).then_inc(h_hi_ready, 1)
                if not last:
                    split_high(GATE, e + 1)
                    split_high(UP, e + 1)

            run(act, expert)

        @block.vector
        def _(dve):
            def split_low(w, e):
                wait(dve, raw_hi[w], e + 1)
                nc.vector.tensor_tensor(w_lo[w][:], raw[w][:], w_hi[w][:].bitcast(F32), ALU.subtract).then_inc(raw_lo[w], 1)

            split_low(GATE, 0)
            split_low(UP, 0)

            def expert(e, first, last):
                split_low(DOWN, e)
                for f in range(KT):
                    n = e * KT + f
                    wait(dve, silu_ready, n + 1)
                    wait(dve, h_lo_ready, n - 1)
                    nc.vector.tensor_tensor(hidden[:, f % 2, :], ps_up[:, f % 2, :], silu[:, f % 2, :], ALU.mult).then_inc(product_ready, 1)
                    wait(dve, product_ready, n + 1)
                    nc.vector.tensor_tensor(hidden[:, f % 2, :], hidden[:, f % 2, :], weight_rows[:, e, :], ALU.mult).then_inc(hidden_ready, 1)
                    wait(dve, h_hi_ready, n + 1)
                    nc.vector.tensor_tensor(h_lo[:, f, :], hidden[:, f % 2, :], h_hi[:, f, :].bitcast(F32), ALU.subtract).then_inc(h_lo_ready, 1)
                if not last:
                    split_low(GATE, e + 1)
                    split_low(UP, e + 1)

            run(dve, expert)
            dve.wait_ge(down_done, ALL_EXPERTS)
            for b in range(BATCH):
                nc.vector.tensor_tensor(y[:, b, :], ps_y[:, b, :], x3[:, b, :], ALU.add).then_inc(y_ready, 1)

        @block.tensor
        def _(pe):
            def product(out, left, right, first, last):
                nc.tensor.matmul(out, left[0], right[0], start=first, stop=False)
                nc.tensor.matmul(out, left[0], right[1], start=False, stop=False)
                return nc.tensor.matmul(out, left[1], right[0], start=False, stop=last)

            def expert(e, first, last):
                for w in (GATE, UP):
                    wait(pe, raw_lo[w], e + 1)
                for f in range(KT):
                    wait(pe, product_ready, e * KT + (f - 1))
                    for out, w in ((ps_gate, GATE), (ps_up, UP)):
                        for t in range(KT):
                            cols = slice(f * P, (f + 1) * P)
                            mm = product(out[:, f % 2, :], (w_hi[w][:, t, cols], w_lo[w][:, t, cols]),
                                         (xt_hi[:, t, :], xt_lo[:, t, :]), t == 0, t == KT - 1)
                    mm.then_inc(gate_up_done, 1)
                wait(pe, raw_lo[DOWN], e + 1)
                for t in range(KT):
                    wait(pe, h_lo_ready, e * KT + (t + 1))
                    for b in range(BATCH):
                        cols = slice(b * P, (b + 1) * P)
                        mm = product(ps_y[:, b, :], (h_hi[:, t, cols], h_lo[:, t, cols]),
                                     (w_hi[DOWN][:, t, :], w_lo[DOWN][:, t, :]),
                                     first and t == 0, last and t == KT - 1)
                mm.then_inc(down_done, 1)

            run(pe, expert)


def program(nc, d):
    d["q_scratch"] = nc.dram_tensor("q_scratch", (BATCH, PAIRS, P, 2, 2, QUERIES), F32).ap()
    d["attn_scratch"] = nc.dram_tensor("attn_scratch", (BATCH, P, INNER), F32).ap()
    with ExitStack() as ctx:
        def sb(name, shape, dt=F32):
            return ctx.enter_context(nc.sbuf_tensor(name, shape, dt))

        keep = {"ident": sb("ident", [P, P]), "minus_half": sb("minus_half", [P, 8])}
        with ExitStack() as inner:
            def sbi(name, shape, dt=F32):
                return inner.enter_context(nc.sbuf_tensor(name, shape, dt))

            for w in ("wk", "wv"):
                for part in ("hi", "lo"):
                    keep[f"{w}_{part}"] = sbi(f"{w}_{part}", [P, KT, INNER], F32R)
            keep["cos"] = sbi("cos", [P, CTX])
            keep["sin"] = sbi("sin", [P, CTX])
            keep["ctx_g"] = sbi("ctx_g", [P, KT])
            keep["ctx_b"] = sbi("ctx_b", [P, KT])
            keep["v"] = sbi("v", [P, ROW_TILES, HEADS, DHEAD + 1])
            prepare(nc, d, keep)
            attend(nc, d, keep)
        keep["x3"] = sb("x3", [P, BATCH, DIM])
        keep["xt_hi"] = sb("xt_hi", [P, KT, TOKENS], F32R)
        keep["xt_lo"] = sb("xt_lo", [P, KT, TOKENS], F32R)
        keep["weight_rows"] = sb("weight_rows", [P, ALL_EXPERTS, TOKENS])
        mix(nc, d, keep)
        experts(nc, d, keep)


def kernel(**inputs):
    import numpy as np
    import concourse.bacc as bacc
    from concourse.bass_utils import run_bass_kernel_spmd

    a = {name: np.asarray(value) for name, value in inputs.items()}

    def column(v):
        return v.reshape(KT, P).T

    wkv = a["L0_xattn_Wkv"]
    wk = wkv[:, :INNER].reshape(DIM, HEADS // 4, 4, 2, HALF).transpose(0, 1, 3, 4, 2).reshape(DIM, INNER)
    arrays = {
        "x": a["x"],
        "ctx": a["ctx_1024"],
        "lat_g": column(a["L0_xattn_ln_lat_g"]),
        "lat_b": column(a["L0_xattn_ln_lat_b"]),
        "ctx_g": column(a["L0_xattn_ln_ctx_g"]),
        "ctx_b": column(a["L0_xattn_ln_ctx_b"]),
        "cos": a["L0_xattn_cos"].T,
        "sin": a["L0_xattn_sin"].T,
        "wq": a["L0_xattn_Wq"],
        "wk": wk,
        "wv": wkv[:, INNER:],
        "wo": a["L0_xattn_Wo"],
        "bo": a["L0_xattn_bo"],
        "qkv_w": a["L0_attn_qkv_w"],
        "qkv_b": a["L0_attn_qkv_b"],
        "proj_w": a["L0_attn_proj_w"],
        "proj_b": a["L0_attn_proj_b"],
        "router_w": a["L0_ffn_router_w"],
        "gate": np.concatenate([a["L0_ffn_wg"], a["L0_ffn_sg"][None]]),
        "up": np.concatenate([a["L0_ffn_wu"], a["L0_ffn_su"][None]]),
        "down": np.concatenate([a["L0_ffn_wd"], a["L0_ffn_sd"][None]]),
    }
    nc = bacc.Bacc("TRN2", target_bir_lowering=False, num_devices=1)
    feed, d = {}, {}
    for name, value in arrays.items():
        value = np.ascontiguousarray(value)
        feed[f"in_{name}"] = value
        d[name] = nc.dram_tensor(f"in_{name}", value.shape, mybir.dt.from_np(value.dtype), kind="ExternalInput").ap()
    d["out"] = nc.dram_tensor("out_y", (BATCH, QUERIES, DIM), F32, kind="ExternalOutput").ap()
    program(nc, d)
    result = run_bass_kernel_spmd(nc, [feed], core_ids=[0])
    return result.results[0]["out_y"]
```

```python
from contextlib import ExitStack

import concourse.bass as bass
from concourse import mybir
from concourse.alu_op_type import AluOpType as ALU

F32 = mybir.dt.float32
F32R = mybir.dt.float32r
U32 = mybir.dt.uint32
ACT = mybir.ActivationFunctionType
AX_X = mybir.AxisListType.X

P = 128
BATCH = 4
QUERIES = 128
CTX = 2048
DIM = 512
KT = DIM // P
EPS = 1e-5

HEADS = 16
DHEAD = 64
HALF = DHEAD // 2
INNER = HEADS * DHEAD
CLIP = 11.0
SCALE = DHEAD ** -0.5
CHUNK = 512
ROW_TILES = CHUNK // P
CHUNKS = CTX // CHUNK
STEPS = 8
BSTEPS = STEPS * CHUNKS
PAIRS = HEADS // 2
SCORE_LAG = 3
VALUE_LAG = 4

LHEADS = 16
LD = DIM // LHEADS
NORM_EPS = 1e-12
GROUP = P // LD

EXPERTS = 8
ALL_EXPERTS = EXPERTS + 1
GATE, UP, DOWN = range(3)
WEIGHTS = ("gate", "up", "down")
TOKENS = BATCH * QUERIES


def wait(eng, sem, value):
    if isinstance(value, int) and value <= 0:
        return
    eng.wait_ge(sem, value)




def context_rows(nc, ctx, d, keep):
    def sb(name, shape, dt=F32):
        return ctx.enter_context(nc.sbuf_tensor(name, shape, dt))

    def sem(name):
        return ctx.enter_context(nc.semaphore(name))

    r = {}
    r["ident"], r["minus_half"], r["ctx_g"], r["ctx_b"] = (keep[n] for n in ("ident", "minus_half", "ctx_g", "ctx_b"))
    r["source"] = d["ctx"].rearrange("b (t p) d -> (b t) p d", p=P)
    r["row_in"] = keep["row_in"]
    r["stats"] = sb("stats", [P, ROW_TILES, 6])
    r["mean_var"] = sb("mean_var", [P, ROW_TILES, 2])
    r["var_eps"] = sb("var_eps", [P, ROW_TILES])
    r["rstd"] = sb("rstd", [P, ROW_TILES])
    r["x_full"] = keep["x_full"]
    r["x_hi"] = keep["x_hi"]
    r["x_lo"] = sb("x_lo", [P, 2, KT, CHUNK], F32R)
    r["ps_tr"] = ctx.enter_context(nc.psum_tensor("ps_tr", [P, KT, P], F32))
    r["row_landed"] = [sem(f"row_landed{i}") for i in range(ROW_TILES)]
    r["stats_ready"] = sem("stats_ready")
    r["mean_ready"] = sem("mean_ready")
    r["var_ready"] = sem("var_ready")
    r["rstd_ready"] = sem("rstd_ready")
    r["row_ready"] = sem("row_ready")
    r["tr_ready"] = sem("tr_ready")
    r["full_ready"] = sem("full_ready")
    r["hi_ready"] = sem("hi_ready")
    r["lo_ready"] = sem("lo_ready")
    return r


def load_row_tile(nc, r, sp, tile, slot):
    wait(sp, r["tr_ready"], tile - (ROW_TILES - 1))
    sp.dma_start(r["row_in"][:, slot, :], r["source"][tile]).then_inc(r["row_landed"][slot], 16)


def measure_row_tile(nc, r, dve, tile, slot, turn):
    wait(dve, r["row_landed"][slot], 16 * turn)
    wait(dve, r["row_ready"], tile - (ROW_TILES - 1))
    nc.vector.bn_stats(r["stats"][:, slot, :], r["row_in"][:, slot, :]).then_inc(r["stats_ready"], 1)


def row_tile_variance(nc, r, dve, tile, slot):
    var = r["mean_var"][:, slot, 1:2]
    nc.vector.bn_aggr(r["mean_var"][:, slot, :], r["stats"][:, slot, :]).then_inc(r["mean_ready"], 1)
    wait(dve, r["mean_ready"], tile + 1)
    nc.vector.tensor_scalar(r["var_eps"][:, slot:slot + 1], var, EPS, None, ALU.add).then_inc(r["var_ready"], 1)


def row_tile_power(nc, r, pool, tile, slot):
    wait(pool, r["var_ready"], tile + 1)
    nc.gpsimd.tensor_tensor(r["rstd"][:, slot:slot + 1], r["var_eps"][:, slot:slot + 1],
                            r["minus_half"][:, 0:1], ALU.pow).then_inc(r["rstd_ready"], 1)


def normalise_row_tile(nc, r, dve, tile, slot):
    wait(dve, r["rstd_ready"], tile + 1)
    nc.vector.tensor_scalar(r["row_in"][:, slot, :], r["row_in"][:, slot, :], r["mean_var"][:, slot, 0:1],
                            r["rstd"][:, slot:slot + 1], ALU.subtract, ALU.mult).then_inc(r["row_ready"], 1)


def transpose_row_tile(nc, r, pe, tile, slot):
    wait(pe, r["row_ready"], tile + 1)
    wait(pe, r["full_ready"], tile)
    for k in range(KT):
        tr = nc.tensor.transpose(r["ps_tr"][:, k, :], r["row_in"][:, slot, k * P:(k + 1) * P], r["ident"][:])
    tr.then_inc(r["tr_ready"], 1)


def scale_row_tile(nc, r, dve, tile, slot):
    wait(dve, r["tr_ready"], tile + 1)
    wait(dve, r["lo_ready"], tile - 1)
    for k in range(KT):
        out = nc.vector.tensor_scalar(r["x_full"][:, slot % 2, k, :], r["ps_tr"][:, k, :], r["ctx_g"][:, k:k + 1],
                                      r["ctx_b"][:, k:k + 1], ALU.mult, ALU.add)
    out.then_inc(r["full_ready"], 1)


def row_tile_high(nc, r, act, tile, buf, slot):
    wait(act, r["full_ready"], tile + 1)
    nc.scalar.activation(r["x_hi"][:, buf, :, slot * P:(slot + 1) * P], r["x_full"][:, slot % 2],
                         ACT.Copy).then_inc(r["hi_ready"], 1)


def row_tile_low(nc, r, pool, tile, buf, slot):
    wait(pool, r["hi_ready"], tile + 1)
    cols = slice(slot * P, (slot + 1) * P)
    nc.gpsimd.tensor_tensor(r["x_lo"][:, buf, :, cols], r["x_full"][:, slot % 2],
                            r["x_hi"][:, buf, :, cols].bitcast(F32), ALU.subtract).then_inc(r["lo_ready"], 1)


def prepare(nc, d, keep, rows):
    with ExitStack() as ctx:
        def sb(name, shape, dt=F32):
            return ctx.enter_context(nc.sbuf_tensor(name, shape, dt))

        def sem(name):
            return ctx.enter_context(nc.semaphore(name))

        x_in = sb("x_in", [P, BATCH, DIM])
        wq = sb("wq", [P, KT, INNER])
        w_raw = sb("w_raw", [P, 2, INNER])
        lat_g = sb("lat_g", [P, KT])
        lat_b = sb("lat_b", [P, KT])
        stats = sb("a_stats", [P, BATCH, 6])
        mean_var = sb("a_mean_var", [P, BATCH, 2])
        var_eps = sb("a_var_eps", [P, BATCH])
        rstd = sb("a_rstd", [P, BATCH])
        lat_t = sb("lat_t", [P, KT, TOKENS])
        q_stage = sb("q_stage", [P, 2, BATCH, 2, QUERIES], F32R)
        ps = ctx.enter_context(nc.psum_tensor("a_ps", [P, 7, 512], F32))

        x_landed = [sem(f"a_x_landed{i}") for i in range(BATCH)]
        small_landed = sem("a_small_landed")
        angles_landed = sem("a_angles_landed")
        wq_landed = sem("a_wq_landed")
        raw_landed = [sem(f"a_raw_landed{i}") for i in range(2)]
        raw_hi = sem("a_raw_hi")
        raw_lo = sem("a_raw_lo")
        const_ready = sem("a_const_ready")
        dve_step = sem("a_dve_step")
        var_ready = sem("a_var_ready")
        rstd_ready = sem("a_rstd_ready")
        norm_ready = sem("a_norm_ready")
        tr_ready = sem("a_tr_ready")
        lat_ready = sem("a_lat_ready")
        q_ready = sem("a_q_ready")
        q_hi = sem("a_q_hi")
        q_lo = sem("a_q_lo")
        q_stored = keep["q_stored"]

        pieces = [(w, k) for w in ("wv", "wk") for k in range(KT)]

        def piece(part, n):
            w, k = pieces[n]
            return keep[f"{w}_{part}"][:, k, :]

        def q_bank(m):
            return (BATCH + m) % 7

        def by_batch(m):
            return ps[:, q_bank(m), :].rearrange("p (b n) -> p b n", n=QUERIES)

        block = ctx.enter_context(nc.Block())

        @block.sync
        def _(sp):
            for b in range(BATCH):
                sp.dma_start(x_in[:, b, :], d["x"][b]).then_inc(x_landed[b], 16)
            for n, to in (("lat_g", lat_g), ("lat_b", lat_b), ("ctx_g", keep["ctx_g"]), ("ctx_b", keep["ctx_b"])):
                sp.dma_start(to[:], d[n]).then_inc(small_landed, 16)
            for i in range(ROW_TILES):
                load_row_tile(nc, rows, sp, i, i)
            sp.dma_start(wq[:], d["wq"].rearrange("(t p) n -> p t n", p=P)).then_inc(wq_landed, 16)

            def load_piece(n):
                if n >= 2:
                    sp.wait_ge(raw_lo, n - 1)
                w, k = pieces[n]
                sp.dma_start(w_raw[:, n % 2], d[w][k * P:(k + 1) * P, :]).then_inc(raw_landed[n % 2], 16)

            load_piece(0)
            load_piece(1)
            for m in range(PAIRS):
                if m + 2 < len(pieces):
                    load_piece(m + 2)
                if m < 2:
                    n = ("cos", "sin")[m]
                    angles = bass.AP(d[n].tensor, 0, [[CTX, HALF], [0, P // HALF], [1, CTX]])
                    sp.dma_start(keep[n], angles).then_inc(angles_landed, 16)
                if m == 4:
                    load_row_tile(nc, rows, sp, ROW_TILES, 0)
                sp.wait_ge(q_lo, m + 1)
                sp.dma_start(d["q_scratch"][m], q_stage[:, m % 2].rearrange("p b w n -> p b (w n)").bitcast(F32)).then_inc(q_stored[m % 2], 16)
            sp.wait_ge(angles_landed, 16 * 2)

        @block.gpsimd
        def _(pool):
            nc.gpsimd.memset(keep["ident"][:], 0.0).then_inc(const_ready, 1)
            nc.gpsimd.memset(keep["minus_half"][:], -0.5).then_inc(const_ready, 1)
            nc.gpsimd.memset(keep["v"][:, :, :, DHEAD:DHEAD + 1], 1.0).then_inc(const_ready, 1)
            pool.wait_ge(const_ready, 3)
            nc.gpsimd.affine_select(out=keep["ident"][:], in_=keep["ident"][:], compare_op=ALU.not_equal, fill=1.0,
                                    base=0, pattern=[[-1, P]], channel_multiplier=1).then_inc(const_ready, 1)

            def latent_power(r):
                pool.wait_ge(var_ready, r + 1)
                nc.gpsimd.tensor_tensor(rstd[:], var_eps[:], keep["minus_half"][:, 0:BATCH], ALU.pow).then_inc(rstd_ready, 1)

            def weights_low(n):
                pool.wait_ge(raw_hi, n + 1)
                nc.gpsimd.tensor_tensor(piece("lo", n), w_raw[:, n % 2], piece("hi", n).bitcast(F32),
                                        ALU.subtract).then_inc(raw_lo, 1)

            latent_power(0)
            latent_power(1)
            for i in range(ROW_TILES):
                row_tile_power(nc, rows, pool, i, i)
            weights_low(0)
            weights_low(1)
            for i in range(ROW_TILES):
                row_tile_low(nc, rows, pool, i, 0, i)
                weights_low(i + 2)
            for n in range(ROW_TILES + 2, len(pieces)):
                weights_low(n)

        @block.scalar
        def _(act):
            def weights_high(n):
                act.wait_ge(raw_landed[n % 2], 16 * (n // 2 + 1))
                nc.scalar.activation(piece("hi", n), w_raw[:, n % 2], ACT.Copy).then_inc(raw_hi, 1)

            def queries_high(m):
                act.wait_ge(q_ready, m + 1)
                if m >= 2:
                    act.wait_ge(q_stored[m % 2], 16 * (m // 2))
                nc.scalar.activation(q_stage[:, m % 2, :, 0, :], by_batch(m), ACT.Copy).then_inc(q_hi, 1)

            weights_high(0)
            weights_high(1)
            for m in range(PAIRS):
                queries_high(m)
                if m < ROW_TILES:
                    row_tile_high(nc, rows, act, m, 0, m)
                if m + 2 < len(pieces):
                    weights_high(m + 2)

        @block.vector
        def _(dve):
            chain = [0]

            def link(ins):
                chain[0] += 1
                ins.then_inc(dve_step, 1)
                dve.wait_ge(dve_step, chain[0])

            def latent_variances(r):
                for b in range(BATCH):
                    if r == 0:
                        dve.wait_ge(x_landed[b], 16)
                    stat = nc.vector.bn_stats(stats[:, b, :], x_in[:, b, :])
                link(stat)
                for b in range(BATCH):
                    stat = nc.vector.bn_aggr(mean_var[:, b, :], stats[:, b, :])
                link(stat)
                nc.vector.tensor_scalar(var_eps[:], mean_var[:, :, 1], EPS, None, ALU.add).then_inc(var_ready, 1)

            def latent_norm(r):
                dve.wait_ge(rstd_ready, r + 1)
                for b in range(BATCH):
                    nc.vector.tensor_scalar(x_in[:, b, :], x_in[:, b, :], mean_var[:, b, 0:1],
                                            rstd[:, b:b + 1], ALU.subtract, ALU.mult).then_inc(norm_ready, 1)

            latent_variances(0)
            for i in range(2):
                measure_row_tile(nc, rows, dve, i, i, 1)
            latent_norm(0)
            dve.wait_ge(norm_ready, BATCH)
            latent_variances(1)
            for i in range(2, ROW_TILES):
                measure_row_tile(nc, rows, dve, i, i, 1)
            latent_norm(1)
            dve.wait_ge(small_landed, 16 * 4)
            for b in range(BATCH):
                dve.wait_ge(tr_ready, b + 1)
                for t in range(KT):
                    out = nc.vector.tensor_scalar(lat_t[:, t, b * P:(b + 1) * P], ps[:, b, t * P:(t + 1) * P],
                                                  lat_g[:, t:t + 1], lat_b[:, t:t + 1], ALU.mult, ALU.add)
                out.then_inc(lat_ready, 1)
            for i in range(ROW_TILES):
                dve.wait_ge(rows["stats_ready"], i + 1)
                row_tile_variance(nc, rows, dve, i, i)
            for i in range(ROW_TILES):
                normalise_row_tile(nc, rows, dve, i, i)
            for m in range(PAIRS):
                dve.wait_ge(q_hi, m + 1)
                nc.vector.tensor_tensor(q_stage[:, m % 2, :, 1, :], by_batch(m), q_stage[:, m % 2, :, 0, :].bitcast(F32),
                                        ALU.subtract).then_inc(q_lo, 1)
                if m < ROW_TILES:
                    scale_row_tile(nc, rows, dve, m, m)
                if m == 5:
                    measure_row_tile(nc, rows, dve, ROW_TILES, 0, 2)

        @block.tensor
        def _(pe):
            pe.wait_ge(const_ready, 4)
            for b in range(BATCH):
                pe.wait_ge(norm_ready, BATCH + b + 1)
                for t in range(KT):
                    tr = nc.tensor.transpose(ps[:, b, t * P:(t + 1) * P], x_in[:, b, t * P:(t + 1) * P], keep["ident"][:])
                tr.then_inc(tr_ready, 1)
            pe.wait_ge(lat_ready, BATCH)
            pe.wait_ge(wq_landed, 16)
            for m in range(PAIRS):
                if m >= 7:
                    pe.wait_ge(q_lo, m - 6)
                for t in range(KT):
                    mm = nc.tensor.matmul(ps[:, q_bank(m), :], wq[:, t, m * P:(m + 1) * P], lat_t[:, t, :],
                                          start=(t == 0), stop=(t == KT - 1))
                mm.then_inc(q_ready, 1)
                if m < ROW_TILES:
                    transpose_row_tile(nc, rows, pe, m, m)


def attend(nc, d, keep, rows):
    with ExitStack() as ctx:
        def sb(name, shape, dt=F32):
            return ctx.enter_context(nc.sbuf_tensor(name, shape, dt))

        def psum(name, shape):
            return ctx.enter_context(nc.psum_tensor(name, shape, F32))

        def sem(name):
            return ctx.enter_context(nc.semaphore(name))

        wk_hi, wk_lo, wv_hi, wv_lo = (keep[n] for n in ("wk_hi", "wk_lo", "wv_hi", "wv_lo"))
        cos, sin, v = keep["cos"], keep["sin"], keep["v"]
        x_hi, x_lo = rows["x_hi"], rows["x_lo"]
        a_cos = sb("a_cos", [P, CHUNK])
        b_sin = sb("b_sin", [P, CHUNK])
        b_cos = sb("b_cos", [P, CHUNK])
        a_sin = sb("a_sin", [P, CHUNK])
        first_hi = sb("first_hi", [P, CHUNK], F32R)
        second_hi = sb("second_hi", [P, CHUNK], F32R)
        keys = sb("keys", [P, 2, 4, CHUNK], F32R)
        queries = sb("queries", [P, PAIRS, 2, 2, QUERIES], F32R)
        probs = sb("probs", [P, 2, 2, CHUNK])
        acc = sb("acc", [P, HEADS, DHEAD + 1])
        recip = sb("recip", [P, 2])
        attn = keep["attn"]

        ps_v = psum("ps_v", [P, 2, 512])
        ps_k = psum("ps_k", [P, 2, 512])
        ps_s = psum("ps_s", [P, ROW_TILES, 2, QUERIES])
        ps_o = psum("ps_o", [P, 512])

        v_ready = sem("v_ready")
        v_stored = sem("v_stored")
        k_ready = sem("k_ready")
        k_turned = sem("k_turned")
        rope_ready = sem("rope_ready")
        rope_hi = sem("rope_hi")
        rope_lo = sem("rope_lo")
        keys_landed = [sem(f"keys_landed{i}") for i in range(2)]
        q_landed = [sem(f"q_landed{i}") for i in range(PAIRS)]
        s_ready = sem("s_ready")
        s_copied = sem("s_copied")
        s_taken = sem("s_taken")
        clipped = sem("clipped")
        probs_ready = sem("probs_ready")
        o_ready = sem("o_ready")
        o_added = sem("o_added")
        recip_ready = sem("recip_ready")
        attn_ready = sem("attn_ready")
        attn_stored = sem("attn_stored")

        ROWS_OF_BATCH = CTX // P
        last_step = BATCH * BSTEPS

        def run(eng, step):
            for t in range(STEPS):
                step(0, t)
            with eng.Fori(0, BATCH - 1) as b:
                for t in range(STEPS, STEPS + BSTEPS):
                    step(b, t)
            for t in range(STEPS, BSTEPS + VALUE_LAG + 2):
                step(BATCH - 1, t)

        def exists(b, t):
            return not isinstance(b, int) or 0 <= BSTEPS * b + t < last_step

        def next_row_tile(b, t):
            if t % 2 == 0 and exists(b, t) and exists(b, t + STEPS):
                return b * ROWS_OF_BATCH + (t // 2 + ROW_TILES)
            return None

        block = ctx.enter_context(nc.Block())

        @block.sync
        def _(sp):
            def load_queries(whose, m):
                for side in range(2):
                    source = d["q_scratch"][m].rearrange("(j e) b c -> b e j c", j=2)[whose]
                    there = queries[DHEAD * side:DHEAD * (side + 1), m].rearrange("e j w n -> e j (w n)")
                    sp.dma_start(there.bitcast(F32), source).then_inc(q_landed[m], 16)

            for i in range(2):
                sp.wait_ge(keep["q_stored"][i], 16 * PAIRS // 2)
            load_queries(0, 0)
            load_queries(0, 1)

            def step(b, t):
                tile = next_row_tile(b, t)
                if tile is not None:
                    if not (isinstance(tile, int) and tile == ROW_TILES):
                        load_row_tile(nc, rows, sp, tile, t // 2 % ROW_TILES)
                if isinstance(b, int) and b == 0 and t + 2 < PAIRS:
                    load_queries(0, t + 2)
                if t % 2 == 0 and exists(b, t - 2):
                    group = b * (BSTEPS // 2) + (t // 2 - 1)
                    slot = (t // 2 - 1) % 2
                    parts = ((rope_hi, first_hi, 1), (rope_hi, second_hi, 2),
                             (rope_lo, a_cos, 1), (rope_lo, b_cos, 2))
                    for i, (made, part, n) in enumerate(parts):
                        wait(sp, made, 2 * group + n)
                        sp.dma_start(keys[HALF * i:HALF * (i + 1), slot].bitcast(F32),
                                     part[:].bitcast(F32)).then_inc(keys_landed[slot], 16)
                pair = t - SCORE_LAG - 1
                if STEPS * (CHUNKS - 1) <= pair % BSTEPS and pair >= 0 and exists(b, pair + STEPS):
                    m = pair % STEPS
                    whose = b + pair // BSTEPS
                    wait(sp, s_ready, b * (2 * BSTEPS) + 2 * (pair + 1))
                    load_queries(whose + 1, m)
                if isinstance(b, int) and b == BATCH - 1 and t == BSTEPS:
                    wait(sp, k_ready, BATCH * BSTEPS)
                    wait(sp, rope_ready, BATCH * BSTEPS)
                    sp.dma_start(keep["wo"], d["wo"].rearrange("(t p) n -> p t n", p=P)).then_inc(keep["wo_landed"], 16)
                    wait(sp, attn_stored, 16 * (BATCH - 1))
                    wait(sp, rows["lo_ready"], BATCH * ROWS_OF_BATCH)
                    for early in range(BATCH - 1):
                        sp.dma_start(keep["attn_early"][:, early, :], d["attn_scratch"][early]).then_inc(keep["attn_landed"], 16)
                pair = t - VALUE_LAG - 2
                if pair % BSTEPS == BSTEPS - 1 and exists(b, pair) and exists(b, pair + 1):
                    whose = b + pair // BSTEPS
                    wait(sp, attn_ready, PAIRS * whose + PAIRS)
                    sp.dma_start(d["attn_scratch"][whose], attn[:]).then_inc(attn_stored, 16)

            run(sp, step)
            sp.wait_ge(attn_stored, 16 * (BATCH - 1))

        @block.gpsimd
        def _(pool):
            def step(b, t):
                tile = next_row_tile(b, t)
                if tile is not None:
                    row_tile_power(nc, rows, pool, tile, t // 2 % ROW_TILES)
                tile = next_row_tile(b, t - 1)
                if tile is not None:
                    row_tile_low(nc, rows, pool, tile, (t // STEPS + 1) % 2, t // 2 % ROW_TILES)
                if t % 2 == 0 and exists(b, t - 2):
                    group = b * (BSTEPS // 2) + (t // 2 - 1)
                    for n, (full, hi) in enumerate(((a_cos, first_hi), (b_cos, second_hi))):
                        wait(pool, rope_hi, 2 * group + (n + 1))
                        nc.gpsimd.tensor_tensor(full[:].bitcast(F32R), full[:], hi[:].bitcast(F32),
                                                ALU.subtract).then_inc(rope_lo, 1)

            run(pool, step)

        @block.scalar
        def _(act):
            def copy_scores(b, pair, j):
                if exists(b, pair):
                    count = b * (2 * BSTEPS) + (2 * pair + j + 1)
                    if j == 0:
                        wait(act, o_ready, b * BSTEPS + (pair - 1))
                    wait(act, s_ready, count)
                    nc.scalar.activation(probs[:, pair % 2, j, :].rearrange("p (i n) -> p i n", n=P), ps_s[:, :, 1, :],
                                         ACT.Copy).then_inc(s_copied, 1)

            def step(b, t):
                copy_scores(b, t - VALUE_LAG, 1)
                pair = t - VALUE_LAG
                if exists(b, pair):
                    wait(act, clipped, b * (2 * BSTEPS) + 2 * (pair + 1))
                    nc.scalar.activation(probs[:, pair % 2], probs[:, pair % 2], ACT.Exp, scale=SCALE).then_inc(probs_ready, 1)
                if exists(b, t):
                    p = t % STEPS
                    wait(act, v_ready, b * BSTEPS + (t + 1))
                    wait(act, o_ready, b * BSTEPS + (t - p - STEPS + 4 * (p // 4 + 1)))
                    half = p // ROW_TILES
                    nc.scalar.activation(v[:, p % ROW_TILES, 8 * half:8 * half + 8, 0:DHEAD],
                                         ps_v[:, t % 2, :].rearrange("p (h e) -> p h e", e=DHEAD), ACT.Copy).then_inc(v_stored, 1)
                copy_scores(b, t - SCORE_LAG, 0)
                if t % 2 == 0 and exists(b, t - 2):
                    group = b * (BSTEPS // 2) + (t // 2 - 1)
                    for n, (full, hi) in enumerate(((a_cos, first_hi), (b_cos, second_hi))):
                        wait(act, rope_ready, 2 * group + (n + 1))
                        nc.scalar.activation(hi[:], full[:], ACT.Copy).then_inc(rope_hi, 1)
                if t % 2 == 1:
                    tile = next_row_tile(b, t - 1)
                    if tile is not None:
                        wait(act, k_ready, 2 * tile - 2 * (t // 2 % ROW_TILES) - STEPS)
                        row_tile_high(nc, rows, act, tile, (t // STEPS + 1) % 2, t // 2 % ROW_TILES)

            run(act, step)

        @block.vector
        def _(dve):
            def take_scores(b, pair, j):
                if exists(b, pair):
                    taken = b * (2 * BSTEPS) + (2 * pair + j + 1)
                    mine = probs[:, pair % 2, j, :]
                    wait(dve, s_copied, taken)
                    tiles = mine.rearrange("p (i n) -> p i n", n=P)
                    nc.vector.tensor_tensor(tiles, ps_s[:, :, 0, :], tiles, ALU.add).then_inc(s_taken, 1)
                    wait(dve, s_taken, taken)
                    nc.vector.tensor_scalar(mine, mine, CLIP / SCALE, -CLIP / SCALE, ALU.min, ALU.max).then_inc(clipped, 1)

            def step(b, t):
                tile = next_row_tile(b, t)
                if tile is not None:
                    wait(dve, rows["stats_ready"], tile + 1)
                take_scores(b, t - VALUE_LAG, 1)
                if tile is not None:
                    row_tile_variance(nc, rows, dve, tile, t // 2 % ROW_TILES)
                pair = t - VALUE_LAG - 1
                if exists(b, pair):
                    n = b * BSTEPS + pair
                    m = pair % STEPS
                    mine = acc[:, 2 * m:2 * m + 2, :]
                    got = ps_o[:, 0:2 * (DHEAD + 1)].rearrange("p (h e) -> p h e", h=2)
                    chunk = pair // STEPS % CHUNKS
                    wait(dve, o_ready, n + 1)
                    whose = b + pair // BSTEPS
                    if chunk == 0 and m == 0:
                        wait(dve, attn_ready, PAIRS * whose)
                    if chunk == 0 and m == 2:
                        wait(dve, attn_stored, 16 * whose)
                    if chunk == 0:
                        nc.vector.tensor_copy(mine, got).then_inc(o_added, 1)
                    else:
                        wait(dve, o_added, n - (STEPS - 1))
                        nc.vector.tensor_tensor(mine, got, mine, ALU.add).then_inc(o_added, 1)
                    if chunk == CHUNKS - 1:
                        wait(dve, o_added, n + 1)
                        if m >= 1:
                            wait(dve, attn_ready, PAIRS * whose + m)
                        nc.vector.reciprocal(recip[:], acc[:, 2 * m:2 * m + 2, DHEAD]).then_inc(recip_ready, 1)
                        wait(dve, recip_ready, PAIRS * whose + (m + 1))
                        for j in range(2):
                            h = 2 * m + j
                            out = nc.vector.tensor_scalar(attn[:, h * DHEAD:(h + 1) * DHEAD], acc[:, h, 0:DHEAD],
                                                          recip[:, j:j + 1], None, ALU.mult)
                        out.then_inc(attn_ready, 1)
                if exists(b, t - 1):
                    n = b * BSTEPS + (t - 1)
                    group = b * (BSTEPS // 2) + (t - 1) // 2
                    angles = slice((t - 1) // STEPS % CHUNKS * CHUNK, (t - 1) // STEPS % CHUNKS * CHUNK + CHUNK)
                    wait(dve, k_ready, n + 1)
                    if t % 2 == 1:
                        slot = ((t - 1) // 2 - 1) % 2
                        turns = b * (BSTEPS // 4) + ((t - 1) // 2 - 1) // 2 + 1
                        wait(dve, keys_landed[slot], 64 * turns)
                        nc.vector.tensor_tensor(a_cos[:], ps_k[:, 0, :], cos[:, angles], ALU.mult)
                        nc.vector.tensor_tensor(a_sin[:], ps_k[:, 0, :], sin[:, angles], ALU.mult).then_inc(k_turned, 1)
                    else:
                        nc.vector.tensor_tensor(b_sin[:], ps_k[:, 1, :], sin[:, angles], ALU.mult)
                        nc.vector.tensor_tensor(b_cos[:], ps_k[:, 1, :], cos[:, angles], ALU.mult).then_inc(k_turned, 1)
                        wait(dve, k_turned, n + 1)
                        nc.vector.tensor_tensor(a_cos[:], a_cos[:], b_sin[:], ALU.subtract).then_inc(rope_ready, 1)
                        nc.vector.tensor_tensor(b_cos[:], b_cos[:], a_sin[:], ALU.add).then_inc(rope_ready, 1)
                take_scores(b, t - SCORE_LAG, 0)
                tile = next_row_tile(b, t)
                if tile is not None:
                    normalise_row_tile(nc, rows, dve, tile, t // 2 % ROW_TILES)
                tile = next_row_tile(b, t - 1)
                if tile is not None:
                    scale_row_tile(nc, rows, dve, tile, t // 2 % ROW_TILES)
                tile = next_row_tile(b, t + 1)
                if tile is not None:
                    i = (t + 1) // 2
                    measure_row_tile(nc, rows, dve, tile, i % ROW_TILES, b * CHUNKS + (i // ROW_TILES + 2))

            run(dve, step)

        @block.tensor
        def _(pe):
            def product(out, left, right, first, last):
                nc.tensor.matmul(out, left[0], right[0], start=first, stop=False)
                nc.tensor.matmul(out, left[0], right[1], start=False, stop=False)
                return nc.tensor.matmul(out, left[1], right[0], start=False, stop=last)

            def score(b, pair, j):
                if exists(b, pair):
                    m = pair % STEPS
                    slot = pair // 2 % 2
                    if j == 0:
                        wait(pe, keys_landed[slot], 64 * (b * (BSTEPS // 4) + pair // 4 + 1))
                        wait(pe, q_landed[m], 32 * (b + (pair // BSTEPS + 1)))
                    wait(pe, s_taken, b * (2 * BSTEPS) + (2 * pair + j))
                    for i in range(ROW_TILES):
                        mm = nc.tensor.matmul(ps_s[:, i], keys[:, slot, 2 * (pair % 2) + j, i * P:(i + 1) * P],
                                              queries[:, m, j], start=True, stop=True)
                    mm.then_inc(s_ready, 1)

            def step(b, t):
                p = t % STEPS
                buf = t // STEPS % 2
                if exists(b, t):
                    n = b * BSTEPS + t
                    if p == 0:
                        wait(pe, rows["lo_ready"], b * ROWS_OF_BATCH + (t // 2 + ROW_TILES))
                    wait(pe, v_stored, n - 1)
                    for k in range(KT):
                        cols = slice(p % ROW_TILES * P, (p % ROW_TILES + 1) * P)
                        heads = slice(p // ROW_TILES * 512, (p // ROW_TILES + 1) * 512)
                        mm = product(ps_v[:, t % 2, :], (x_hi[:, buf, k, cols], x_lo[:, buf, k, cols]),
                                     (wv_hi[:, k, heads], wv_lo[:, k, heads]), k == 0, k == KT - 1)
                    mm.then_inc(v_ready, 1)
                score(b, t - SCORE_LAG, 0)
                if exists(b, t):
                    n = b * BSTEPS + t
                    wait(pe, k_turned, n - 1)
                    for k in range(KT):
                        cols = slice(p * P, (p + 1) * P)
                        mm = product(ps_k[:, t % 2, :], (wk_hi[:, k, cols], wk_lo[:, k, cols]),
                                     (x_hi[:, buf, k, :], x_lo[:, buf, k, :]), k == 0, k == KT - 1)
                    mm.then_inc(k_ready, 1)
                score(b, t - SCORE_LAG, 1)
                pair = t - VALUE_LAG
                if exists(b, pair):
                    n = b * BSTEPS + pair
                    m = pair % STEPS
                    wait(pe, probs_ready, n + 1)
                    wait(pe, o_added, n)
                    wait(pe, v_stored, b * BSTEPS + (pair - m + 4 * (m // 4 + 1)))
                    for j in range(2):
                        for i in range(ROW_TILES):
                            mm = nc.tensor.matmul(ps_o[:, j * (DHEAD + 1):(j + 1) * (DHEAD + 1)],
                                                  probs[:, pair % 2, j, i * P:(i + 1) * P], v[:, i, 2 * m + j, :],
                                                  start=(i == 0), stop=(i == ROW_TILES - 1))
                    mm.then_inc(o_ready, 1)
                tile = next_row_tile(b, t)
                if tile is not None:
                    transpose_row_tile(nc, rows, pe, tile, t // 2 % ROW_TILES)

            run(pe, step)


def mix(nc, d, keep):
    with ExitStack() as ctx:
        def sb(name, shape, dt=F32):
            return ctx.enter_context(nc.sbuf_tensor(name, shape, dt))

        def sem(name):
            return ctx.enter_context(nc.semaphore(name))

        x3, xt_hi, xt_lo = (keep[n] for n in ("x3", "xt_hi", "xt_lo"))
        ident, wo, routed = keep["ident"], keep["wo"], keep["routed"]
        attn = [keep["attn"][:]] + [keep["attn_early"][:, b, :] for b in range(BATCH - 1)]
        batch_of = [BATCH - 1] + list(range(BATCH - 1))
        attn_t = sb("attn_t", [P, INNER // P, TOKENS])
        x_res = sb("x_res", [P, BATCH, DIM])
        qkv_w = sb("qkv_w", [P, KT, 3 * DIM])
        qkv_b = sb("qkv_b", [P, 3 * DIM])
        proj_w = sb("proj_w", [P, KT, DIM])
        router_w = sb("router_w", [P, KT, EXPERTS])
        x_norm = sb("x_norm", [P, BATCH, DIM])
        x_t = sb("x_t", [P, KT, TOKENS])
        qkv = sb("qkv", [P, BATCH, 3 * DIM])
        stats = sb("c_stats", [P, BATCH, 6])
        mean_var = sb("c_mean_var", [P, BATCH, 2])
        var_eps = sb("c_var_eps", [P, BATCH])
        rstd = sb("c_rstd", [P, BATCH])
        sums = sb("sums", [P, BATCH, 2 * LHEADS])
        norms = sb("norms", [P, BATCH, 2 * LHEADS])
        half = sb("half", [P, BATCH, 2 * LHEADS])
        block_mask = sb("block_mask", [P, P])
        peak = sb("peak", [P, BATCH])
        squares = [keep["attn_early"][:, b, :] for b in range(BATCH - 1)] + [keep["attn"][:]]
        bo, proj_b = (sb(n, [P, DIM])[:] for n in ("bo", "proj_b"))
        out_t = keep["attn_early"][:, 0:2, :].rearrange("p b (t n) -> p (b t) n", n=TOKENS)
        kv = attn_t[:, 0:KT, :]
        q_t = attn_t[:, KT:2 * KT, :]
        ps = ctx.enter_context(nc.psum_tensor("c_ps", [P, 8, 512], F32))

        x_landed = sem("c_x_landed")
        small_landed = sem("c_small_landed")
        qkv_landed = sem("c_qkv_landed")
        proj_landed = sem("c_proj_landed")
        const_ready = sem("c_const_ready")
        attn_turned = sem("c_attn_turned")
        attn_t_ready = [sem(f"c_attn_t_ready{i}") for i in range(2)]
        wo_done = sem("c_wo_done")
        dve_step = sem("c_dve_step")
        var_ready = sem("c_var_ready")
        rstd_ready = sem("c_rstd_ready")
        norm_ready = sem("c_norm_ready")
        x_turned = sem("c_x_turned")
        x_t_ready = sem("c_x_t_ready")
        qkv_done = sem("c_qkv_done")
        qkv_ready = sem("c_qkv_ready")
        squares_ready = sem("c_squares_ready")
        sums_ready = sem("c_sums_ready")
        roots_ready = sem("c_roots_ready")
        unit_ready = sem("c_unit_ready")
        kv_done = sem("c_kv_done")
        kv_ready = sem("c_kv_ready")
        q_turned = sem("c_q_turned")
        q_t_ready = sem("c_q_t_ready")
        out_done = sem("c_out_done")
        out_t_ready = sem("c_out_t_ready")
        proj_done = sem("c_proj_done")
        hi_ready = sem("c_hi_ready")
        lo_ready = sem("c_lo_ready")
        logits_done = sem("c_logits_done")
        shifted_ready = sem("c_shifted_ready")

        def rows_of(name, width):
            return bass.AP(d[name].tensor, 0, [[0, P], [1, width]])

        def tiles(name):
            return d[name].rearrange("(t p) n -> p t n", p=P)

        def qkv_bank(i, j):
            return (3 * i + j) % 8

        block = ctx.enter_context(nc.Block())

        @block.sync
        def _(sp):
            sp.dma_start(x_res[:], d["x"].rearrange("b n d -> n b d")).then_inc(x_landed, 16)
            sp.dma_start(bo, rows_of("bo", DIM)).then_inc(small_landed, 16)
            sp.dma_start(qkv_b[:], rows_of("qkv_b", 3 * DIM)).then_inc(small_landed, 16)
            sp.dma_start(proj_b, rows_of("proj_b", DIM)).then_inc(small_landed, 16)
            sp.dma_start(router_w[:], tiles("router_w")).then_inc(small_landed, 16)
            sp.dma_start(qkv_w[:], tiles("qkv_w")).then_inc(qkv_landed, 16)
            sp.dma_start(proj_w[:], tiles("proj_w")).then_inc(proj_landed, 16)
            for w in (GATE, UP, DOWN):
                sp.dma_start(keep["raw"][w][:], d[WEIGHTS[w]][0].rearrange("(t p) n -> p t n", p=P)).then_inc(keep["raw_landed"][w], 16)

        @block.gpsimd
        def _(pool):
            nc.gpsimd.memset(block_mask[:], 0.0).then_inc(const_ready, 1)
            nc.gpsimd.memset(half[:], 0.5).then_inc(const_ready, 1)
            for e in range(EXPERTS):
                number = nc.gpsimd.memset(keep["numbers"][:, e:e + 1], float(e))
            number.then_inc(const_ready, 1)
            pool.wait_ge(const_ready, 3)
            for g in range(GROUP):
                nc.gpsimd.memset(block_mask[g * LD:(g + 1) * LD, g * LD:(g + 1) * LD], 1.0).then_inc(const_ready, 1)
                pool.wait_ge(const_ready, 3 + g + 1)

            def powers(n, b):
                pool.wait_ge(var_ready, n + 1)
                nc.gpsimd.tensor_tensor(rstd[:, b:b + 1], var_eps[:, b:b + 1], keep["minus_half"][:, 0:1],
                                        ALU.pow).then_inc(rstd_ready, 1)

            for i, b in enumerate(batch_of):
                powers(i, b)
            for i, b in enumerate(batch_of):
                pool.wait_ge(sums_ready, i + 1)
                nc.gpsimd.tensor_tensor(norms[:, b, :], sums[:, b, :], half[:, b, :], ALU.pow).then_inc(roots_ready, 1)
            for b in range(BATCH):
                powers(BATCH + b, b)

        @block.scalar
        def _(act):
            def turned(out, bank, done):
                nc.scalar.activation(out, ps[:, bank, :].rearrange("p (t n) -> p t n", n=P), ACT.Copy).then_inc(done, 1)

            def split_high(w):
                act.wait_ge(keep["raw_landed"][w], 16)
                nc.scalar.activation(keep["gate_hi"], keep["raw"][w][:], ACT.Copy).then_inc(keep["raw_hi"][w], 1)

            for i, b in enumerate(batch_of):
                act.wait_ge(attn_turned, 2 * i + 2)
                turned(attn_t[:, KT:2 * KT, b * P:(b + 1) * P], 2 * i + 1, attn_t_ready[1])
            for i, b in enumerate(batch_of):
                act.wait_ge(x_turned, i + 1)
                turned(x_t[:, :, b * P:(b + 1) * P], 4 + b, x_t_ready)
            split_high(GATE)
            for i, b in enumerate(batch_of):
                act.wait_ge(qkv_ready, 3 * i + 2)
                nc.scalar.activation(squares[b], qkv[:, b, 0:2 * DIM], ACT.Square).then_inc(squares_ready, 1)
            for i, b in enumerate(batch_of):
                act.wait_ge(q_turned, i + 1)
                turned(q_t[:, :, b * P:(b + 1) * P], 4 + b, q_t_ready)
            for i, b in enumerate(batch_of):
                act.wait_ge(out_done, i + 1)
                turned(out_t[:, :, b * P:(b + 1) * P], b, out_t_ready)
            for b in range(BATCH):
                act.wait_ge(x_turned, BATCH + b + 1)
                cols = slice(b * P, (b + 1) * P)
                turned(x_t[:, :, cols], b, x_t_ready)
                turned(xt_hi[:, :, cols], b, hi_ready)

        @block.vector
        def _(dve):
            chain = [0]

            def link(ins):
                chain[0] += 1
                ins.then_inc(dve_step, 1)
                dve.wait_ge(dve_step, chain[0])

            def variance(source, b):
                link(nc.vector.bn_stats(stats[:, b, :], source[:, b, :]))
                link(nc.vector.bn_aggr(mean_var[:, b, :], stats[:, b, :]))
                nc.vector.tensor_scalar(var_eps[:, b:b + 1], mean_var[:, b, 1:2], EPS, None, ALU.add).then_inc(var_ready, 1)

            def normalise(source, n, b):
                dve.wait_ge(rstd_ready, n + 1)
                nc.vector.tensor_scalar(x_norm[:, b, :], source[:, b, :], mean_var[:, b, 0:1],
                                        rstd[:, b:b + 1], ALU.subtract, ALU.mult).then_inc(norm_ready, 1)

            def split_low(w):
                dve.wait_ge(keep["raw_hi"][w], 1)
                nc.vector.tensor_tensor(keep["gate_lo"], keep["raw"][w][:], keep["gate_hi"].bitcast(F32),
                                        ALU.subtract).then_inc(keep["raw_lo"][w], 1)

            for i, b in enumerate(batch_of):
                dve.wait_ge(attn_turned, 2 * i + 1)
                nc.vector.tensor_copy(attn_t[:, 0:KT, b * P:(b + 1) * P],
                                      ps[:, 2 * i, :].rearrange("p (t n) -> p t n", n=P)).then_inc(attn_t_ready[0], 1)
            dve.wait_ge(x_landed, 16)
            dve.wait_ge(small_landed, 16 * 4)
            for b in range(BATCH):
                add = nc.vector.tensor_tensor(x_res[:, b, :], x_res[:, b, :], bo, ALU.add)
            link(add)
            for i, b in enumerate(batch_of):
                dve.wait_ge(wo_done, i + 1)
                link(nc.vector.tensor_tensor(x_res[:, b, :], ps[:, b, :], x_res[:, b, :], ALU.add))
                variance(x_res, b)
                if i >= 1:
                    normalise(x_res, i - 1, batch_of[i - 1])
            normalise(x_res, BATCH - 1, batch_of[-1])

            def unit(i):
                b = batch_of[i]
                dve.wait_ge(roots_ready, i + 1)
                link(nc.vector.tensor_scalar(norms[:, b, :], norms[:, b, :], NORM_EPS, None, ALU.max))
                link(nc.vector.reciprocal(norms[:, b, :], norms[:, b, :]))
                heads = qkv[:, b, 0:2 * DIM].rearrange("p (h e) -> p h e", e=LD)
                scale = norms[:, b, :].unsqueeze(2).to_broadcast([P, 2 * LHEADS, LD])
                nc.vector.tensor_tensor(heads, heads, scale, ALU.mult).then_inc(unit_ready, 1)

            for i, b in enumerate(batch_of):
                for j in range(3):
                    dve.wait_ge(qkv_done, 3 * i + j + 1)
                    nc.vector.tensor_tensor(qkv[:, b, j * DIM:(j + 1) * DIM], ps[:, qkv_bank(i, j), :],
                                            qkv_b[:, j * DIM:(j + 1) * DIM], ALU.add).then_inc(qkv_ready, 1)
                if i == 2:
                    split_low(GATE)
                if i >= 1:
                    unit(i - 1)
                dve.wait_ge(squares_ready, i + 1)
                nc.vector.tensor_reduce(sums[:, b, :], squares[b].rearrange("p (h e) -> p h e", e=LD), AX_X,
                                        ALU.add).then_inc(sums_ready, 1)
            unit(BATCH - 1)
            dve.wait_ge(const_ready, 3 + GROUP)
            for i, b in enumerate(batch_of):
                dve.wait_ge(kv_done, i + 1)
                nc.vector.tensor_tensor(kv[:, :, b * P:(b + 1) * P], ps[:, b, :].rearrange("p (t n) -> p t n", n=P),
                                        block_mask[:].unsqueeze(1).to_broadcast([P, KT, P]), ALU.mult).then_inc(kv_ready, 1)
            for b in range(BATCH):
                add = nc.vector.tensor_tensor(x_res[:, b, :], x_res[:, b, :], proj_b, ALU.add)
            link(add)
            for b in range(BATCH):
                dve.wait_ge(proj_done, b + 1)
                link(nc.vector.tensor_tensor(x3[:, b, :], ps[:, 4 + b, :], x_res[:, b, :], ALU.add))
                variance(x3, b)
                if b >= 1:
                    normalise(x3, BATCH + b - 1, b - 1)
            normalise(x3, 2 * BATCH - 1, BATCH - 1)
            for b in range(BATCH):
                cols = slice(b * P, (b + 1) * P)
                dve.wait_ge(hi_ready, b + 1)
                nc.vector.tensor_tensor(xt_lo[:, :, cols], x_t[:, :, cols], xt_hi[:, :, cols].bitcast(F32),
                                        ALU.subtract).then_inc(lo_ready, 1)
            dve.wait_ge(logits_done, 1)
            logits = ps[:, 4, 0:BATCH * EXPERTS].rearrange("p (b e) -> p b e", b=BATCH)
            link(nc.vector.tensor_reduce(peak[:], logits, AX_X, ALU.max))
            for b in range(BATCH):
                nc.vector.tensor_scalar(routed[:, b, :], logits[:, b, :], peak[:, b:b + 1], None, ALU.subtract)

        @block.tensor
        def _(pe):
            def turn(out_bank, source, done):
                for t in range(KT):
                    tr = nc.tensor.transpose(ps[:, out_bank, t * P:(t + 1) * P], source[:, t * P:(t + 1) * P], ident[:])
                tr.then_inc(done, 1)

            for i in range(BATCH):
                if i == 1:
                    pe.wait_ge(keep["attn_landed"], 16 * (BATCH - 1))
                turn(2 * i, attn[i][:, 0:DIM], attn_turned)
                turn(2 * i + 1, attn[i][:, DIM:2 * DIM], attn_turned)
            pe.wait_ge(keep["wo_landed"], 16)
            for i, b in enumerate(batch_of):
                pe.wait_ge(attn_t_ready[0], max(i, b // 2) + 1)
                pe.wait_ge(attn_t_ready[1], max(i, b // 2) + 1)
                for t in range(INNER // P):
                    mm = nc.tensor.matmul(ps[:, b, :], attn_t[:, t, b * P:(b + 1) * P], wo[:, t, :],
                                          start=(t == 0), stop=(t == INNER // P - 1))
                mm.then_inc(wo_done, 1)
            for i, b in enumerate(batch_of):
                pe.wait_ge(norm_ready, i + 1)
                turn(4 + b, x_norm[:, b, :], x_turned)
            pe.wait_ge(qkv_landed, 16)
            for i, b in enumerate(batch_of):
                pe.wait_ge(x_t_ready, 1 if i == 0 else BATCH)
                for j in range(3):
                    if 3 * i + j >= 8:
                        pe.wait_ge(qkv_ready, 3 * i + j - 7)
                    for t in range(KT):
                        mm = nc.tensor.matmul(ps[:, qkv_bank(i, j), :], x_t[:, t, b * P:(b + 1) * P],
                                              qkv_w[:, t, j * DIM:(j + 1) * DIM], start=(t == 0), stop=(t == KT - 1))
                    mm.then_inc(qkv_done, 1)
            pe.wait_ge(qkv_ready, 3 * BATCH)
            for i, b in enumerate(batch_of):
                pe.wait_ge(unit_ready, i + 1)
                turn(4 + b, qkv[:, b, 0:DIM], q_turned)
                for g in range(KT):
                    k = qkv[:, b, DIM + g * P:DIM + (g + 1) * P]
                    v = qkv[:, b, 2 * DIM + g * P:2 * DIM + (g + 1) * P]
                    mm = nc.tensor.matmul(ps[:, b, g * P:(g + 1) * P], k, v, start=True, stop=True)
                mm.then_inc(kv_done, 1)
            for i, b in enumerate(batch_of):
                pe.wait_ge(kv_ready, i + 1)
                pe.wait_ge(q_t_ready, i + 1)
                for g in range(KT):
                    mm = nc.tensor.matmul(ps[:, b, g * P:(g + 1) * P], kv[:, g, b * P:(b + 1) * P],
                                          q_t[:, g, b * P:(b + 1) * P], start=True, stop=True)
                mm.then_inc(out_done, 1)
            pe.wait_ge(proj_landed, 16)
            for b in range(BATCH):
                pe.wait_ge(out_t_ready, b + 2 if b < BATCH - 1 else BATCH)
                for t in range(KT):
                    mm = nc.tensor.matmul(ps[:, 4 + b, :], out_t[:, t, b * P:(b + 1) * P], proj_w[:, t, :],
                                          start=(t == 0), stop=(t == KT - 1))
                mm.then_inc(proj_done, 1)
            for b in range(BATCH):
                pe.wait_ge(norm_ready, BATCH + b + 1)
                turn(b, x_norm[:, b, :], x_turned)
            for b in range(BATCH):
                pe.wait_ge(x_t_ready, BATCH + b + 1)
                for t in range(KT):
                    mm = nc.tensor.matmul(ps[:, 4, b * EXPERTS:(b + 1) * EXPERTS], x_t[:, t, b * P:(b + 1) * P],
                                          router_w[:, t, :], start=(t == 0), stop=(t == KT - 1))
            mm.then_inc(logits_done, 1)


def experts(nc, d, keep):
    with ExitStack() as ctx:
        def sb(name, shape, dt=F32):
            return ctx.enter_context(nc.sbuf_tensor(name, shape, dt))

        def sem(name):
            return ctx.enter_context(nc.semaphore(name))

        x3, xt_hi, xt_lo, routed = (keep[n] for n in ("x3", "xt_hi", "xt_lo", "routed"))
        raw = keep["raw"]
        w_hi = [keep["gate_hi"]] + [sb(f"{n}_hi", [P, KT, DIM], F32R)[:] for n in ("up", "down")]
        w_lo = [keep["gate_lo"]] + [sb(f"{n}_lo", [P, KT, DIM], F32R)[:] for n in ("up", "down")]
        silu = sb("silu", [P, 2, TOKENS])
        hidden = sb("hidden", [P, 2, TOKENS])
        h_hi = sb("h_hi", [P, KT, TOKENS], F32R)
        h_lo = sb("h_lo", [P, KT, TOKENS], F32R)
        y = sb("y", [P, BATCH, DIM])
        total = sb("total", [P, BATCH])
        top = sb("top", [P, BATCH, 8])
        top_at = sb("top_at", [P, BATCH, 8], U32)
        top_atf = sb("top_atf", [P, BATCH, 8])
        share = sb("share", [P, 2, BATCH, EXPERTS])
        weight = sb("weight", [P, BATCH])
        ps_gate = ctx.enter_context(nc.psum_tensor("ps_gate", [P, 2, 512], F32))
        ps_up = ctx.enter_context(nc.psum_tensor("ps_up", [P, 2, 512], F32))
        ps_y = ctx.enter_context(nc.psum_tensor("ps_y", [P, BATCH, 512], F32))

        raw_landed, raw_hi, raw_lo = keep["raw_landed"], keep["raw_hi"], keep["raw_lo"]
        gate_up_done = sem("gate_up_done")
        silu_ready = sem("silu_ready")
        hidden_ready = sem("hidden_ready")
        h_hi_ready = sem("h_hi_ready")
        h_lo_ready = sem("h_lo_ready")
        down_done = sem("down_done")
        exp_ready = sem("exp_ready")
        router_step = sem("router_step")
        weight_ready = sem("weight_ready")
        y_added = sem("y_added")
        y_stored = sem("y_stored")

        def run(eng, expert):
            expert(0, first=True, last=False)
            with eng.Fori(1, ALL_EXPERTS - 1) as e:
                expert(e, first=False, last=False)
            expert(ALL_EXPERTS - 1, first=False, last=True)

        block = ctx.enter_context(nc.Block())

        @block.sync
        def _(sp):
            def expert(e, first, last):
                if not first:
                    for w in (GATE, UP, DOWN):
                        wait(sp, raw_lo[w], e)
                        sp.dma_start(raw[w][:], d[WEIGHTS[w]][e].rearrange("(t p) n -> p t n", p=P)).then_inc(raw_landed[w], 16)

            run(sp, expert)
            for b in range(BATCH):
                sp.wait_ge(y_added, BATCH * (ALL_EXPERTS - 1) + b + 1)
                sp.dma_start(d["out"][b], y[:, b, :]).then_inc(y_stored, 16)
            sp.wait_ge(y_stored, 16 * BATCH)

        @block.scalar
        def _(act):
            def split_high(w, e):
                wait(act, raw_landed[w], 16 * (e + 1))
                if w == DOWN:
                    wait(act, down_done, BATCH * e)
                else:
                    wait(act, gate_up_done, KT * e)
                nc.scalar.activation(w_hi[w], raw[w][:], ACT.Copy).then_inc(raw_hi[w], 1)

            split_high(UP, 0)
            nc.scalar.activation(routed[:], routed[:], ACT.Exp).then_inc(exp_ready, 1)

            def expert(e, first, last):
                split_high(DOWN, e)
                for f in range(KT):
                    n = e * KT + f
                    wait(act, gate_up_done, n + 1)
                    wait(act, hidden_ready, n - 1)
                    nc.scalar.activation(silu[:, f % 2, :], ps_gate[:, f % 2, :], ACT.Silu).then_inc(silu_ready, 1)
                    wait(act, hidden_ready, n + 1)
                    nc.scalar.activation(h_hi[:, f, :], hidden[:, f % 2, :], ACT.Copy).then_inc(h_hi_ready, 1)
                if not last:
                    split_high(GATE, e + 1)
                    split_high(UP, e + 1)

            run(act, expert)

        @block.vector
        def _(dve):
            chain = [0]

            def link(ins):
                chain[0] += 1
                ins.then_inc(router_step, 1)
                dve.wait_ge(router_step, chain[0])

            def split_low(w, e):
                wait(dve, raw_hi[w], e + 1)
                nc.vector.tensor_tensor(w_lo[w], raw[w][:], w_hi[w].bitcast(F32), ALU.subtract).then_inc(raw_lo[w], 1)

            def router_probabilities():
                dve.wait_ge(exp_ready, 1)
                link(nc.vector.tensor_reduce(total[:], routed[:], AX_X, ALU.add))
                link(nc.vector.reciprocal(total[:], total[:]))
                for b in range(BATCH):
                    prob = nc.vector.tensor_scalar(routed[:, b, :], routed[:, b, :], total[:, b:b + 1], None, ALU.mult)
                link(prob)

            def router_best():
                for b in range(BATCH):
                    best = nc.vector.max(top[:, b, :], routed[:, b, :])
                link(best)
                for b in range(BATCH):
                    where = nc.vector.max_index(top_at[:, b, :], top[:, b, :], routed[:, b, :])
                link(where)
                nc.vector.tensor_copy(top_atf[:], top_at[:])
                link(nc.vector.tensor_tensor(total[:], top[:, :, 0], top[:, :, 1], ALU.add))
                link(nc.vector.tensor_scalar(total[:], total[:], 1e-9, None, ALU.add))
                link(nc.vector.reciprocal(total[:], total[:]))

            def router_shares():
                for b in range(BATCH):
                    scaled = nc.vector.tensor_scalar(top[:, b, 0:2], top[:, b, 0:2], total[:, b:b + 1], None, ALU.mult)
                link(scaled)
                for k in range(2):
                    for b in range(BATCH):
                        part = nc.vector.tensor_scalar(share[:, k, b, :], keep["numbers"][:], top_atf[:, b, k:k + 1],
                                                       top[:, b, k:k + 1], ALU.is_equal, ALU.mult)
                link(part)
                link(nc.vector.tensor_tensor(share[:, 0], share[:, 0], share[:, 1], ALU.add))

            split_low(UP, 0)
            router = (router_probabilities, router_best, router_shares)

            def expert(e, first, last):
                split_low(DOWN, e)
                for f in range(KT):
                    n = e * KT + f
                    wait(dve, silu_ready, n + 1)
                    wait(dve, h_lo_ready, n - 1)
                    nc.vector.tensor_tensor(hidden[:, f % 2, :], ps_up[:, f % 2, :], silu[:, f % 2, :], ALU.mult).then_inc(hidden_ready, 1)
                    wait(dve, h_hi_ready, n + 1)
                    nc.vector.tensor_tensor(h_lo[:, f, :], hidden[:, f % 2, :], h_hi[:, f, :].bitcast(F32), ALU.subtract).then_inc(h_lo_ready, 1)
                    if first and f < len(router):
                        router[f]()
                if not last:
                    split_low(GATE, e + 1)
                    split_low(UP, e + 1)
                if not first:
                    wait(dve, y_added, BATCH * e)
                    nc.vector.tensor_copy(weight[:], share[:, 0, :, e - 1]).then_inc(weight_ready, 1)
                    wait(dve, weight_ready, e)
                for b in range(BATCH):
                    wait(dve, down_done, BATCH * e + (b + 1))
                    if first:
                        add = nc.vector.tensor_tensor(y[:, b, :], ps_y[:, b, :], x3[:, b, :], ALU.add)
                    else:
                        add = nc.vector.scalar_tensor_tensor(y[:, b, :], ps_y[:, b, :], weight[:, b:b + 1], y[:, b, :],
                                                             ALU.mult, ALU.add)
                    add.then_inc(y_added, 1)

            run(dve, expert)

        @block.tensor
        def _(pe):
            def product(out, left, right, first, last):
                nc.tensor.matmul(out, left[0], right[0], start=first, stop=False)
                nc.tensor.matmul(out, left[0], right[1], start=False, stop=False)
                return nc.tensor.matmul(out, left[1], right[0], start=False, stop=last)

            def expert(e, first, last):
                for f in range(KT):
                    wait(pe, hidden_ready, e * KT + (f - 1))
                    for out, w in ((ps_gate, GATE), (ps_up, UP)):
                        if f == 0:
                            wait(pe, raw_lo[w], e + 1)
                        for t in range(KT):
                            cols = slice(f * P, (f + 1) * P)
                            mm = product(out[:, f % 2, :], (w_hi[w][:, t, cols], w_lo[w][:, t, cols]),
                                         (xt_hi[:, t, :], xt_lo[:, t, :]), t == 0, t == KT - 1)
                    mm.then_inc(gate_up_done, 1)
                wait(pe, raw_lo[DOWN], e + 1)
                for t in range(KT):
                    wait(pe, h_lo_ready, e * KT + (t + 1))
                    if t == 0:
                        wait(pe, y_added, BATCH * e)
                    for b in range(BATCH):
                        cols = slice(b * P, (b + 1) * P)
                        mm = product(ps_y[:, b, :], (h_hi[:, t, cols], h_lo[:, t, cols]),
                                     (w_hi[DOWN][:, t, :], w_lo[DOWN][:, t, :]), t == 0, t == KT - 1)
                        if t == KT - 1:
                            mm.then_inc(down_done, 1)

            run(pe, expert)


def program(nc, d):
    d["q_scratch"] = nc.dram_tensor("q_scratch", (PAIRS, P, BATCH, 2 * QUERIES), F32).ap()
    d["attn_scratch"] = nc.dram_tensor("attn_scratch", (BATCH, P, INNER), F32).ap()
    with ExitStack() as ctx:
        def sb(name, shape, dt=F32):
            return ctx.enter_context(nc.sbuf_tensor(name, shape, dt))

        def sem(name):
            return ctx.enter_context(nc.semaphore(name))

        keep = {"ident": sb("ident", [P, P]), "minus_half": sb("minus_half", [P, 8])}
        keep["x_hi"] = sb("x_hi", [P, 2, KT, CHUNK], F32R)
        room = sb("row_room", [P, BATCH - 1, INNER])
        keep["row_in"] = room[:, 0:2, :].rearrange("p a (t n) -> p (a t) n", n=DIM)
        keep["x_full"] = room[:, 2, :].rearrange("p (a t n) -> p a t n", a=2, n=P)
        keep["attn_early"] = room
        angles = sb("angles", [P, 2, CTX])
        keep["cos"], keep["sin"] = angles[:, 0], angles[:, 1]
        keep["wo"] = angles[:].rearrange("p a (t n) -> p (a t) n", n=DIM)
        keep["attn"] = sb("attn", [P, INNER])
        keep["wo_landed"] = sem("wo_landed")
        keep["attn_landed"] = sem("attn_landed")
        with ExitStack() as inner:
            def sbi(name, shape, dt=F32):
                return inner.enter_context(nc.sbuf_tensor(name, shape, dt))

            for w in ("wk", "wv"):
                for part in ("hi", "lo"):
                    keep[f"{w}_{part}"] = sbi(f"{w}_{part}", [P, KT, INNER], F32R)
            keep["ctx_g"] = sbi("ctx_g", [P, KT])
            keep["ctx_b"] = sbi("ctx_b", [P, KT])
            keep["v"] = sbi("v", [P, ROW_TILES, HEADS, DHEAD + 1])
            keep["q_stored"] = [inner.enter_context(nc.semaphore(f"q_stored{i}")) for i in range(2)]
            rows = context_rows(nc, inner, d, keep)
            prepare(nc, d, keep, rows)
            attend(nc, d, keep, rows)
        keep["x3"] = sb("x3", [P, BATCH, DIM])
        keep["xt_hi"] = sb("xt_hi", [P, KT, TOKENS], F32R)
        keep["xt_lo"] = sb("xt_lo", [P, KT, TOKENS], F32R)
        keep["routed"] = sb("routed", [P, BATCH, EXPERTS])
        keep["numbers"] = sb("numbers", [P, EXPERTS])
        keep["raw"] = [sb(f"{n}_raw", [P, KT, DIM]) for n in WEIGHTS]
        keep["gate_hi"], keep["gate_lo"] = keep["x_hi"][:, 0], keep["x_hi"][:, 1]
        keep["raw_landed"] = [sem(f"{n}_landed") for n in WEIGHTS]
        keep["raw_hi"] = [sem(f"{n}_hi_ready") for n in WEIGHTS]
        keep["raw_lo"] = [sem(f"{n}_lo_ready") for n in WEIGHTS]
        mix(nc, d, keep)
        experts(nc, d, keep)


def kernel(**inputs):
    import numpy as np
    import concourse.bacc as bacc
    from concourse.bass_utils import run_bass_kernel_spmd

    a = {name: np.asarray(value) for name, value in inputs.items()}

    def column(v):
        return v.reshape(KT, P).T

    wkv = a["L0_xattn_Wkv"]
    wk = wkv[:, :INNER].reshape(DIM, HEADS // 4, 4, 2, HALF).transpose(0, 1, 3, 4, 2).reshape(DIM, INNER)
    arrays = {
        "x": a["x"],
        "ctx": a["ctx_1024"],
        "lat_g": column(a["L0_xattn_ln_lat_g"]),
        "lat_b": column(a["L0_xattn_ln_lat_b"]),
        "ctx_g": column(a["L0_xattn_ln_ctx_g"]),
        "ctx_b": column(a["L0_xattn_ln_ctx_b"]),
        "cos": a["L0_xattn_cos"].T,
        "sin": a["L0_xattn_sin"].T,
        "wq": a["L0_xattn_Wq"],
        "wk": wk,
        "wv": wkv[:, INNER:],
        "wo": a["L0_xattn_Wo"],
        "bo": a["L0_xattn_bo"],
        "qkv_w": a["L0_attn_qkv_w"],
        "qkv_b": a["L0_attn_qkv_b"],
        "proj_w": a["L0_attn_proj_w"],
        "proj_b": a["L0_attn_proj_b"],
        "router_w": a["L0_ffn_router_w"],
        "gate": np.concatenate([a["L0_ffn_sg"][None], a["L0_ffn_wg"]]),
        "up": np.concatenate([a["L0_ffn_su"][None], a["L0_ffn_wu"]]),
        "down": np.concatenate([a["L0_ffn_sd"][None], a["L0_ffn_wd"]]),
    }
    nc = bacc.Bacc("TRN2", target_bir_lowering=False, num_devices=1)
    feed, d = {}, {}
    for name, value in arrays.items():
        value = np.ascontiguousarray(value)
        feed[f"in_{name}"] = value
        d[name] = nc.dram_tensor(f"in_{name}", value.shape, mybir.dt.from_np(value.dtype), kind="ExternalInput").ap()
    d["out"] = nc.dram_tensor("out_y", (BATCH, QUERIES, DIM), F32, kind="ExternalOutput").ap()
    program(nc, d)
    result = run_bass_kernel_spmd(nc, [feed], core_ids=[0])
    return result.results[0]["out_y"]
```

```python
from contextlib import ExitStack

import concourse.bass as bass
from concourse import mybir
from concourse.alu_op_type import AluOpType as ALU

F32 = mybir.dt.float32
F32R = mybir.dt.float32r
U32 = mybir.dt.uint32
ACT = mybir.ActivationFunctionType
AX_X = mybir.AxisListType.X

P = 128
BATCH = 4
QUERIES = 128
CTX = 2048
DIM = 512
KT = DIM // P
EPS = 1e-5

HEADS = 16
DHEAD = 64
HALF = DHEAD // 2
INNER = HEADS * DHEAD
CLIP = 11.0
SCALE = DHEAD ** -0.5
CHUNK = 512
ROW_TILES = CHUNK // P
CHUNKS = CTX // CHUNK
STEPS = 8
BSTEPS = STEPS * CHUNKS
PAIRS = HEADS // 2
SCORE_LAG = 4
QUERY_SLOTS = 4
VALUE_LAG = 5

LHEADS = 16
LD = DIM // LHEADS
NORM_EPS = 1e-12
GROUP = P // LD

EXPERTS = 8
ALL_EXPERTS = EXPERTS + 1
GATE, UP, DOWN = range(3)
WEIGHTS = ("gate", "up", "down")
TOKENS = BATCH * QUERIES


def wait(eng, sem, value):
    if isinstance(value, int) and value <= 0:
        return
    eng.wait_ge(sem, value)




def context_rows(nc, ctx, d, keep):
    def sb(name, shape, dt=F32):
        return ctx.enter_context(nc.sbuf_tensor(name, shape, dt))

    def sem(name):
        return ctx.enter_context(nc.semaphore(name))

    r = {}
    r["ident"], r["minus_half"], r["ctx_g"], r["ctx_b"] = (keep[n] for n in ("ident", "minus_half", "ctx_g", "ctx_b"))
    r["source"] = d["ctx"].rearrange("b (t p) d -> (b t) p d", p=P)
    r["row_in"] = keep["row_in"]
    r["stats"] = sb("stats", [P, ROW_TILES, 6])
    r["mean_var"] = sb("mean_var", [P, ROW_TILES, 2])
    r["var_eps"] = sb("var_eps", [P, ROW_TILES])
    r["rstd"] = sb("rstd", [P, ROW_TILES])
    r["x_full"] = keep["x_full"]
    r["x_hi"] = keep["x_hi"]
    r["x_lo"] = sb("x_lo", [P, 2, KT, CHUNK], F32R)
    r["ps_tr"] = ctx.enter_context(nc.psum_tensor("ps_tr", [P, KT, P], F32))
    r["row_landed"] = [sem(f"row_landed{i}") for i in range(ROW_TILES)]
    r["stats_ready"] = sem("stats_ready")
    r["mean_ready"] = sem("mean_ready")
    r["var_ready"] = sem("var_ready")
    r["rstd_ready"] = sem("rstd_ready")
    r["row_ready"] = sem("row_ready")
    r["tr_ready"] = sem("tr_ready")
    r["full_ready"] = sem("full_ready")
    r["hi_ready"] = sem("hi_ready")
    r["lo_ready"] = sem("lo_ready")
    return r


def load_row_tile(nc, r, sp, tile, slot):
    wait(sp, r["tr_ready"], tile - (ROW_TILES - 1))
    sp.dma_start(r["row_in"][:, slot, :], r["source"][tile]).then_inc(r["row_landed"][slot], 16)


def measure_row_tile(nc, r, dve, tile, slot, turn):
    wait(dve, r["row_landed"][slot], 16 * turn)
    wait(dve, r["row_ready"], tile - (ROW_TILES - 1))
    nc.vector.bn_stats(r["stats"][:, slot, :], r["row_in"][:, slot, :]).then_inc(r["stats_ready"], 1)


def row_tile_variance(nc, r, dve, tile, slot):
    var = r["mean_var"][:, slot, 1:2]
    nc.vector.bn_aggr(r["mean_var"][:, slot, :], r["stats"][:, slot, :]).then_inc(r["mean_ready"], 1)
    wait(dve, r["mean_ready"], tile + 1)
    nc.vector.tensor_scalar(r["var_eps"][:, slot:slot + 1], var, EPS, None, ALU.add).then_inc(r["var_ready"], 1)


def row_tile_power(nc, r, pool, tile, slot):
    wait(pool, r["var_ready"], tile + 1)
    nc.gpsimd.tensor_tensor(r["rstd"][:, slot:slot + 1], r["var_eps"][:, slot:slot + 1],
                            r["minus_half"][:, 0:1], ALU.pow).then_inc(r["rstd_ready"], 1)


def normalise_row_tile(nc, r, dve, tile, slot):
    wait(dve, r["rstd_ready"], tile + 1)
    nc.vector.tensor_scalar(r["row_in"][:, slot, :], r["row_in"][:, slot, :], r["mean_var"][:, slot, 0:1],
                            r["rstd"][:, slot:slot + 1], ALU.subtract, ALU.mult).then_inc(r["row_ready"], 1)


def transpose_row_tile(nc, r, pe, tile, slot):
    wait(pe, r["row_ready"], tile + 1)
    wait(pe, r["full_ready"], tile)
    for k in range(KT):
        tr = nc.tensor.transpose(r["ps_tr"][:, k, :], r["row_in"][:, slot, k * P:(k + 1) * P], r["ident"][:])
    tr.then_inc(r["tr_ready"], 1)


def scale_row_tile(nc, r, dve, tile, slot):
    wait(dve, r["tr_ready"], tile + 1)
    wait(dve, r["lo_ready"], tile - 1)
    for k in range(KT):
        out = nc.vector.tensor_scalar(r["x_full"][:, slot % 2, k, :], r["ps_tr"][:, k, :], r["ctx_g"][:, k:k + 1],
                                      r["ctx_b"][:, k:k + 1], ALU.mult, ALU.add)
    out.then_inc(r["full_ready"], 1)


def row_tile_high(nc, r, act, tile, buf, slot):
    wait(act, r["full_ready"], tile + 1)
    nc.scalar.activation(r["x_hi"][:, buf, :, slot * P:(slot + 1) * P], r["x_full"][:, slot % 2],
                         ACT.Copy).then_inc(r["hi_ready"], 1)


def row_tile_low(nc, r, pool, tile, buf, slot):
    wait(pool, r["hi_ready"], tile + 1)
    cols = slice(slot * P, (slot + 1) * P)
    nc.gpsimd.tensor_tensor(r["x_lo"][:, buf, :, cols], r["x_full"][:, slot % 2],
                            r["x_hi"][:, buf, :, cols].bitcast(F32), ALU.subtract).then_inc(r["lo_ready"], 1)


def load_angles(sp, d, keep, chunk, slot):
    for i, n in enumerate(("cos", "sin")):
        angles = bass.AP(d[n].tensor, chunk * CHUNK, [[CTX, HALF], [0, P // HALF], [1, CHUNK]])
        sp.dma_start(keep["angles"][:, slot, i, :], angles).then_inc(keep["angles_landed"][slot], 16)


def prepare(nc, d, keep, rows):
    with ExitStack() as ctx:
        def sb(name, shape, dt=F32):
            return ctx.enter_context(nc.sbuf_tensor(name, shape, dt))

        def sem(name):
            return ctx.enter_context(nc.semaphore(name))

        x_in = sb("x_in", [P, BATCH, DIM])
        wq = sb("wq", [P, KT, INNER])
        w_raw = sb("w_raw", [P, 2, INNER])
        lat_g = sb("lat_g", [P, KT])
        lat_b = sb("lat_b", [P, KT])
        stats = sb("a_stats", [P, BATCH, 6])
        mean_var = sb("a_mean_var", [P, BATCH, 2])
        var_eps = sb("a_var_eps", [P, BATCH])
        rstd = sb("a_rstd", [P, BATCH])
        lat_t = sb("lat_t", [P, KT, TOKENS])
        ones = sb("ones", [P, ROW_TILES, HEADS, 1])
        q_stage = sb("q_stage", [P, 2, BATCH, 2, QUERIES], F32R)
        ps = ctx.enter_context(nc.psum_tensor("a_ps", [P, 7, 512], F32))

        x_landed = [sem(f"a_x_landed{i}") for i in range(BATCH)]
        small_landed = sem("a_small_landed")
        wq_landed = sem("a_wq_landed")
        raw_landed = [sem(f"a_raw_landed{i}") for i in range(2)]
        raw_hi = sem("a_raw_hi")
        raw_lo = sem("a_raw_lo")
        const_ready = sem("a_const_ready")
        ones_ready = sem("a_ones_ready")
        dve_step = sem("a_dve_step")
        var_ready = sem("a_var_ready")
        rstd_ready = sem("a_rstd_ready")
        norm_ready = sem("a_norm_ready")
        tr_ready = sem("a_tr_ready")
        lat_ready = sem("a_lat_ready")
        q_ready = sem("a_q_ready")
        q_hi = sem("a_q_hi")
        q_lo = sem("a_q_lo")
        q_stored = keep["q_stored"]

        pieces = [(w, k) for w in ("wv", "wk") for k in range(KT)]

        def piece(part, n):
            w, k = pieces[n]
            return keep[f"{w}_{part}"][:, k, :]

        def q_bank(m):
            return (BATCH + m) % 7

        def by_batch(m):
            return ps[:, q_bank(m), :].rearrange("p (b n) -> p b n", n=QUERIES)

        block = ctx.enter_context(nc.Block())

        @block.sync
        def _(sp):
            for b in range(BATCH):
                sp.dma_start(x_in[:, b, :], d["x"][b]).then_inc(x_landed[b], 16)
            for n, to in (("lat_g", lat_g), ("lat_b", lat_b), ("ctx_g", keep["ctx_g"]), ("ctx_b", keep["ctx_b"])):
                sp.dma_start(to[:], d[n]).then_inc(small_landed, 16)
            for i in range(ROW_TILES):
                load_row_tile(nc, rows, sp, i, i)
            sp.dma_start(wq[:], d["wq"].rearrange("(t p) n -> p t n", p=P)).then_inc(wq_landed, 16)

            def load_piece(n):
                if n >= 2:
                    sp.wait_ge(raw_lo, n - 1)
                w, k = pieces[n]
                sp.dma_start(w_raw[:, n % 2], d[w][k * P:(k + 1) * P, :]).then_inc(raw_landed[n % 2], 16)

            load_piece(0)
            load_piece(1)
            for m in range(PAIRS):
                if m + 2 < len(pieces):
                    load_piece(m + 2)
                if m == 1:
                    load_angles(sp, d, keep, 0, 0)
                if m == 4:
                    load_row_tile(nc, rows, sp, ROW_TILES, 0)
                sp.wait_ge(q_lo, m + 1)
                sp.dma_start(d["q_scratch"][m], q_stage[:, m % 2].rearrange("p b w n -> p b (w n)").bitcast(F32)).then_inc(q_stored[m % 2], 16)

        @block.gpsimd
        def _(pool):
            nc.gpsimd.memset(keep["ident"][:], 0.0).then_inc(const_ready, 1)
            nc.gpsimd.memset(keep["minus_half"][:], -0.5).then_inc(const_ready, 1)
            nc.gpsimd.memset(ones[:], 1.0).then_inc(const_ready, 1)
            pool.wait_ge(const_ready, 3)
            nc.gpsimd.affine_select(out=keep["ident"][:], in_=keep["ident"][:], compare_op=ALU.not_equal, fill=1.0,
                                    base=0, pattern=[[-1, P]], channel_multiplier=1).then_inc(const_ready, 1)

            def latent_power(r):
                pool.wait_ge(var_ready, r + 1)
                nc.gpsimd.tensor_tensor(rstd[:], var_eps[:], keep["minus_half"][:, 0:BATCH], ALU.pow).then_inc(rstd_ready, 1)

            def weights_low(n):
                pool.wait_ge(raw_hi, n + 1)
                nc.gpsimd.tensor_tensor(piece("lo", n), w_raw[:, n % 2], piece("hi", n).bitcast(F32),
                                        ALU.subtract).then_inc(raw_lo, 1)

            latent_power(0)
            latent_power(1)
            for i in range(ROW_TILES):
                row_tile_power(nc, rows, pool, i, i)
            weights_low(0)
            weights_low(1)
            for i in range(ROW_TILES):
                row_tile_low(nc, rows, pool, i, 0, i)
                weights_low(i + 2)
            for n in range(ROW_TILES + 2, len(pieces)):
                weights_low(n)

        @block.scalar
        def _(act):
            def weights_high(n):
                act.wait_ge(raw_landed[n % 2], 16 * (n // 2 + 1))
                nc.scalar.activation(piece("hi", n), w_raw[:, n % 2], ACT.Copy).then_inc(raw_hi, 1)

            def queries_high(m):
                act.wait_ge(q_ready, m + 1)
                if m >= 2:
                    act.wait_ge(q_stored[m % 2], 16 * (m // 2))
                nc.scalar.activation(q_stage[:, m % 2, :, 0, :], by_batch(m), ACT.Copy).then_inc(q_hi, 1)

            act.wait_ge(const_ready, 4)
            nc.scalar.activation(keep["v_hi"][:, :, :, DHEAD:DHEAD + 1], ones[:], ACT.Copy).then_inc(ones_ready, 1)
            weights_high(0)
            weights_high(1)
            for m in range(PAIRS):
                queries_high(m)
                if m < ROW_TILES:
                    row_tile_high(nc, rows, act, m, 0, m)
                if m + 2 < len(pieces):
                    weights_high(m + 2)

        @block.vector
        def _(dve):
            chain = [0]

            def link(ins):
                chain[0] += 1
                ins.then_inc(dve_step, 1)
                dve.wait_ge(dve_step, chain[0])

            def latent_variances(r):
                for b in range(BATCH):
                    if r == 0:
                        dve.wait_ge(x_landed[b], 16)
                    stat = nc.vector.bn_stats(stats[:, b, :], x_in[:, b, :])
                link(stat)
                for b in range(BATCH):
                    stat = nc.vector.bn_aggr(mean_var[:, b, :], stats[:, b, :])
                link(stat)
                nc.vector.tensor_scalar(var_eps[:], mean_var[:, :, 1], EPS, None, ALU.add).then_inc(var_ready, 1)

            def latent_norm(r):
                dve.wait_ge(rstd_ready, r + 1)
                for b in range(BATCH):
                    nc.vector.tensor_scalar(x_in[:, b, :], x_in[:, b, :], mean_var[:, b, 0:1],
                                            rstd[:, b:b + 1], ALU.subtract, ALU.mult).then_inc(norm_ready, 1)

            latent_variances(0)
            for i in range(2):
                measure_row_tile(nc, rows, dve, i, i, 1)
            latent_norm(0)
            dve.wait_ge(norm_ready, BATCH)
            latent_variances(1)
            for i in range(2, ROW_TILES):
                measure_row_tile(nc, rows, dve, i, i, 1)
            latent_norm(1)
            dve.wait_ge(small_landed, 16 * 4)
            for b in range(BATCH):
                dve.wait_ge(tr_ready, b + 1)
                for t in range(KT):
                    out = nc.vector.tensor_scalar(lat_t[:, t, b * P:(b + 1) * P], ps[:, b, t * P:(t + 1) * P],
                                                  lat_g[:, t:t + 1], lat_b[:, t:t + 1], ALU.mult, ALU.add)
                out.then_inc(lat_ready, 1)
            for i in range(ROW_TILES):
                dve.wait_ge(rows["stats_ready"], i + 1)
                row_tile_variance(nc, rows, dve, i, i)
            for i in range(ROW_TILES):
                normalise_row_tile(nc, rows, dve, i, i)
            for m in range(PAIRS):
                dve.wait_ge(q_hi, m + 1)
                nc.vector.tensor_tensor(q_stage[:, m % 2, :, 1, :], by_batch(m), q_stage[:, m % 2, :, 0, :].bitcast(F32),
                                        ALU.subtract).then_inc(q_lo, 1)
                if m < ROW_TILES:
                    scale_row_tile(nc, rows, dve, m, m)
                if m == 5:
                    measure_row_tile(nc, rows, dve, ROW_TILES, 0, 2)

        @block.tensor
        def _(pe):
            pe.wait_ge(const_ready, 4)
            for b in range(BATCH):
                pe.wait_ge(norm_ready, BATCH + b + 1)
                for t in range(KT):
                    tr = nc.tensor.transpose(ps[:, b, t * P:(t + 1) * P], x_in[:, b, t * P:(t + 1) * P], keep["ident"][:])
                tr.then_inc(tr_ready, 1)
            pe.wait_ge(lat_ready, BATCH)
            pe.wait_ge(wq_landed, 16)
            for m in range(PAIRS):
                if m >= 7:
                    pe.wait_ge(q_lo, m - 6)
                for t in range(KT):
                    mm = nc.tensor.matmul(ps[:, q_bank(m), :], wq[:, t, m * P:(m + 1) * P], lat_t[:, t, :],
                                          start=(t == 0), stop=(t == KT - 1))
                mm.then_inc(q_ready, 1)
                if m < ROW_TILES:
                    transpose_row_tile(nc, rows, pe, m, m)


def attend(nc, d, keep, rows):
    with ExitStack() as ctx:
        def sb(name, shape, dt=F32):
            return ctx.enter_context(nc.sbuf_tensor(name, shape, dt))

        def psum(name, shape):
            return ctx.enter_context(nc.psum_tensor(name, shape, F32))

        def sem(name):
            return ctx.enter_context(nc.semaphore(name))

        wk_hi, wk_lo, wv_hi, wv_lo = (keep[n] for n in ("wk_hi", "wk_lo", "wv_hi", "wv_lo"))
        angles, v_hi = keep["angles"], keep["v_hi"]
        x_hi, x_lo = rows["x_hi"], rows["x_lo"]
        a_cos, b_cos, b_sin, a_sin = (keep["turned"][:, i, :] for i in range(4))
        first_hi, second_hi = b_sin.bitcast(F32R), a_sin.bitcast(F32R)
        keys = sb("keys", [P, 2, 4, CHUNK], F32R)
        queries = sb("queries", [P, QUERY_SLOTS, 2, 2, QUERIES], F32R)
        v_lo = sb("v_lo", [P, ROW_TILES, HEADS, DHEAD], F32R)
        probs = sb("probs", [P, 2, 2, CHUNK])
        p_parts = sb("p_parts", [P, 2, 2, CHUNK], F32R)
        acc = sb("acc", [DHEAD + 1, HEADS, QUERIES])
        recip = sb("recip", [P, 2])
        attn = sb("attn", [P, 2, 2 * DHEAD])

        ps_v = psum("ps_v", [P, 2, 512])
        ps_k = psum("ps_k", [P, 2, 512])
        ps_s = psum("ps_s", [P, ROW_TILES, 2, QUERIES])
        ps_o = psum("ps_o", [P, 2, 2, QUERIES])

        v_ready = sem("v_ready")
        v_hi_ready = sem("v_hi_ready")
        v_stored = sem("v_stored")
        k_ready = sem("k_ready")
        k_turned = sem("k_turned")
        rope_ready = sem("rope_ready")
        rope_hi = sem("rope_hi")
        rope_lo = sem("rope_lo")
        keys_landed = [sem(f"keys_landed{i}") for i in range(2)]
        q_landed = [sem(f"q_landed{i}") for i in range(QUERY_SLOTS)]
        s_ready = sem("s_ready")
        s_copied = sem("s_copied")
        s_taken = sem("s_taken")
        clipped = sem("clipped")
        probs_ready = sem("probs_ready")
        p_hi_ready = sem("p_hi_ready")
        p_lo_ready = sem("p_lo_ready")
        o_ready = sem("o_ready")
        o_first = sem("o_first")
        o_added = sem("o_added")
        o_turned = sem("o_turned")
        recip_ready = sem("recip_ready")
        attn_ready = sem("attn_ready")
        attn_stored = [sem(f"attn_stored{i}") for i in range(2)]
        STORES = PAIRS // 2

        ROWS_OF_BATCH = CTX // P
        last_step = BATCH * BSTEPS

        def run(eng, step):
            for t in range(STEPS):
                step(0, t)
            with eng.Fori(0, BATCH - 1) as b:
                for t in range(STEPS, STEPS + BSTEPS):
                    step(b, t)
            for t in range(STEPS, BSTEPS + VALUE_LAG + 2):
                step(BATCH - 1, t)

        def exists(b, t):
            return not isinstance(b, int) or 0 <= BSTEPS * b + t < last_step

        def turned_sums():
            return ps_o[:, :, 0, 0:DHEAD + 1]

        def last_batch(b, pair):
            return isinstance(b, int) and BSTEPS * b + pair >= BSTEPS * (BATCH - 1)

        def next_row_tile(b, t):
            if t % 2 == 0 and exists(b, t) and exists(b, t + STEPS):
                return b * ROWS_OF_BATCH + (t // 2 + ROW_TILES)
            return None

        block = ctx.enter_context(nc.Block())

        @block.sync
        def _(sp):
            def load_queries(b, pair):
                slot = pair % QUERY_SLOTS
                for side in range(2):
                    whose = d["q_scratch"][pair % PAIRS].rearrange("(j e) b c -> b e j c", j=2)[b + pair // BSTEPS]
                    there = queries[DHEAD * side:DHEAD * (side + 1), slot].rearrange("e j w n -> e j (w n)")
                    sp.dma_start(there.bitcast(F32), whose).then_inc(q_landed[slot], 16)

            for i in range(2):
                sp.wait_ge(keep["q_stored"][i], 16 * PAIRS // 2)

            def step(b, t):
                if t % 2 == 0 and exists(b, t - 3):
                    wait(sp, s_ready, b * (2 * BSTEPS) + 2 * (t - 1 - QUERY_SLOTS))
                tile = next_row_tile(b, t)
                if tile is not None:
                    if not (isinstance(tile, int) and tile == ROW_TILES):
                        slot = t // 2 % ROW_TILES
                        sp.dma_start(rows["row_in"][:, slot, :], rows["source"][tile]).then_inc(rows["row_landed"][slot], 16)
                for pair in (t - 3, t - 2):
                    if t % 2 == 0 and exists(b, pair):
                        load_queries(b, pair)
                if t % STEPS == 2 and exists(b, t - 2 + STEPS):
                    wait(sp, k_turned, b * BSTEPS + t - 2)
                    load_angles(sp, d, keep, (t // STEPS + 1) % CHUNKS, (t // STEPS + 1) % 2)
                if t % 2 == 0 and exists(b, t - 2):
                    group = b * (BSTEPS // 2) + (t // 2 - 1)
                    slot = (t // 2 - 1) % 2
                    parts = ((rope_hi, first_hi, 1), (rope_hi, second_hi, 2),
                             (rope_lo, a_cos, 1), (rope_lo, b_cos, 2))
                    for i, (made, part, n) in enumerate(parts):
                        wait(sp, made, 2 * group + n)
                        sp.dma_start(keys[HALF * i:HALF * (i + 1), slot].bitcast(F32),
                                     part.bitcast(F32)).then_inc(keys_landed[slot], 16)
                if isinstance(b, int) and b == BATCH - 1 and t == BSTEPS + 1:
                    for i in range(2):
                        wait(sp, keys_landed[i], 64 * BATCH * BSTEPS // 4)
                    sp.dma_start(keep["wo"][:], d["wo"].rearrange("(t p) n -> p t n", p=P)).then_inc(keep["wo_landed"], 16)
                    wait(sp, rows["tr_ready"], BATCH * ROWS_OF_BATCH)
                    for i in range(2):
                        wait(sp, attn_stored[i], 16 * STORES * (BATCH - 1))
                    for early in range(2):
                        sp.dma_start(keep["attn_early"][:, early, :], d["attn_scratch"][early]).then_inc(keep["attn_landed"], 16)
                pair = t - VALUE_LAG - 2
                if exists(b, pair) and pair // STEPS % CHUNKS == CHUNKS - 1 and not last_batch(b, pair):
                    m = pair % STEPS
                    whose = b + pair // BSTEPS
                    wait(sp, attn_ready, PAIRS * whose + (m + 1))
                    sp.dma_start(d["attn_scratch"][whose][:, m * P:(m + 1) * P], attn[:, m % 2, :]).then_inc(attn_stored[m % 2], 16)

            run(sp, step)
            for i in range(2):
                sp.wait_ge(attn_stored[i], 16 * STORES * (BATCH - 1))

        @block.gpsimd
        def _(pool):
            def step(b, t):
                tile = next_row_tile(b, t)
                if tile is not None:
                    row_tile_power(nc, rows, pool, tile, t // 2 % ROW_TILES)
                pair = t - VALUE_LAG
                if exists(b, pair):
                    for j in range(2):
                        wait(pool, p_hi_ready, b * (2 * BSTEPS) + (2 * pair + j + 1))
                        nc.gpsimd.tensor_tensor(p_parts[:, 1, j, :], probs[:, pair % 2, j, :], p_parts[:, 0, j, :].bitcast(F32),
                                                ALU.subtract).then_inc(p_lo_ready, 1)
                tile = next_row_tile(b, t - 1)
                if tile is not None:
                    row_tile_low(nc, rows, pool, tile, (t // STEPS + 1) % 2, t // 2 % ROW_TILES)
                if t % 2 == 0 and exists(b, t - 2):
                    group = b * (BSTEPS // 2) + (t // 2 - 1)
                    for n, (full, hi) in enumerate(((a_cos, first_hi), (b_cos, second_hi))):
                        wait(pool, rope_hi, 2 * group + (n + 1))
                        nc.gpsimd.tensor_tensor(full.bitcast(F32R), full, hi.bitcast(F32),
                                                ALU.subtract).then_inc(rope_lo, 1)

            run(pool, step)

        @block.scalar
        def _(act):
            def copy_scores(b, pair, j):
                if exists(b, pair):
                    count = b * (2 * BSTEPS) + (2 * pair + j + 1)
                    if j == 0:
                        wait(act, o_ready, b * BSTEPS + (pair - 1))
                    wait(act, s_ready, count)
                    nc.scalar.activation(probs[:, pair % 2, j, :].rearrange("p (i n) -> p i n", n=P), ps_s[:, :, 1, :],
                                         ACT.Copy).then_inc(s_copied, 1)

            def step(b, t):
                copy_scores(b, t - VALUE_LAG, 1)
                pair = t - VALUE_LAG
                if exists(b, pair):
                    wait(act, clipped, b * (2 * BSTEPS) + 2 * (pair + 1))
                    nc.scalar.activation(probs[:, pair % 2], probs[:, pair % 2], ACT.Exp, scale=SCALE).then_inc(probs_ready, 1)
                    wait(act, probs_ready, b * BSTEPS + (pair + 1))
                    wait(act, o_ready, b * BSTEPS + pair)
                    for j in range(2):
                        nc.scalar.activation(p_parts[:, 0, j, :], probs[:, pair % 2, j, :], ACT.Copy).then_inc(p_hi_ready, 1)
                copy_scores(b, t - SCORE_LAG, 0)
                if t % 2 == 1:
                    tile = next_row_tile(b, t - 1)
                    if tile is not None:
                        wait(act, k_ready, 2 * tile - 2 * (t // 2 % ROW_TILES) - STEPS)
                        row_tile_high(nc, rows, act, tile, (t // STEPS + 1) % 2, t // 2 % ROW_TILES)
                if exists(b, t - 1):
                    p = (t - 1) % STEPS
                    wait(act, v_ready, b * BSTEPS + t)
                    wait(act, o_ready, b * BSTEPS + (t - 1 - p - STEPS + 4 * (p // 4 + 1)))
                    half = p // ROW_TILES
                    nc.scalar.activation(v_hi[:, p % ROW_TILES, 8 * half:8 * half + 8, 0:DHEAD],
                                         ps_v[:, (t - 1) % 2, :].rearrange("p (h e) -> p h e", e=DHEAD), ACT.Copy).then_inc(v_hi_ready, 1)
                if t % 2 == 0 and exists(b, t - 2):
                    group = b * (BSTEPS // 2) + (t // 2 - 1)
                    for n, (full, hi) in enumerate(((a_cos, first_hi), (b_cos, second_hi))):
                        wait(act, rope_ready, 2 * group + (n + 1))
                        nc.scalar.activation(hi, full, ACT.Copy).then_inc(rope_hi, 1)

            run(act, step)

        @block.vector
        def _(dve):
            def take_scores(b, pair, j):
                if exists(b, pair):
                    taken = b * (2 * BSTEPS) + (2 * pair + j + 1)
                    mine = probs[:, pair % 2, j, :]
                    wait(dve, s_copied, taken)
                    tiles = mine.rearrange("p (i n) -> p i n", n=P)
                    nc.vector.tensor_tensor(tiles, ps_s[:, :, 0, :], tiles, ALU.add).then_inc(s_taken, 1)
                    wait(dve, s_taken, taken)
                    nc.vector.tensor_scalar(mine, mine, CLIP / SCALE, -CLIP / SCALE, ALU.min, ALU.max).then_inc(clipped, 1)

            def finish(b, pair):
                if exists(b, pair) and pair // STEPS % CHUNKS == CHUNKS - 1:
                    m = pair % STEPS
                    whose = b + pair // BSTEPS
                    done = PAIRS * whose + m
                    wait(dve, o_turned, done + 1)
                    if m >= 1:
                        wait(dve, attn_ready, done)
                    if m >= 2 and not last_batch(b, pair):
                        wait(dve, attn_stored[m % 2], 16 * (STORES * whose + m // 2))
                    rows_of = turned_sums()
                    nc.vector.reciprocal(recip[:], rows_of[:, :, DHEAD]).then_inc(recip_ready, 1)
                    wait(dve, recip_ready, done + 1)
                    there = keep["attn_last"][:, m * P:(m + 1) * P] if last_batch(b, pair) else attn[:, m % 2, :]
                    for j in range(2):
                        out = nc.vector.tensor_scalar(there[:, j * DHEAD:(j + 1) * DHEAD], rows_of[:, j, 0:DHEAD],
                                                      recip[:, j:j + 1], None, ALU.mult)
                    out.then_inc(attn_ready, 1)

            def rotate(b, t, last):
                if not exists(b, t - 1):
                    return
                n = b * BSTEPS + (t - 1)
                turn = (t - 1) // STEPS % 2
                if not last and (t - 1) % STEPS == 0:
                    wait(dve, keep["angles_landed"][turn], 32 * (b * (CHUNKS // 2) + ((t - 1) // STEPS // 2 + 1)))
                if not last:
                    wait(dve, k_ready, n + 1)
                if t % 2 == 1 and not last:
                    slot = ((t - 1) // 2 - 1) % 2
                    turns = b * (BSTEPS // 4) + ((t - 1) // 2 - 1) // 2 + 1
                    wait(dve, keys_landed[slot], 64 * turns)
                    nc.vector.tensor_tensor(a_cos, ps_k[:, 0, :], angles[:, turn, 0, :], ALU.mult)
                    nc.vector.tensor_tensor(a_sin, ps_k[:, 0, :], angles[:, turn, 1, :], ALU.mult).then_inc(k_turned, 1)
                if t % 2 == 0 and not last:
                    nc.vector.tensor_tensor(b_sin, ps_k[:, 1, :], angles[:, turn, 1, :], ALU.mult)
                    nc.vector.tensor_tensor(b_cos, ps_k[:, 1, :], angles[:, turn, 0, :], ALU.mult).then_inc(k_turned, 1)
                    wait(dve, k_turned, n + 1)
                    nc.vector.tensor_tensor(a_cos, a_cos, b_sin, ALU.subtract).then_inc(rope_ready, 1)
                if t % 2 == 0 and last:
                    nc.vector.tensor_tensor(b_cos, b_cos, a_sin, ALU.add).then_inc(rope_ready, 1)

            def values_low(b, t):
                if exists(b, t):
                    p = t % STEPS
                    half = p // ROW_TILES
                    wait(dve, v_hi_ready, b * BSTEPS + (t + 1))
                    place = (slice(None), p % ROW_TILES, slice(8 * half, 8 * half + 8), slice(0, DHEAD))
                    nc.vector.tensor_tensor(v_lo[place], ps_v[:, t % 2, :].rearrange("p (h e) -> p h e", e=DHEAD),
                                            v_hi[place].bitcast(F32), ALU.subtract).then_inc(v_stored, 1)

            def step(b, t):
                tile = next_row_tile(b, t)
                if tile is not None:
                    wait(dve, rows["stats_ready"], tile + 1)
                take_scores(b, t - VALUE_LAG, 1)
                if tile is not None:
                    row_tile_variance(nc, rows, dve, tile, t // 2 % ROW_TILES)
                pair = t - VALUE_LAG - 1
                if exists(b, pair):
                    n = b * BSTEPS + pair
                    m = pair % STEPS
                    mine = acc[:, 2 * m:2 * m + 2, :]
                    got = ps_o[0:DHEAD + 1]
                    chunk = pair // STEPS % CHUNKS
                    wait(dve, o_ready, n + 1)
                    whose = b + pair // BSTEPS
                    if chunk == 0 and m == 1:
                        for slot in range(2):
                            wait(dve, attn_stored[slot], 16 * STORES * whose)
                    if chunk == 0:
                        nc.vector.tensor_copy(mine, got[:, :, 0, :]).then_inc(o_first, 1)
                    else:
                        wait(dve, o_added, n - (STEPS - 1))
                        nc.vector.tensor_tensor(mine, got[:, :, 0, :], mine, ALU.add).then_inc(o_first, 1)
                    wait(dve, o_first, n + 1)
                    nc.vector.tensor_tensor(mine, got[:, :, 1, :], mine, ALU.add).then_inc(o_added, 1)
                if t % 2 == 0:
                    rotate(b, t, last=False)
                    take_scores(b, t - SCORE_LAG, 0)
                    rotate(b, t, last=True)
                    finish(b, t - VALUE_LAG - 1)
                    if tile is not None:
                        normalise_row_tile(nc, rows, dve, tile, t // 2 % ROW_TILES)
                    values_low(b, t - 1)
                else:
                    tile = next_row_tile(b, t - 1)
                    if tile is not None:
                        scale_row_tile(nc, rows, dve, tile, t // 2 % ROW_TILES)
                    take_scores(b, t - SCORE_LAG, 0)
                    finish(b, t - VALUE_LAG - 1)
                    rotate(b, t, last=False)
                    values_low(b, t - 1)
                    tile = next_row_tile(b, t + 1)
                    if tile is not None:
                        i = (t + 1) // 2
                        measure_row_tile(nc, rows, dve, tile, i % ROW_TILES, b * CHUNKS + (i // ROW_TILES + 2))

            run(dve, step)

        @block.tensor
        def _(pe):
            def product(out, left, right, first, last):
                nc.tensor.matmul(out, left[0], right[0], start=first, stop=False)
                nc.tensor.matmul(out, left[0], right[1], start=False, stop=False)
                return nc.tensor.matmul(out, left[1], right[0], start=False, stop=last)

            def ends_batch(b, pair):
                return exists(b, pair) and pair // STEPS % CHUNKS == CHUNKS - 1

            def turn_sums(b, pair):
                if ends_batch(b, pair):
                    wait(pe, o_added, b * BSTEPS + (pair + 1))
                    for j in range(2):
                        tr = nc.tensor.transpose(turned_sums()[:, j, :], acc[:, 2 * (pair % STEPS) + j, :],
                                                 keep["ident"][0:DHEAD + 1, 0:DHEAD + 1])
                    tr.then_inc(o_turned, 1)

            def score(b, pair, j):
                if exists(b, pair):
                    slot = pair // 2 % 2
                    if j == 0:
                        wait(pe, keys_landed[slot], 64 * (b * (BSTEPS // 4) + pair // 4 + 1))
                        wait(pe, q_landed[pair % QUERY_SLOTS], 32 * (b * (BSTEPS // QUERY_SLOTS) + (pair // QUERY_SLOTS + 1)))
                    wait(pe, s_taken, b * (2 * BSTEPS) + (2 * pair + j))
                    for i in range(ROW_TILES):
                        mm = nc.tensor.matmul(ps_s[:, i], keys[:, slot, 2 * (pair % 2) + j, i * P:(i + 1) * P],
                                              queries[:, pair % QUERY_SLOTS, j], start=True, stop=True)
                    mm.then_inc(s_ready, 1)

            def step(b, t):
                p = t % STEPS
                buf = t // STEPS % 2
                if exists(b, t):
                    n = b * BSTEPS + t
                    if p == 0:
                        wait(pe, rows["lo_ready"], b * ROWS_OF_BATCH + (t // 2 + ROW_TILES))
                    wait(pe, v_stored, n - 1)
                    for k in range(KT):
                        cols = slice(p % ROW_TILES * P, (p % ROW_TILES + 1) * P)
                        heads = slice(p // ROW_TILES * 512, (p // ROW_TILES + 1) * 512)
                        mm = product(ps_v[:, t % 2, :], (x_hi[:, buf, k, cols], x_lo[:, buf, k, cols]),
                                     (wv_hi[:, k, heads], wv_lo[:, k, heads]), k == 0, k == KT - 1)
                    mm.then_inc(v_ready, 1)
                score(b, t - SCORE_LAG, 0)
                turn_sums(b, t - VALUE_LAG - 1)
                if exists(b, t):
                    n = b * BSTEPS + t
                    wait(pe, k_turned, n - 1)
                    for k in range(KT):
                        cols = slice(p * P, (p + 1) * P)
                        mm = product(ps_k[:, t % 2, :], (wk_hi[:, k, cols], wk_lo[:, k, cols]),
                                     (x_hi[:, buf, k, :], x_lo[:, buf, k, :]), k == 0, k == KT - 1)
                    mm.then_inc(k_ready, 1)
                score(b, t - SCORE_LAG, 1)
                pair = t - VALUE_LAG
                if exists(b, pair):
                    n = b * BSTEPS + pair
                    m = pair % STEPS
                    wait(pe, o_added, n)
                    if ends_batch(b, pair - 1):
                        wait(pe, attn_ready, PAIRS * (b + (pair - 1) // BSTEPS) + ((pair - 1) % STEPS + 1))
                    wait(pe, v_stored, b * BSTEPS + (pair - m + 4 * (m // 4 + 1)))
                    for j in range(2):
                        wait(pe, p_lo_ready, b * (2 * BSTEPS) + (2 * pair + j + 1))
                        out = ps_o[0:DHEAD + 1, j]
                        for i in range(ROW_TILES):
                            cols = slice(i * P, (i + 1) * P)
                            if i >= 1:
                                nc.tensor.matmul(ps_o[0:DHEAD, j, 0, :], v_lo[:, i, 2 * m + j, :], p_parts[:, 0, j, cols],
                                                 start=False, stop=False)
                            mm = nc.tensor.matmul(out, v_hi[:, i, 2 * m + j, :], p_parts[:, :, j, cols],
                                                  start=(i == 0), stop=(i == ROW_TILES - 1))
                            if i == 0:
                                nc.tensor.matmul(ps_o[0:DHEAD, j, 0, :], v_lo[:, i, 2 * m + j, :], p_parts[:, 0, j, cols],
                                                 start=False, stop=False)
                    mm.then_inc(o_ready, 1)
                tile = next_row_tile(b, t)
                if tile is not None:
                    transpose_row_tile(nc, rows, pe, tile, t // 2 % ROW_TILES)

            run(pe, step)


def mix(nc, d, keep):
    with ExitStack() as ctx:
        def sb(name, shape, dt=F32):
            return ctx.enter_context(nc.sbuf_tensor(name, shape, dt))

        def sem(name):
            return ctx.enter_context(nc.semaphore(name))

        x3, xt_hi, xt_lo = (keep[n] for n in ("x3", "xt_hi", "xt_lo"))
        ident, wo, routed = keep["ident"], keep["wo"], keep["routed"]
        late = sb("attn_late", [P, INNER])
        attn = [keep["attn_last"], keep["attn_early"][:, 0, :], keep["attn_early"][:, 1, :], late[:]]
        batch_of = [BATCH - 1] + list(range(BATCH - 1))
        attn_t = sb("attn_t", [P, INNER // P, TOKENS])
        x_res = sb("x_res", [P, BATCH, DIM])
        qkv_hi = [keep["gate_hi"]] + [sb(f"qkv_hi{j}", [P, KT, DIM], F32R)[:] for j in (1, 2)]
        qkv_lo = [keep["gate_lo"]] + [sb(f"qkv_lo{j}", [P, KT, DIM], F32R)[:] for j in (1, 2)]
        qkv_b = sb("qkv_b", [P, 3 * DIM])
        proj_w = sb("proj_w", [P, KT, DIM])
        router_w = sb("router_w", [P, KT, EXPERTS])
        x_norm = sb("x_norm", [P, BATCH, DIM])
        qkv = sb("qkv", [P, BATCH, 3 * DIM])
        stats = sb("c_stats", [P, BATCH, 6])
        mean_var = sb("c_mean_var", [P, BATCH, 2])
        var_eps = sb("c_var_eps", [P, BATCH])
        rstd = sb("c_rstd", [P, BATCH])
        sums = sb("sums", [P, BATCH, 2 * LHEADS])
        norms = sb("norms", [P, BATCH, 2 * LHEADS])
        half = sb("half", [P, BATCH, 2 * LHEADS])
        block_mask = sb("block_mask", [P, P])
        peak = sb("peak", [P, BATCH])
        squares = attn
        bo, proj_b = (sb(n, [P, DIM])[:] for n in ("bo", "proj_b"))
        out_t = keep["attn_early"].rearrange("p b (t n) -> p (b t) n", n=TOKENS)
        kv = attn_t[:, 0:KT, :]
        x_t = kv
        q_t = attn_t[:, KT:2 * KT, :]
        ps = ctx.enter_context(nc.psum_tensor("c_ps", [P, 8, 512], F32))

        late_landed = sem("c_late_landed")
        x_landed = sem("c_x_landed")
        small_landed = sem("c_small_landed")
        qkv_landed = [sem(f"c_qkv_landed{j}") for j in range(3)]
        qkv_hi_ready = sem("c_qkv_hi_ready")
        qkv_lo_ready = sem("c_qkv_lo_ready")
        proj_landed = sem("c_proj_landed")
        const_ready = sem("c_const_ready")
        attn_turned = sem("c_attn_turned")
        attn_t_ready = [sem(f"c_attn_t_ready{i}") for i in range(2)]
        wo_done = sem("c_wo_done")
        dve_step = sem("c_dve_step")
        var_ready = sem("c_var_ready")
        rstd_ready = sem("c_rstd_ready")
        norm_ready = sem("c_norm_ready")
        x_turned = sem("c_x_turned")
        x_t_ready = sem("c_x_t_ready")
        qkv_done = sem("c_qkv_done")
        qkv_ready = sem("c_qkv_ready")
        squares_ready = sem("c_squares_ready")
        sums_ready = sem("c_sums_ready")
        roots_ready = sem("c_roots_ready")
        unit_ready = sem("c_unit_ready")
        kv_done = sem("c_kv_done")
        kv_ready = sem("c_kv_ready")
        q_turned = sem("c_q_turned")
        q_t_ready = sem("c_q_t_ready")
        out_done = sem("c_out_done")
        out_t_ready = sem("c_out_t_ready")
        proj_done = sem("c_proj_done")
        hi_ready = sem("c_hi_ready")
        lo_ready = sem("c_lo_ready")
        logits_done = sem("c_logits_done")

        def rows_of(name, width):
            return bass.AP(d[name].tensor, 0, [[0, P], [1, width]])

        def tiles(name):
            return d[name].rearrange("(t p) n -> p t n", p=P)

        products = [(0, 0), (0, 1), (0, 2), (1, 0), (1, 1), (1, 2), (2, 0), (2, 1), (3, 0), (3, 1), (2, 2), (3, 2)]
        until_keys = {i: n + 1 for n, (i, j) in enumerate(products) if j == 1}

        block = ctx.enter_context(nc.Block())

        @block.sync
        def _(sp):
            sp.dma_start(late[:], d["attn_scratch"][2]).then_inc(late_landed, 16)
            sp.dma_start(x_res[:], d["x"].rearrange("b n d -> n b d")).then_inc(x_landed, 16)
            sp.dma_start(bo, rows_of("bo", DIM)).then_inc(small_landed, 16)
            sp.dma_start(qkv_b[:], rows_of("qkv_b", 3 * DIM)).then_inc(small_landed, 16)
            sp.dma_start(proj_b, rows_of("proj_b", DIM)).then_inc(small_landed, 16)
            sp.dma_start(router_w[:], tiles("router_w")).then_inc(small_landed, 16)
            for j in range(3):
                sp.dma_start(keep["raw"][j][:], tiles("qkv_w")[:, :, j * DIM:(j + 1) * DIM]).then_inc(qkv_landed[j], 16)
            sp.dma_start(proj_w[:], tiles("proj_w")).then_inc(proj_landed, 16)
            for w in (GATE, UP, DOWN):
                sp.wait_ge(qkv_lo_ready, w + 1)
                sp.dma_start(keep["raw"][w][:], d[WEIGHTS[w]][0].rearrange("(t p) n -> p t n", p=P)).then_inc(keep["raw_landed"][w], 16)

        @block.gpsimd
        def _(pool):
            nc.gpsimd.memset(block_mask[:], 0.0).then_inc(const_ready, 1)
            nc.gpsimd.memset(half[:], 0.5).then_inc(const_ready, 1)
            for e in range(EXPERTS):
                number = nc.gpsimd.memset(keep["numbers"][:, e:e + 1], float(e))
            number.then_inc(const_ready, 1)
            pool.wait_ge(const_ready, 3)
            for g in range(GROUP):
                nc.gpsimd.memset(block_mask[g * LD:(g + 1) * LD, g * LD:(g + 1) * LD], 1.0).then_inc(const_ready, 1)
                pool.wait_ge(const_ready, 3 + g + 1)

            def powers(n, b):
                pool.wait_ge(var_ready, n + 1)
                nc.gpsimd.tensor_tensor(rstd[:, b:b + 1], var_eps[:, b:b + 1], keep["minus_half"][:, 0:1],
                                        ALU.pow).then_inc(rstd_ready, 1)

            for i, b in enumerate(batch_of):
                powers(i, b)
            for i, b in enumerate(batch_of):
                pool.wait_ge(sums_ready, i + 1)
                nc.gpsimd.tensor_tensor(norms[:, b, :], sums[:, b, :], half[:, b, :], ALU.pow).then_inc(roots_ready, 1)
            for b in range(BATCH):
                powers(BATCH + b, b)

        @block.scalar
        def _(act):
            def turned(out, bank, done):
                nc.scalar.activation(out, ps[:, bank, :].rearrange("p (t n) -> p t n", n=P), ACT.Copy).then_inc(done, 1)

            def split_high(w):
                act.wait_ge(keep["raw_landed"][w], 16)
                nc.scalar.activation(keep["gate_hi"], keep["raw"][w][:], ACT.Copy).then_inc(keep["raw_hi"][w], 1)

            for i, b in enumerate(batch_of):
                act.wait_ge(attn_turned, 2 * i + 2)
                turned(attn_t[:, KT:2 * KT, b * P:(b + 1) * P], 2 * i + 1, attn_t_ready[1])
            for j in range(3):
                act.wait_ge(qkv_landed[j], 16)
                nc.scalar.activation(qkv_hi[j], keep["raw"][j][:], ACT.Copy).then_inc(qkv_hi_ready, 1)
            for i, b in enumerate(batch_of):
                act.wait_ge(x_turned, i + 1)
                turned(xt_hi[:, :, b * P:(b + 1) * P], 4 + b, hi_ready)
            for i, b in enumerate(batch_of):
                act.wait_ge(qkv_ready, until_keys[i])
                nc.scalar.activation(squares[b], qkv[:, b, 0:2 * DIM], ACT.Square).then_inc(squares_ready, 1)
            act.wait_ge(qkv_done, until_keys[BATCH - 1])
            split_high(GATE)
            for i, b in enumerate(batch_of):
                act.wait_ge(q_turned, i + 1)
                turned(q_t[:, :, b * P:(b + 1) * P], 4 + b, q_t_ready)
            for i, b in enumerate(batch_of):
                act.wait_ge(out_done, i + 1)
                turned(out_t[:, :, b * P:(b + 1) * P], b, out_t_ready)
            for b in range(BATCH):
                act.wait_ge(x_turned, BATCH + b + 1)
                cols = slice(b * P, (b + 1) * P)
                turned(x_t[:, :, cols], b, x_t_ready)
                turned(xt_hi[:, :, cols], b, hi_ready)

        @block.vector
        def _(dve):
            chain = [0]

            def link(ins):
                chain[0] += 1
                ins.then_inc(dve_step, 1)
                dve.wait_ge(dve_step, chain[0])

            def variance(source, b):
                link(nc.vector.bn_stats(stats[:, b, :], source[:, b, :]))
                link(nc.vector.bn_aggr(mean_var[:, b, :], stats[:, b, :]))
                nc.vector.tensor_scalar(var_eps[:, b:b + 1], mean_var[:, b, 1:2], EPS, None, ALU.add).then_inc(var_ready, 1)

            def normalise(source, n, b):
                dve.wait_ge(rstd_ready, n + 1)
                nc.vector.tensor_scalar(x_norm[:, b, :], source[:, b, :], mean_var[:, b, 0:1],
                                        rstd[:, b:b + 1], ALU.subtract, ALU.mult).then_inc(norm_ready, 1)

            def split_low(w):
                dve.wait_ge(keep["raw_hi"][w], 1)
                nc.vector.tensor_tensor(keep["gate_lo"], keep["raw"][w][:], keep["gate_hi"].bitcast(F32),
                                        ALU.subtract).then_inc(keep["raw_lo"][w], 1)

            for i, b in enumerate(batch_of):
                dve.wait_ge(attn_turned, 2 * i + 1)
                nc.vector.tensor_copy(attn_t[:, 0:KT, b * P:(b + 1) * P],
                                      ps[:, 2 * i, :].rearrange("p (t n) -> p t n", n=P)).then_inc(attn_t_ready[0], 1)
            dve.wait_ge(x_landed, 16)
            dve.wait_ge(small_landed, 16 * 4)
            for b in range(BATCH):
                add = nc.vector.tensor_tensor(x_res[:, b, :], x_res[:, b, :], bo, ALU.add)
            link(add)
            def rows_low(i):
                b = batch_of[i]
                cols = slice(b * P, (b + 1) * P)
                dve.wait_ge(hi_ready, i + 1)
                nc.vector.tensor_tensor(xt_lo[:, :, cols], ps[:, 4 + b, :].rearrange("p (t n) -> p t n", n=P),
                                        xt_hi[:, :, cols].bitcast(F32), ALU.subtract).then_inc(lo_ready, 1)

            for i, b in enumerate(batch_of):
                dve.wait_ge(wo_done, i + 1)
                link(nc.vector.tensor_tensor(x_res[:, b, :], ps[:, b, :], x_res[:, b, :], ALU.add))
                variance(x_res, b)
                if i < 3:
                    dve.wait_ge(qkv_hi_ready, i + 1)
                    nc.vector.tensor_tensor(qkv_lo[i], keep["raw"][i][:], qkv_hi[i].bitcast(F32),
                                            ALU.subtract).then_inc(qkv_lo_ready, 1)
                normalise(x_res, i, b)
            for i in range(BATCH):
                rows_low(i)

            def unit(i):
                b = batch_of[i]
                dve.wait_ge(roots_ready, i + 1)
                link(nc.vector.tensor_scalar(norms[:, b, :], norms[:, b, :], NORM_EPS, None, ALU.max))
                link(nc.vector.reciprocal(norms[:, b, :], norms[:, b, :]))
                heads = qkv[:, b, 0:2 * DIM].rearrange("p (h e) -> p h e", e=LD)
                scale = norms[:, b, :].unsqueeze(2).to_broadcast([P, 2 * LHEADS, LD])
                nc.vector.tensor_tensor(heads, heads, scale, ALU.mult).then_inc(unit_ready, 1)

            for n, (i, j) in enumerate(products):
                b = batch_of[i]
                dve.wait_ge(qkv_done, n + 1)
                nc.vector.tensor_tensor(qkv[:, b, j * DIM:(j + 1) * DIM], ps[:, n % 8, :],
                                        qkv_b[:, j * DIM:(j + 1) * DIM], ALU.add).then_inc(qkv_ready, 1)
                if j == 1:
                    dve.wait_ge(squares_ready, i + 1)
                    nc.vector.tensor_reduce(sums[:, b, :], squares[b].rearrange("p (h e) -> p h e", e=LD), AX_X,
                                            ALU.add).then_inc(sums_ready, 1)
                    if i >= 1:
                        unit(i - 1)
            unit(BATCH - 1)
            split_low(GATE)
            dve.wait_ge(const_ready, 3 + GROUP)
            for i, b in enumerate(batch_of):
                dve.wait_ge(kv_done, i + 1)
                nc.vector.tensor_tensor(kv[:, :, b * P:(b + 1) * P], ps[:, b, :].rearrange("p (t n) -> p t n", n=P),
                                        block_mask[:].unsqueeze(1).to_broadcast([P, KT, P]), ALU.mult).then_inc(kv_ready, 1)
            for b in range(BATCH):
                add = nc.vector.tensor_tensor(x_res[:, b, :], x_res[:, b, :], proj_b, ALU.add)
            link(add)
            for b in range(BATCH):
                dve.wait_ge(proj_done, b + 1)
                link(nc.vector.tensor_tensor(x3[:, b, :], ps[:, 4 + b, :], x_res[:, b, :], ALU.add))
                variance(x3, b)
                if b >= 1:
                    normalise(x3, BATCH + b - 1, b - 1)
            normalise(x3, 2 * BATCH - 1, BATCH - 1)
            for b in range(BATCH):
                cols = slice(b * P, (b + 1) * P)
                dve.wait_ge(hi_ready, BATCH + b + 1)
                nc.vector.tensor_tensor(xt_lo[:, :, cols], x_t[:, :, cols], xt_hi[:, :, cols].bitcast(F32),
                                        ALU.subtract).then_inc(lo_ready, 1)
            dve.wait_ge(logits_done, 1)
            logits = ps[:, 4, 0:BATCH * EXPERTS].rearrange("p (b e) -> p b e", b=BATCH)
            link(nc.vector.tensor_reduce(peak[:], logits, AX_X, ALU.max))
            for b in range(BATCH):
                nc.vector.tensor_scalar(routed[:, b, :], logits[:, b, :], peak[:, b:b + 1], None, ALU.subtract)

        @block.tensor
        def _(pe):
            def turn(out_bank, source, done):
                for t in range(KT):
                    tr = nc.tensor.transpose(ps[:, out_bank, t * P:(t + 1) * P], source[:, t * P:(t + 1) * P], ident[:])
                tr.then_inc(done, 1)

            for i in range(BATCH):
                if i == 1:
                    pe.wait_ge(keep["attn_landed"], 16 * 2)
                if i == 3:
                    pe.wait_ge(late_landed, 16)
                turn(2 * i, attn[i][:, 0:DIM], attn_turned)
                turn(2 * i + 1, attn[i][:, DIM:2 * DIM], attn_turned)
            pe.wait_ge(keep["wo_landed"], 16)
            for i, b in enumerate(batch_of):
                pe.wait_ge(attn_t_ready[0], max(i, b // 2) + 1)
                pe.wait_ge(attn_t_ready[1], max(i, b // 2) + 1)
                for t in range(INNER // P):
                    mm = nc.tensor.matmul(ps[:, b, :], attn_t[:, t, b * P:(b + 1) * P], wo[:, t, :],
                                          start=(t == 0), stop=(t == INNER // P - 1))
                mm.then_inc(wo_done, 1)
            for i, b in enumerate(batch_of):
                pe.wait_ge(norm_ready, i + 1)
                turn(4 + b, x_norm[:, b, :], x_turned)
            pe.wait_ge(qkv_lo_ready, 3)
            for n, (i, j) in enumerate(products):
                b = batch_of[i]
                pe.wait_ge(lo_ready, 1 if i == 0 else BATCH)
                if n >= 8:
                    pe.wait_ge(qkv_ready, n - 7)
                for t in range(KT):
                    cols = slice(b * P, (b + 1) * P)
                    out = ps[:, n % 8, :]
                    nc.tensor.matmul(out, xt_hi[:, t, cols], qkv_hi[j][:, t, :], start=(t == 0), stop=False)
                    nc.tensor.matmul(out, xt_hi[:, t, cols], qkv_lo[j][:, t, :], start=False, stop=False)
                    mm = nc.tensor.matmul(out, xt_lo[:, t, cols], qkv_hi[j][:, t, :], start=False, stop=(t == KT - 1))
                mm.then_inc(qkv_done, 1)
            pe.wait_ge(qkv_ready, 3 * BATCH)
            for i, b in enumerate(batch_of):
                pe.wait_ge(unit_ready, i + 1)
                turn(4 + b, qkv[:, b, 0:DIM], q_turned)
                for g in range(KT):
                    k = qkv[:, b, DIM + g * P:DIM + (g + 1) * P]
                    v = qkv[:, b, 2 * DIM + g * P:2 * DIM + (g + 1) * P]
                    mm = nc.tensor.matmul(ps[:, b, g * P:(g + 1) * P], k, v, start=True, stop=True)
                mm.then_inc(kv_done, 1)
            for i, b in enumerate(batch_of):
                pe.wait_ge(kv_ready, i + 1)
                pe.wait_ge(q_t_ready, i + 1)
                for g in range(KT):
                    mm = nc.tensor.matmul(ps[:, b, g * P:(g + 1) * P], kv[:, g, b * P:(b + 1) * P],
                                          q_t[:, g, b * P:(b + 1) * P], start=True, stop=True)
                mm.then_inc(out_done, 1)
            pe.wait_ge(proj_landed, 16)
            for b in range(BATCH):
                pe.wait_ge(out_t_ready, b + 2 if b < BATCH - 1 else BATCH)
                for t in range(KT):
                    mm = nc.tensor.matmul(ps[:, 4 + b, :], out_t[:, t, b * P:(b + 1) * P], proj_w[:, t, :],
                                          start=(t == 0), stop=(t == KT - 1))
                mm.then_inc(proj_done, 1)
            for b in range(BATCH):
                pe.wait_ge(norm_ready, BATCH + b + 1)
                turn(b, x_norm[:, b, :], x_turned)
            for b in range(BATCH):
                pe.wait_ge(x_t_ready, b + 1)
                for t in range(KT):
                    mm = nc.tensor.matmul(ps[:, 4, b * EXPERTS:(b + 1) * EXPERTS], x_t[:, t, b * P:(b + 1) * P],
                                          router_w[:, t, :], start=(t == 0), stop=(t == KT - 1))
            mm.then_inc(logits_done, 1)


def experts(nc, d, keep):
    with ExitStack() as ctx:
        def sb(name, shape, dt=F32):
            return ctx.enter_context(nc.sbuf_tensor(name, shape, dt))

        def sem(name):
            return ctx.enter_context(nc.semaphore(name))

        x3, xt_hi, xt_lo, routed = (keep[n] for n in ("x3", "xt_hi", "xt_lo", "routed"))
        raw = keep["raw"]
        w_hi = [keep["gate_hi"]] + [sb(f"{n}_hi", [P, KT, DIM], F32R)[:] for n in ("up", "down")]
        w_lo = [keep["gate_lo"]] + [sb(f"{n}_lo", [P, KT, DIM], F32R)[:] for n in ("up", "down")]
        silu = sb("silu", [P, 2, TOKENS])
        hidden = sb("hidden", [P, 2, TOKENS])
        h_hi = sb("h_hi", [P, KT, TOKENS], F32R)
        h_lo = sb("h_lo", [P, KT, TOKENS], F32R)
        y = sb("y", [P, BATCH, DIM])
        total = sb("total", [P, BATCH])
        top = sb("top", [P, BATCH, 8])
        top_at = sb("top_at", [P, BATCH, 8], U32)
        top_atf = sb("top_atf", [P, BATCH, 8])
        share = sb("share", [P, 2, BATCH, EXPERTS])
        weight = sb("weight", [P, BATCH])
        ps_gate = ctx.enter_context(nc.psum_tensor("ps_gate", [P, 2, 512], F32))
        ps_up = ctx.enter_context(nc.psum_tensor("ps_up", [P, 2, 512], F32))
        ps_y = ctx.enter_context(nc.psum_tensor("ps_y", [P, BATCH, 512], F32))

        raw_landed, raw_hi, raw_lo = keep["raw_landed"], keep["raw_hi"], keep["raw_lo"]
        gate_up_done = sem("gate_up_done")
        silu_ready = sem("silu_ready")
        hidden_ready = sem("hidden_ready")
        h_hi_ready = sem("h_hi_ready")
        h_lo_ready = sem("h_lo_ready")
        down_done = sem("down_done")
        exp_ready = sem("exp_ready")
        router_step = sem("router_step")
        weight_ready = sem("weight_ready")
        y_added = sem("y_added")
        y_stored = sem("y_stored")

        def run(eng, expert):
            expert(0, first=True, last=False)
            with eng.Fori(1, ALL_EXPERTS - 1) as e:
                expert(e, first=False, last=False)
            expert(ALL_EXPERTS - 1, first=False, last=True)

        block = ctx.enter_context(nc.Block())

        @block.sync
        def _(sp):
            def expert(e, first, last):
                if not first:
                    for w in (GATE, UP, DOWN):
                        wait(sp, raw_lo[w], e)
                        sp.dma_start(raw[w][:], d[WEIGHTS[w]][e].rearrange("(t p) n -> p t n", p=P)).then_inc(raw_landed[w], 16)

            run(sp, expert)
            for b in range(BATCH):
                sp.wait_ge(y_added, BATCH * (ALL_EXPERTS - 1) + b + 1)
                sp.dma_start(d["out"][b], y[:, b, :]).then_inc(y_stored, 16)
            sp.wait_ge(y_stored, 16 * BATCH)

        @block.scalar
        def _(act):
            def split_high(w, e):
                wait(act, raw_landed[w], 16 * (e + 1))
                if w == DOWN:
                    wait(act, down_done, BATCH * e)
                else:
                    wait(act, gate_up_done, KT * e)
                nc.scalar.activation(w_hi[w], raw[w][:], ACT.Copy).then_inc(raw_hi[w], 1)

            split_high(UP, 0)
            nc.scalar.activation(routed[:], routed[:], ACT.Exp).then_inc(exp_ready, 1)

            def expert(e, first, last):
                split_high(DOWN, e)
                for f in range(KT):
                    n = e * KT + f
                    wait(act, gate_up_done, n + 1)
                    wait(act, hidden_ready, n - 1)
                    nc.scalar.activation(silu[:, f % 2, :], ps_gate[:, f % 2, :], ACT.Silu).then_inc(silu_ready, 1)
                    wait(act, hidden_ready, n + 1)
                    nc.scalar.activation(h_hi[:, f, :], hidden[:, f % 2, :], ACT.Copy).then_inc(h_hi_ready, 1)
                if not last:
                    split_high(GATE, e + 1)
                    split_high(UP, e + 1)

            run(act, expert)

        @block.vector
        def _(dve):
            chain = [0]

            def link(ins):
                chain[0] += 1
                ins.then_inc(router_step, 1)
                dve.wait_ge(router_step, chain[0])

            def split_low(w, e):
                wait(dve, raw_hi[w], e + 1)
                nc.vector.tensor_tensor(w_lo[w], raw[w][:], w_hi[w].bitcast(F32), ALU.subtract).then_inc(raw_lo[w], 1)

            def router_probabilities():
                dve.wait_ge(exp_ready, 1)
                link(nc.vector.tensor_reduce(total[:], routed[:], AX_X, ALU.add))
                link(nc.vector.reciprocal(total[:], total[:]))
                for b in range(BATCH):
                    prob = nc.vector.tensor_scalar(routed[:, b, :], routed[:, b, :], total[:, b:b + 1], None, ALU.mult)
                link(prob)

            def router_best():
                for b in range(BATCH):
                    best = nc.vector.max(top[:, b, :], routed[:, b, :])
                link(best)
                for b in range(BATCH):
                    where = nc.vector.max_index(top_at[:, b, :], top[:, b, :], routed[:, b, :])
                link(where)
                nc.vector.tensor_copy(top_atf[:], top_at[:])
                link(nc.vector.tensor_tensor(total[:], top[:, :, 0], top[:, :, 1], ALU.add))
                link(nc.vector.tensor_scalar(total[:], total[:], 1e-9, None, ALU.add))
                link(nc.vector.reciprocal(total[:], total[:]))

            def router_shares():
                for b in range(BATCH):
                    scaled = nc.vector.tensor_scalar(top[:, b, 0:2], top[:, b, 0:2], total[:, b:b + 1], None, ALU.mult)
                link(scaled)
                for k in range(2):
                    for b in range(BATCH):
                        part = nc.vector.tensor_scalar(share[:, k, b, :], keep["numbers"][:], top_atf[:, b, k:k + 1],
                                                       top[:, b, k:k + 1], ALU.is_equal, ALU.mult)
                link(part)
                link(nc.vector.tensor_tensor(share[:, 0], share[:, 0], share[:, 1], ALU.add))

            split_low(UP, 0)
            router = (router_probabilities, router_best, router_shares)

            def expert(e, first, last):
                split_low(DOWN, e)
                for f in range(KT):
                    n = e * KT + f
                    wait(dve, silu_ready, n + 1)
                    wait(dve, h_lo_ready, n - 1)
                    nc.vector.tensor_tensor(hidden[:, f % 2, :], ps_up[:, f % 2, :], silu[:, f % 2, :], ALU.mult).then_inc(hidden_ready, 1)
                    wait(dve, h_hi_ready, n + 1)
                    nc.vector.tensor_tensor(h_lo[:, f, :], hidden[:, f % 2, :], h_hi[:, f, :].bitcast(F32), ALU.subtract).then_inc(h_lo_ready, 1)
                    if first and f < len(router):
                        router[f]()
                if not last:
                    split_low(GATE, e + 1)
                    split_low(UP, e + 1)
                if not first:
                    wait(dve, y_added, BATCH * e)
                    nc.vector.tensor_copy(weight[:], share[:, 0, :, e - 1]).then_inc(weight_ready, 1)
                    wait(dve, weight_ready, e)
                for b in range(BATCH):
                    wait(dve, down_done, BATCH * e + (b + 1))
                    if first:
                        add = nc.vector.tensor_tensor(y[:, b, :], ps_y[:, b, :], x3[:, b, :], ALU.add)
                    else:
                        add = nc.vector.scalar_tensor_tensor(y[:, b, :], ps_y[:, b, :], weight[:, b:b + 1], y[:, b, :],
                                                             ALU.mult, ALU.add)
                    add.then_inc(y_added, 1)

            run(dve, expert)

        @block.tensor
        def _(pe):
            def product(out, left, right, first, last):
                nc.tensor.matmul(out, left[0], right[0], start=first, stop=False)
                nc.tensor.matmul(out, left[0], right[1], start=False, stop=False)
                return nc.tensor.matmul(out, left[1], right[0], start=False, stop=last)

            def expert(e, first, last):
                for f in range(KT):
                    wait(pe, hidden_ready, e * KT + (f - 1))
                    for out, w in ((ps_gate, GATE), (ps_up, UP)):
                        if f == 0:
                            wait(pe, raw_lo[w], e + 1)
                        for t in range(KT):
                            cols = slice(f * P, (f + 1) * P)
                            mm = product(out[:, f % 2, :], (w_hi[w][:, t, cols], w_lo[w][:, t, cols]),
                                         (xt_hi[:, t, :], xt_lo[:, t, :]), t == 0, t == KT - 1)
                    mm.then_inc(gate_up_done, 1)
                wait(pe, raw_lo[DOWN], e + 1)
                for t in range(KT):
                    wait(pe, h_lo_ready, e * KT + (t + 1))
                    if t == 0:
                        wait(pe, y_added, BATCH * e)
                    for b in range(BATCH):
                        cols = slice(b * P, (b + 1) * P)
                        mm = product(ps_y[:, b, :], (h_hi[:, t, cols], h_lo[:, t, cols]),
                                     (w_hi[DOWN][:, t, :], w_lo[DOWN][:, t, :]), t == 0, t == KT - 1)
                        if t == KT - 1:
                            mm.then_inc(down_done, 1)

            run(pe, expert)


def program(nc, d):
    d["q_scratch"] = nc.dram_tensor("q_scratch", (PAIRS, P, BATCH, 2 * QUERIES), F32).ap()
    d["attn_scratch"] = nc.dram_tensor("attn_scratch", (BATCH, P, INNER), F32).ap()
    with ExitStack() as ctx:
        def sb(name, shape, dt=F32):
            return ctx.enter_context(nc.sbuf_tensor(name, shape, dt))

        def sem(name):
            return ctx.enter_context(nc.semaphore(name))

        keep = {"ident": sb("ident", [P, P]), "minus_half": sb("minus_half", [P, 8])}
        keep["x_hi"] = sb("x_hi", [P, 2, KT, CHUNK], F32R)
        room = sb("row_room", [P, BATCH - 1, INNER])
        keep["row_in"] = room[:, 0:2, :].rearrange("p a (t n) -> p (a t) n", n=DIM)
        keep["x_full"] = room[:, 2, :].rearrange("p (a t n) -> p a t n", a=2, n=P)
        keep["attn_early"], keep["attn_last"] = room[:, 0:2, :], room[:, 2, :]
        room = sb("wo_room", [P, 2 * KT, DIM])
        keep["angles"] = room[:, 0:KT, :].rearrange("p (a c) n -> p a c n", a=2)
        keep["turned"] = room[:, KT:2 * KT, :]
        keep["wo"] = room
        keep["angles_landed"] = [sem(f"angles_landed{i}") for i in range(2)]
        keep["wo_landed"] = sem("wo_landed")
        keep["attn_landed"] = sem("attn_landed")
        with ExitStack() as inner:
            def sbi(name, shape, dt=F32):
                return inner.enter_context(nc.sbuf_tensor(name, shape, dt))

            for w in ("wk", "wv"):
                for part in ("hi", "lo"):
                    keep[f"{w}_{part}"] = sbi(f"{w}_{part}", [P, KT, INNER], F32R)
            keep["ctx_g"] = sbi("ctx_g", [P, KT])
            keep["ctx_b"] = sbi("ctx_b", [P, KT])
            keep["v_hi"] = sbi("v_hi", [P, ROW_TILES, HEADS, DHEAD + 1], F32R)
            keep["q_stored"] = [inner.enter_context(nc.semaphore(f"q_stored{i}")) for i in range(2)]
            rows = context_rows(nc, inner, d, keep)
            prepare(nc, d, keep, rows)
            attend(nc, d, keep, rows)
        keep["x3"] = sb("x3", [P, BATCH, DIM])
        keep["xt_hi"] = sb("xt_hi", [P, KT, TOKENS], F32R)
        keep["xt_lo"] = sb("xt_lo", [P, KT, TOKENS], F32R)
        keep["routed"] = sb("routed", [P, BATCH, EXPERTS])
        keep["numbers"] = sb("numbers", [P, EXPERTS])
        keep["raw"] = [sb(f"{n}_raw", [P, KT, DIM]) for n in WEIGHTS]
        keep["gate_hi"], keep["gate_lo"] = keep["x_hi"][:, 0], keep["x_hi"][:, 1]
        keep["raw_landed"] = [sem(f"{n}_landed") for n in WEIGHTS]
        keep["raw_hi"] = [sem(f"{n}_hi_ready") for n in WEIGHTS]
        keep["raw_lo"] = [sem(f"{n}_lo_ready") for n in WEIGHTS]
        mix(nc, d, keep)
        experts(nc, d, keep)


def kernel(**inputs):
    import numpy as np
    import concourse.bacc as bacc
    from concourse.bass_utils import run_bass_kernel_spmd

    a = {name: np.asarray(value) for name, value in inputs.items()}

    def column(v):
        return v.reshape(KT, P).T

    wkv = a["L0_xattn_Wkv"]
    wk = wkv[:, :INNER].reshape(DIM, HEADS // 4, 4, 2, HALF).transpose(0, 1, 3, 4, 2).reshape(DIM, INNER)
    arrays = {
        "x": a["x"],
        "ctx": a["ctx_1024"],
        "lat_g": column(a["L0_xattn_ln_lat_g"]),
        "lat_b": column(a["L0_xattn_ln_lat_b"]),
        "ctx_g": column(a["L0_xattn_ln_ctx_g"]),
        "ctx_b": column(a["L0_xattn_ln_ctx_b"]),
        "cos": a["L0_xattn_cos"].T,
        "sin": a["L0_xattn_sin"].T,
        "wq": a["L0_xattn_Wq"],
        "wk": wk,
        "wv": wkv[:, INNER:],
        "wo": a["L0_xattn_Wo"],
        "bo": a["L0_xattn_bo"],
        "qkv_w": a["L0_attn_qkv_w"],
        "qkv_b": a["L0_attn_qkv_b"],
        "proj_w": a["L0_attn_proj_w"],
        "proj_b": a["L0_attn_proj_b"],
        "router_w": a["L0_ffn_router_w"],
        "gate": np.concatenate([a["L0_ffn_sg"][None], a["L0_ffn_wg"]]),
        "up": np.concatenate([a["L0_ffn_su"][None], a["L0_ffn_wu"]]),
        "down": np.concatenate([a["L0_ffn_sd"][None], a["L0_ffn_wd"]]),
    }
    nc = bacc.Bacc("TRN2", target_bir_lowering=False, num_devices=1)
    feed, d = {}, {}
    for name, value in arrays.items():
        value = np.ascontiguousarray(value)
        feed[f"in_{name}"] = value
        d[name] = nc.dram_tensor(f"in_{name}", value.shape, mybir.dt.from_np(value.dtype), kind="ExternalInput").ap()
    d["out"] = nc.dram_tensor("out_y", (BATCH, QUERIES, DIM), F32, kind="ExternalOutput").ap()
    program(nc, d)
    result = run_bass_kernel_spmd(nc, [feed], core_ids=[0])
    return result.results[0]["out_y"]
```
